# Optimizing a Trainium2 kernel written in Bass

```python
import numpy as np
import jax
import jax.numpy as jnp

def _softmax(x, axis=-1):
    return jax.nn.softmax(x, axis=axis)

def _gelu(x):
    return jax.nn.gelu(x, approximate=True)

def _silu(x):
    return jax.nn.silu(x)

def _sigmoid(x):
    return jax.nn.sigmoid(x)

def _layernorm(x, axis=-1, eps=1e-05):
    m = jnp.mean(x, axis=axis, keepdims=True)
    v = jnp.var(x, axis=axis, keepdims=True)
    return (x - m) / jnp.sqrt(v + eps)

def _scatter_add(tgt, idx, src, axis=0):
    return tgt.at[idx].add(src)

def _segment_sum(src, seg, n):
    return jax.ops.segment_sum(src, seg, n)
kernel_name = 'mk_early_fusion_d2_tok_img512_r4_e7622a'

def setup_inputs(seed: int=0):
    np.random.seed(seed)
    _w = jnp.asarray

    def _rec_inputs():
        import jax
        import jax.numpy as jnp
        _rk = jax.random.key(seed)
        x = -0.000356955 + 1 * jax.random.normal(jax.random.fold_in(_rk, 1), (16, 3, 96, 96), jnp.float32)
        txt = 0.0185972 + 1.43333 * jax.random.normal(jax.random.fold_in(_rk, 2), (16, 512, 128), jnp.float32)
        return (x, txt)
    x, txt = _rec_inputs()

    def _L0_tok_setup():
        import jax, jax.numpy as jnp
        import numpy as np
        key = jax.random.key(seed)
        k1, k2, k3 = jax.random.split(key, 3)
        B, C, H, W = (128, 3, 224, 224)
        E, p = (128, 16)
        K = C * p * p
        img = jax.random.normal(k1, (B, C, H, W), dtype=jnp.float32)
        w = jax.random.normal(k2, (E, K), dtype=jnp.float32) * (1.0 / np.sqrt(K))
        b = jax.random.normal(k3, (E,), dtype=jnp.float32)
        return {'img': img, 'w': w, 'b': b, 'patch_size': p}
    _L0_tok_all = _L0_tok_setup()
    _L0_tok_in = {k: v for k, v in _L0_tok_all.items() if k in ('w', 'b')}
    del _L0_tok_all

    def _L0_attn_setup():
        import jax, jax.numpy as jnp
        import numpy as np
        DIM = 128
        MAX_LEN = 128
        SHARED = 128
        EXPAND = DIM * 2
        PROJ = 2 * EXPAND + SHARED
        EPS = 1e-06
        BATCH = 32

        def _rope(x):
            b, n, m = x.shape
            half = m // 2
            pos = jnp.arange(n, dtype=x.dtype)
            inv_freq = 10000.0 ** (-jnp.arange(half, dtype=x.dtype) / half)
            sinusoid = pos[:, None] * inv_freq[None, :]
            sin = jnp.sin(sinusoid)[None]
            cos = jnp.cos(sinusoid)[None]
            x1, x2 = jnp.split(x, 2, axis=-1)
            return jnp.concatenate([x1 * cos - x2 * sin, x2 * cos + x1 * sin], axis=-1)
        key = jax.random.key(seed)
        ks = jax.random.split(key, 5)
        x = jax.random.normal(ks[0], (BATCH, MAX_LEN, DIM), jnp.float32)
        W1 = jax.random.normal(ks[1], (DIM, PROJ), jnp.float32) * 0.02
        b1 = jnp.zeros((PROJ,), jnp.float32)
        W2 = jax.random.normal(ks[2], (EXPAND, DIM), jnp.float32) * 0.02
        b2 = jnp.zeros((DIM,), jnp.float32)
        gamma = jax.random.normal(ks[3], (2, SHARED), jnp.float32) * 0.02
        beta = jnp.zeros((2, SHARED), jnp.float32)
        norm_scale = jnp.ones((), jnp.float32)
        return dict(x=x, W1=W1, b1=b1, W2=W2, b2=b2, gamma=gamma, beta=beta, norm_scale=norm_scale)
    _L0_attn_all = _L0_attn_setup()
    _L0_attn_in = {k: v for k, v in _L0_attn_all.items() if k in ('W1', 'b1', 'W2', 'b2', 'gamma', 'beta', 'norm_scale')}
    del _L0_attn_all

    def _L0_ffn_setup():
        import jax, jax.numpy as jnp
        import numpy as np
        NUM_EXPERTS = 32
        GROUP_SIZE = 4
        NUM_GROUPS = NUM_EXPERTS // GROUP_SIZE
        C_CAP = 1.0
        key = jax.random.key(seed)
        ks = jax.random.split(key, 5)
        B, S, H = (16, 512, 128)
        D_FF = int(H * 4 * (2.0 / 3.0))
        x = jax.random.normal(ks[0], (B, S, H), dtype=jnp.float32)
        W_router = jax.random.normal(ks[1], (H, NUM_EXPERTS), dtype=jnp.float32) * (1.0 / np.sqrt(H))
        b_router = jnp.zeros((NUM_EXPERTS,), dtype=jnp.float32)
        W_up = jax.random.normal(ks[2], (NUM_GROUPS, H, D_FF), dtype=jnp.float32) * (1.0 / np.sqrt(H))
        b_up = jnp.zeros((NUM_GROUPS, D_FF), dtype=jnp.float32)
        W_down = jax.random.normal(ks[3], (NUM_EXPERTS, D_FF, H), dtype=jnp.float32) * (1.0 / np.sqrt(D_FF))
        b_down = jnp.zeros((NUM_EXPERTS, H), dtype=jnp.float32)
        return {'x': x, 'W_router': W_router, 'b_router': b_router, 'W_up': W_up, 'b_up': b_up, 'W_down': W_down, 'b_down': b_down}
    _L0_ffn_all = _L0_ffn_setup()
    _L0_ffn_in = {k: v for k, v in _L0_ffn_all.items() if k in ('W_router', 'b_router', 'W_up', 'b_up', 'W_down', 'b_down')}
    del _L0_ffn_all

    def _L1_attn_setup():
        import jax, jax.numpy as jnp
        import numpy as np
        THRE = 4.0
        EPS = 1e-05

        @jax.custom_vjp
        def spike(x):
            return jnp.floor(jnp.clip(x, 0.0, THRE) + 0.5)

        def _spike_fwd(x):
            return (spike(x), x)

        def _spike_bwd(x, g):
            return (g * ((x > 0) & (x < THRE)).astype(g.dtype),)
        spike.defvjp(_spike_fwd, _spike_bwd)
        key = jax.random.key(seed)
        k0, k1, k2 = jax.random.split(key, 3)
        B, N, C = (4, 256, 128)
        x = jax.random.normal(k0, (B, N, C), jnp.float32)
        Wqkv = jax.random.normal(k1, (3 * C, C), jnp.float32) * C ** (-0.5)
        gamma = jnp.ones((3 * C,), jnp.float32)
        beta = jnp.zeros((3 * C,), jnp.float32)
        Wproj = jax.random.normal(k2, (C, C), jnp.float32) * C ** (-0.5)
        bproj = jnp.zeros((C,), jnp.float32)
        return {'x': x, 'Wqkv': Wqkv, 'gamma': gamma, 'beta': beta, 'Wproj': Wproj, 'bproj': bproj}
    _L1_attn_all = _L1_attn_setup()
    _L1_attn_in = {k: v for k, v in _L1_attn_all.items() if k in ('Wqkv', 'gamma', 'beta', 'Wproj', 'bproj')}
    del _L1_attn_all

    def _L1_ffn_setup():
        import jax, jax.numpy as jnp
        import numpy as np
        B, T, C = (8, 256, 128)
        H = 256
        G, EG = (2, 4)
        E = G * EG
        K = 2
        LN_EPS = 1e-05

        def _swiglu(x):
            a, b = jnp.split(x, 2, axis=-1)
            return jax.nn.silu(a) * b
        key = jax.random.key(seed)
        ks = jax.random.split(key, 8)
        n = lambda k, shape, s: jax.random.normal(k, shape, dtype=jnp.float32) * s
        return {'x': n(ks[0], (B, T, C), 1.0), 'ln_scale': jnp.ones((C,), jnp.float32), 'ln_bias': jnp.zeros((C,), jnp.float32), 'shared_in_w': n(ks[1], (2 * H, C), 0.02), 'shared_out_w': n(ks[2], (C, H), 0.02), 'shared_out_b': jnp.zeros((C,), jnp.float32), 'expert_in_w': n(ks[3], (2 * H, C), 0.02), 'expert_out_weight': n(ks[4], (E, C, H), 0.02), 'expert_out_bias': jnp.zeros((E, C), jnp.float32), 'group_gate_w': n(ks[5], (G, C), 0.02), 'expert_gate_w': n(ks[6], (E, C), 0.02), 'group_bias': jnp.zeros((G,), jnp.float32), 'expert_bias': jnp.zeros((E,), jnp.float32)}
    _L1_ffn_all = _L1_ffn_setup()
    _L1_ffn_in = {k: v for k, v in _L1_ffn_all.items() if k in ('ln_scale', 'ln_bias', 'shared_in_w', 'shared_out_w', 'shared_out_b', 'expert_in_w', 'expert_out_weight', 'expert_out_bias', 'group_gate_w', 'expert_gate_w', 'group_bias', 'expert_bias')}
    del _L1_ffn_all
    return {'x': x, 'txt': txt, 'L0_tok_w': _L0_tok_in['w'], 'L0_tok_b': _L0_tok_in['b'], 'L0_attn_W1': _L0_attn_in['W1'], 'L0_attn_b1': _L0_attn_in['b1'], 'L0_attn_W2': _L0_attn_in['W2'], 'L0_attn_b2': _L0_attn_in['b2'], 'L0_attn_gamma': _L0_attn_in['gamma'], 'L0_attn_beta': _L0_attn_in['beta'], 'L0_attn_norm_scale': _L0_attn_in['norm_scale'], 'L0_ffn_W_router': _L0_ffn_in['W_router'], 'L0_ffn_b_router': _L0_ffn_in['b_router'], 'L0_ffn_W_up': _L0_ffn_in['W_up'], 'L0_ffn_b_up': _L0_ffn_in['b_up'], 'L0_ffn_W_down': _L0_ffn_in['W_down'], 'L0_ffn_b_down': _L0_ffn_in['b_down'], 'L1_attn_Wqkv': _L1_attn_in['Wqkv'], 'L1_attn_gamma': _L1_attn_in['gamma'], 'L1_attn_beta': _L1_attn_in['beta'], 'L1_attn_Wproj': _L1_attn_in['Wproj'], 'L1_attn_bproj': _L1_attn_in['bproj'], 'L1_ffn_ln_scale': _L1_ffn_in['ln_scale'], 'L1_ffn_ln_bias': _L1_ffn_in['ln_bias'], 'L1_ffn_shared_in_w': _L1_ffn_in['shared_in_w'], 'L1_ffn_shared_out_w': _L1_ffn_in['shared_out_w'], 'L1_ffn_shared_out_b': _L1_ffn_in['shared_out_b'], 'L1_ffn_expert_in_w': _L1_ffn_in['expert_in_w'], 'L1_ffn_expert_out_weight': _L1_ffn_in['expert_out_weight'], 'L1_ffn_expert_out_bias': _L1_ffn_in['expert_out_bias'], 'L1_ffn_group_gate_w': _L1_ffn_in['group_gate_w'], 'L1_ffn_expert_gate_w': _L1_ffn_in['expert_gate_w'], 'L1_ffn_group_bias': _L1_ffn_in['group_bias'], 'L1_ffn_expert_bias': _L1_ffn_in['expert_bias']}

def reference(x, txt, L0_tok_w, L0_tok_b, L0_attn_W1, L0_attn_b1, L0_attn_W2, L0_attn_b2, L0_attn_gamma, L0_attn_beta, L0_attn_norm_scale, L0_ffn_W_router, L0_ffn_b_router, L0_ffn_W_up, L0_ffn_b_up, L0_ffn_W_down, L0_ffn_b_down, L1_attn_Wqkv, L1_attn_gamma, L1_attn_beta, L1_attn_Wproj, L1_attn_bproj, L1_ffn_ln_scale, L1_ffn_ln_bias, L1_ffn_shared_in_w, L1_ffn_shared_out_w, L1_ffn_shared_out_b, L1_ffn_expert_in_w, L1_ffn_expert_out_weight, L1_ffn_expert_out_bias, L1_ffn_group_gate_w, L1_ffn_expert_gate_w, L1_ffn_group_bias, L1_ffn_expert_bias):
    import jax
    import jax.numpy as jnp

    def _L0_tok_ref(img, w, b, patch_size):
        import jax, jax.numpy as jnp
        import numpy as np
        B, C, H, W = img.shape
        p = patch_size
        Hp, Wp = (H // p, W // p)
        S = Hp * Wp
        patches = img.reshape(B, C, Hp, p, Wp, p)
        patches = patches.transpose(0, 2, 4, 1, 3, 5).reshape(B, S, C * p * p)
        out = jnp.einsum('bsk,ek->bse', patches, w) + b
        return out

    def _L0_attn_ref(x, W1, b1, W2, b2, gamma, beta, norm_scale):
        import jax, jax.numpy as jnp
        import numpy as np
        DIM = 128
        MAX_LEN = 128
        SHARED = 128
        EXPAND = DIM * 2
        PROJ = 2 * EXPAND + SHARED
        EPS = 1e-06
        BATCH = 32

        def _rope(x):
            b, n, m = x.shape
            half = m // 2
            pos = jnp.arange(n, dtype=x.dtype)
            inv_freq = 10000.0 ** (-jnp.arange(half, dtype=x.dtype) / half)
            sinusoid = pos[:, None] * inv_freq[None, :]
            sin = jnp.sin(sinusoid)[None]
            cos = jnp.cos(sinusoid)[None]
            x1, x2 = jnp.split(x, 2, axis=-1)
            return jnp.concatenate([x1 * cos - x2 * sin, x2 * cos + x1 * sin], axis=-1)
        shortcut = x
        ms = jnp.mean(jnp.square(x), axis=-1, keepdims=True)
        h = x * jax.lax.rsqrt(ms + EPS) * norm_scale
        uv = jax.nn.silu(h @ W1 + b1)
        u, v, base = jnp.split(uv, [EXPAND, 2 * EXPAND], axis=-1)
        qk_base = base[:, :, None, :] * gamma + beta
        q = qk_base[:, :, 0]
        k = qk_base[:, :, 1]
        qk = jnp.einsum('bnd,bmd->bnm', q, k) / MAX_LEN
        qk = _rope(qk)
        kernel = jnp.square(jax.nn.relu(qk))
        out = u * jnp.einsum('bnm,bme->bne', kernel, v)
        return out @ W2 + b2 + shortcut

    def _L0_ffn_ref(x, W_router, b_router, W_up, b_up, W_down, b_down):
        import jax, jax.numpy as jnp
        import numpy as np
        NUM_EXPERTS = 32
        GROUP_SIZE = 4
        NUM_GROUPS = NUM_EXPERTS // GROUP_SIZE
        C_CAP = 1.0
        B, S, H = x.shape
        bs = B * S
        E = NUM_EXPERTS
        k = min(int(bs * C_CAP) // E, bs)
        xf = x.reshape(bs, H)
        h = xf @ W_router + b_router
        Sm = jax.nn.softmax(h, axis=-1)
        G_ek, idx_ek = jax.lax.top_k(Sm.T, k)
        tokens = xf[idx_ek]
        D_FF = W_up.shape[-1]
        tok_g = tokens.reshape(NUM_GROUPS, GROUP_SIZE, k, H)
        up = jnp.einsum('gjkh,ghf->gjkf', tok_g, W_up) + b_up[:, None, None, :]
        act = jax.nn.silu(up).reshape(E, k, D_FF)
        Eout = jnp.einsum('ekf,efh->ekh', act, W_down) + b_down[:, None, :]
        weighted = G_ek[..., None] * Eout
        y = jnp.zeros((bs, H), dtype=x.dtype).at[idx_ek.reshape(-1)].add(weighted.reshape(-1, H))
        return y.reshape(B, S, H)

    def _L1_attn_ref(x, Wqkv, gamma, beta, Wproj, bproj):
        import jax, jax.numpy as jnp
        import numpy as np
        THRE = 4.0
        EPS = 1e-05

        @jax.custom_vjp
        def spike(x):
            return jnp.floor(jnp.clip(x, 0.0, THRE) + 0.5)

        def _spike_fwd(x):
            return (spike(x), x)

        def _spike_bwd(x, g):
            return (g * ((x > 0) & (x < THRE)).astype(g.dtype),)
        spike.defvjp(_spike_fwd, _spike_bwd)
        B, N, C = x.shape
        H = 8
        hd = C // H
        scale = hd ** (-0.5)
        xs = spike(x)
        qkv = jnp.einsum('bnc,dc->bnd', xs, Wqkv)
        mu = qkv.mean(axis=(0, 1))
        var = qkv.var(axis=(0, 1))
        qkv = (qkv - mu) * jax.lax.rsqrt(var + EPS) * gamma + beta
        qkv = qkv.reshape(B, N, 3, H, hd).transpose(2, 0, 3, 1, 4)
        q = spike(qkv[0])
        k = spike(qkv[1])
        v = spike(qkv[2])
        attn = jnp.einsum('bhnd,bhmd->bhnm', q, k)
        attn = spike(attn)
        out = jnp.einsum('bhnm,bhmd->bhnd', attn, v) * scale
        out = out.transpose(0, 2, 1, 3).reshape(B, N, C)
        out = spike(out)
        return jnp.einsum('bnc,dc->bnd', out, Wproj) + bproj

    def _L1_ffn_ref(x, ln_scale, ln_bias, shared_in_w, shared_out_w, shared_out_b, expert_in_w, expert_out_weight, expert_out_bias, group_gate_w, expert_gate_w, group_bias, expert_bias):
        import jax, jax.numpy as jnp
        import numpy as np
        B, T, C = (8, 256, 128)
        H = 256
        G, EG = (2, 4)
        E = G * EG
        K = 2
        LN_EPS = 1e-05

        def _swiglu(x):
            a, b = jnp.split(x, 2, axis=-1)
            return jax.nn.silu(a) * b
        Bx, Tx, Cx = x.shape
        S = Bx * Tx
        flat = x.reshape(S, Cx)
        mu = flat.mean(-1, keepdims=True)
        var = ((flat - mu) ** 2).mean(-1, keepdims=True)
        flat = (flat - mu) * jax.lax.rsqrt(var + LN_EPS) * ln_scale + ln_bias
        h_shared = _swiglu(flat @ shared_in_w.T)
        out_shared = h_shared @ shared_out_w.T + shared_out_b
        g_logits = flat @ group_gate_w.T + group_bias
        g_idx = jnp.argmax(g_logits, axis=-1)
        e_logits = (flat @ expert_gate_w.T).reshape(S, G, EG)
        e_sel = jnp.take_along_axis(e_logits, g_idx[:, None, None], axis=1)[:, 0, :]
        e_sel = e_sel + expert_bias.reshape(G, EG)[g_idx]
        e_probs = jax.nn.softmax(e_sel, axis=-1)
        topv, topi = jax.lax.top_k(e_probs, K)
        topv = topv / (topv.sum(-1, keepdims=True) + 1e-08)
        disp = g_idx[:, None] * EG + topi
        h_expert = _swiglu(flat @ expert_in_w.T)
        rows = jnp.arange(S)[:, None]
        comb = jnp.zeros((S, E), flat.dtype).at[rows, disp].add(topv)
        cnt = jnp.zeros((S, E), flat.dtype).at[rows, disp].add(1.0)
        routed = cnt @ expert_out_bias
        for e in range(E):
            routed = routed + comb[:, e:e + 1] * (h_expert @ expert_out_weight[e].T)
        return (out_shared + routed).reshape(Bx, Tx, Cx)
    h = _L0_tok_ref(x, L0_tok_w, L0_tok_b, 16)
    h = jnp.concatenate([h, txt], axis=1)
    h = h + _L0_attn_ref(_layernorm(h, axis=-1), L0_attn_W1, L0_attn_b1, L0_attn_W2, L0_attn_b2, L0_attn_gamma, L0_attn_beta, L0_attn_norm_scale)
    h = h + _L0_ffn_ref(_layernorm(h, axis=-1), L0_ffn_W_router, L0_ffn_b_router, L0_ffn_W_up, L0_ffn_b_up, L0_ffn_W_down, L0_ffn_b_down)
    h = h + _L1_attn_ref(_layernorm(h, axis=-1), L1_attn_Wqkv, L1_attn_gamma, L1_attn_beta, L1_attn_Wproj, L1_attn_bproj)
    h = h + _L1_ffn_ref(_layernorm(h, axis=-1), L1_ffn_ln_scale, L1_ffn_ln_bias, L1_ffn_shared_in_w, L1_ffn_shared_out_w, L1_ffn_shared_out_b, L1_ffn_expert_in_w, L1_ffn_expert_out_weight, L1_ffn_expert_out_bias, L1_ffn_group_gate_w, L1_ffn_expert_gate_w, L1_ffn_group_bias, L1_ffn_expert_bias)
    return h

_drawn_inputs = setup_inputs


def setup_inputs(seed=0):
    import zlib

    import numpy as np

    out = dict(_drawn_inputs(seed))
    spreads = {'L0_attn_b1': (0.0, 0.8),
     'L0_attn_b2': (0.0, 0.1),
     'L0_attn_beta': (0.0, 0.8),
     'L0_ffn_b_router': (0.0, 0.578),
     'L0_ffn_b_up': (0.0, 0.61),
     'L0_ffn_b_down': (0.0, 0.499),
     'L1_attn_gamma': (1.0, 0.57),
     'L1_attn_beta': (0.0, 0.1),
     'L1_attn_bproj': (0.0, 0.338),
     'L1_ffn_ln_scale': (1.0, 0.6),
     'L1_ffn_ln_bias': (0.0, 0.512),
     'L1_ffn_shared_out_b': (0.0, 1.184),
     'L1_ffn_expert_out_bias': (0.0, 0.922),
     'L1_ffn_group_bias': (0.0, 0.43),
     'L1_ffn_expert_bias': (0.0, 0.407)}
    factors = {'L0_attn_W1': 8.0,
     'L0_attn_W2': 8.0,
     'L0_attn_gamma': 8.0,
     'L1_ffn_shared_in_w': 8.0,
     'L1_ffn_shared_out_w': 8.0,
     'L1_ffn_expert_in_w': 8.0,
     'L1_ffn_expert_out_weight': 8.0,
     'L1_ffn_group_gate_w': 2.825}
    for name, (base, spread) in spreads.items():
        noise = np.random.default_rng([zlib.crc32(name.encode()), seed]).standard_normal(out[name].shape)
        drawn = base * np.exp(spread * noise) if base else spread * noise
        out[name] = jnp.asarray(drawn.astype(out[name].dtype))
    for name, factor in factors.items():
        out[name] = (out[name] * factor).astype(out[name].dtype)
    return out
```

```python
import concourse.bass as bass
from concourse import mybir
from contextlib import ExitStack
import numpy as np

F32 = mybir.dt.float32
BF16 = mybir.dt.bfloat16
I32 = mybir.dt.int32
F32R = mybir.dt.float32r
ALU = mybir.AluOpType
ACT = mybir.ActivationFunctionType
AX = mybir.AxisListType

B = 16
P = 128
TEXT = 512
PATCHES = 36
S = TEXT + PATCHES
NT = B * S
HALF = S // 2
ROPE = S // 2
EXPAND = 256
TOK_K = 768 // P
NE = 32
NGRP = 4
SEG = NT // NGRP
SEGP = -(-SEG // 32) * 32
TOPK = NT // NE
BLK = 8
BLOCKS = -(-TOPK // BLK) + NGRP - 1
SLOTS = BLOCKS * BLK
SLOT_TILES = [(0, 128), (128, 128), (256, SLOTS - 256)]
ROUNDS = -(-TOPK // BLK)
TRASH = NT
NROWS = NT + 448
ROWW = P + NE
DFF = 341
FT = [(0, 128), (128, 128), (256, DFF - 256)]
HEADS = 8
HD = 16
CT = 3
CH = CT * P
TILES = -(-NT // CH) * CT
CHUNKS = TILES // CT
NTP = TILES * P
NEX = 8

COLS = {}


def _columns():
    at = 0
    for name, n in [("tok_b", 1), ("b2", 1), ("gamma", 2), ("beta", 2), ("norm", 1), ("b1_base", 1), ("b1_u", 2),
                    ("router_b", 1), ("bn_gamma", 3), ("bn_beta", 3), ("proj_b", 1), ("ln_scale", 1), ("ln_bias", 1),
                    ("up_b", 8 * 3), ("gate_b", 10)]:
        COLS[name] = (at, n)
        at += n
    return at


NCOLS = _columns()
MTILES = [(0, 128), (128, 128), (256, ROPE - 256)]


LN_TOTALS = {"centred": lambda n: 8 * NGRP, "evacuated": lambda n: 8 * NGRP + 2, "squared": lambda n: 4 * NGRP,
             "var": lambda n: 4 * NGRP + 1, "std": lambda n: NGRP * n + 1, "rstd": lambda n: NGRP * n,
             "bc": lambda n: 4 * NGRP * n, "scaled": lambda n: 4 * NGRP * n + 2, "eps": lambda n: n}


def split_matmul(nc, out, weights, moving, start, stop):
    nc.tensor.matmul(out, weights[0], moving[0], start=start, stop=False)
    nc.tensor.matmul(out, weights[0], moving[1], start=False, stop=False)
    return nc.tensor.matmul(out, weights[1], moving[0], start=False, stop=stop)


def layernorm(nc, k, H, XN, variants, tag):
    sets = NGRP
    with ExitStack() as st:
        sb = lambda n, s, d: st.enter_context(nc.sbuf_tensor(f"{tag}_{n}", s, d))
        ps = lambda n, s: st.enter_context(nc.psum_tensor(f"{tag}_{n}", s, F32))
        nv = len(variants)
        sq = [sb(f"square{g}", [P, S], F32) for g in range(NGRP)]
        rstd = [sb(f"rstd{v}", [P, 2, HALF], F32) for v in range(nv)]
        eps = [sb(f"eps{v}", [P, 1], F32) for v in range(nv)]
        xc_ps = [ps(f"centred{j}", [P, 512]) for j in range(2)]
        var_ps = ps("var", [P, 2, 512])
        bc_ps = [ps(f"bcast{j}", [P, 2, 512]) for j in range(2)]
        centred, evacuated, squared, var_done, std_done, rstd_done, bc_done, scaled, eps_set = (
            k["ln_sems"][n][0] for n in LN_TOTALS)
        (centred0, evacuated0, squared0, var0, std0, rstd0, bc0, scaled0, eps0) = (k["ln_sems"][n][1] for n in LN_TOTALS)
        for n, total in LN_TOTALS.items():
            k["ln_sems"][n][1] += total(nv)
        base = XN[0]
        block = st.enter_context(nc.Block())

        def tokens(t, i, g, j):
            return t[:, bass.ds(((g * NGRP) + i) * S + j * HALF, HALF)]

        def whole(t, i, g):
            return t[:, bass.ds(((g * NGRP) + i) * S, S)]

        @block.tensor
        def _(pe):
            def center(i):
                for g in range(NGRP):
                    for j in range(2):
                        pe.wait_ge(evacuated, evacuated0 + 8 * i + 2 * g + j + 1)
                        nc.tensor.matmul(xc_ps[j][:, 0:HALF], k["center"][:], tokens(H, i, g, j),
                                         start=True, stop=True).then_inc(centred, 1)

            def variance(i):
                for g in range(NGRP):
                    pe.wait_ge(squared, squared0 + 4 * i + g + 1)
                    if g == 0:
                        pe.wait_ge(std_done, std0 + nv * i + 1)
                    for j in range(2):
                        last = nc.tensor.matmul(var_ps[32 * g:32 * g + 32, j, 0:HALF], k["mean32"][:],
                                                sq[g][:, j * HALF:(j + 1) * HALF], start=True, stop=True)
                    last.then_inc(var_done, 1)

            def broadcast(i):
                for v in range(nv):
                    pe.wait_ge(rstd_done, rstd0 + nv * i + v + 1)
                    for g in range(NGRP):
                        n = (4 * v + g) % 2
                        pe.wait_ge(scaled, scaled0 + 4 * nv * i + 4 * v + g + 1)
                        for j in range(2):
                            last = nc.tensor.matmul(bc_ps[n][:, j, 0:HALF], k["pick_row"][32 * g:32 * g + 32, :],
                                                    rstd[v][32 * g:32 * g + 32, j, :], start=True, stop=True)
                        last.then_inc(bc_done, 1)

            pe.sem_inc(var_done, 1)
            center(0)
            variance(0)
            with pe.Fori(0, sets - 1) as i:
                center(i + 1)
                broadcast(i)
                variance(i + 1)
            broadcast(sets - 1)

        @block.scalar
        def _(act):
            act.sem_inc(evacuated, 2)
            act.sem_inc(std_done, 1)
            act.wait_ge(eps_set, eps0 + nv)

            def evacuate(i):
                for g in range(NGRP):
                    for j in range(2):
                        act.wait_ge(centred, centred0 + 8 * i + 2 * g + j + 1)
                        nc.scalar.activation(tokens(base, i, g, j), xc_ps[j][:, 0:HALF], ACT.Copy).then_inc(evacuated, 1)

            def std(i):
                act.wait_ge(var_done, var0 + 4 * i + 5)
                act.wait_ge(scaled, scaled0 + 4 * nv * i + 2)
                for v, (a, _) in enumerate(variants):
                    nc.scalar.activation(rstd[v][:], var_ps[:, :, 0:HALF], ACT.Sqrt, bias=eps[v][:], scale=a).then_inc(std_done, 1)

            evacuate(0)
            std(0)
            with act.Fori(0, sets - 1) as i:
                evacuate(i + 1)
                std(i + 1)

        @block.gpsimd
        def _(pool):
            with pool.Fori(0, sets) as i:
                for g in range(NGRP):
                    pool.wait_ge(evacuated, evacuated0 + 8 * i + 2 * g + 2 + 2)
                    pool.wait_ge(var_done, var0 + 4 * i + 1)
                    nc.gpsimd.tensor_tensor(sq[g][:], whole(base, i, g), whole(base, i, g), ALU.mult).then_inc(squared, 1)

        @block.vector
        def _(dve):
            dve.sem_inc(scaled, 2)
            for v, (_, b) in enumerate(variants):
                nc.vector.memset(eps[v][:], b).then_inc(eps_set, 1)
            with dve.Fori(0, sets) as i:
                for v in range(nv):
                    dve.wait_ge(std_done, std0 + nv * i + v + 2)
                    nc.vector.reciprocal(rstd[v][:], rstd[v][:]).then_inc(rstd_done, 1)
                for v in range(nv):
                    for g in range(NGRP):
                        n = (4 * v + g) % 2
                        dve.wait_ge(bc_done, bc0 + 4 * nv * i + 4 * v + g + 1)
                        if v == 0:
                            dve.wait_ge(squared, squared0 + 4 * i + g + 1)
                        dst = XN[v] if nv == 1 else XN[nv - 1 - v]
                        nc.vector.tensor_tensor(
                            whole(dst, i, g).rearrange("p (a b) -> p a b", a=2),
                            whole(base, i, g).rearrange("p (a b) -> p a b", a=2),
                            bc_ps[n][:, :, 0:HALF], ALU.mult).then_inc(scaled, 1)


def load_inputs(nc, x, k, H):
    with ExitStack() as st:
        sem = lambda n: st.enter_context(nc.semaphore(f"in_{n}"))
        patches = st.enter_context(nc.sbuf_tensor("patches", [P, TOK_K, B * PATCHES], F32))
        tok_w = st.enter_context(nc.sbuf_tensor("tok_w_sb", [P, TOK_K, P], F32))
        emb = [st.enter_context(nc.psum_tensor(f"embedding{j}", [P, 512], F32)) for j in range(2)]
        row_parts = [st.enter_context(nc.sbuf_tensor(f"row_parts{n}", [P, 4096], F32)) for n in range(2)]
        row_bf = st.enter_context(nc.sbuf_tensor("row_bf", [P, 4096], BF16))
        img_in, text_in, const_in, embedded, evacuated, cleared, rows_in, cut = (
            sem(n) for n in ("image", "text", "const", "embedded", "evacuated", "cleared", "rows", "cut"))
        half = B * PATCHES // 2
        Hb = H[:, 0:NT].rearrange("p (b s) -> p b s", b=B)
        block = st.enter_context(nc.Block())
        consts = [("center", "center"), ("mean32", "mean32"), ("pick_row", "pick_row"), ("cols", "cols"),
                  ("ident", "ident"), ("W1", "W1"), ("W2", "W2"), ("same_expert", "same_expert"),
                  ("earlier_group", "earlier_group"), ("router", "router"), ("group_row", "group_row"), ("rowmask", "rowmask"), ("lanes", "lanes")]

        @block.sync
        def _(sp):
            sp.dma_start(patches[:], x["patches"].rearrange("k p n -> p k n")).then_inc(img_in, 16)
            sp.dma_start(tok_w[:], x["tok_w"].rearrange("k p n -> p k n")).then_inc(img_in, 16)
            sp.dma_start(Hb[:, :, PATCHES:S], x["text"]).then_inc(text_in, 16)
            sp.wait_ge(img_in, 32)
            sp.wait_ge(text_in, 16)

        @block.scalar
        def _(act):
            for name, src in consts:
                act.dma_start(k[name][:], x[src]).then_inc(const_in, 16)
            act.wait_ge(cleared, 1)
            for r in range(3):
                act.dma_start(row_parts[0][32 * r:32 * r + 1, 0:EXPAND], x["b1_v"]).then_inc(rows_in, 16)
                act.dma_start(row_parts[1][32 * r:32 * r + 1, :], x["down_b"]).then_inc(rows_in, 16)
            act.wait_ge(const_in, 16 * len(consts))
            at, _ = COLS["tok_b"]
            for j in range(2):
                act.wait_ge(embedded, j + 1)
                nc.scalar.activation(Hb[:, 8 * j:8 * j + 8, 0:PATCHES],
                                     emb[j][:, 0:half].rearrange("p (b s) -> p b s", b=8),
                                     ACT.Identity, bias=k["cols"][:, at:at + 1]).then_inc(evacuated, 1)

        @block.tensor
        def _(pe):
            pe.wait_ge(img_in, 32)
            for j in range(2):
                for t in range(TOK_K):
                    last = nc.tensor.matmul(emb[j][:, 0:half], tok_w[:, t, :], patches[:, t, j * half:(j + 1) * half],
                                            start=t == 0, stop=t == TOK_K - 1)
                last.then_inc(embedded, 1)

        @block.vector
        def _(dve):
            nc.vector.memset(row_parts[0][:], 0.0)
            nc.vector.memset(row_parts[1][:], 0.0).then_inc(cleared, 1)
            nc.vector.memset(k["ones_bf"][:], 1.0)
            nc.vector.memset(H[:, NT:NTP], 0.0)
            dve.wait_ge(rows_in, 96)
            dve.wait_ge(const_in, 16 * len(consts))
            n = 0
            for src, dst, width in ((row_parts[0], k["b1_v3"], EXPAND), (row_parts[1], k["down_b3"], 4096)):
                for part in range(3):
                    nc.vector.tensor_copy(row_bf[:, 0:width], src[:, 0:width]).then_inc(cut, 1)
                    n += 1
                    dve.wait_ge(cut, n)
                    mask = k["rowmask"][:, part:part + 1]
                    if part == 0:
                        nc.vector.tensor_scalar(dst[:], row_bf[:, 0:width], mask, None, ALU.mult).then_inc(cut, 1)
                    else:
                        nc.vector.scalar_tensor_tensor(dst[:], row_bf[:, 0:width], mask, dst[:], ALU.mult, ALU.add).then_inc(cut, 1)
                    nc.vector.tensor_tensor(src[:, 0:width], src[:, 0:width], row_bf[:, 0:width], ALU.subtract).then_inc(cut, 1)
                    n += 2
                    dve.wait_ge(cut, n)


def gated_attention(nc, k, x, H, HN, XN):
    with ExitStack() as st:
        sb = lambda n, s, d=F32: st.enter_context(nc.sbuf_tensor(f"ga_{n}", s, d))
        ps = lambda n, s: st.enter_context(nc.psum_tensor(f"ga_{n}", s, F32))
        sem = lambda n: st.enter_context(nc.semaphore(f"ga_{n}"))
        cos = sb("cos", [P, 3, S])
        sin = sb("sin", [P, 3, 2, S])
        hs = [sb(f"hs{p}", [P, S]) for p in range(2)]
        base = sb("base", [P, 2, HALF])
        q = [sb(f"q{p}", [P, S]) for p in range(2)]
        key = [sb(f"k{p}", [P, S]) for p in range(2)]
        u = [sb(f"u{p}", [P, 2, 2, HALF]) for p in range(2)]
        v = [sb(f"v{p}", [P, 5, EXPAND]) for p in range(2)]
        by_cos = [sb(f"by_cos{p}", [P, 2, HALF]) for p in range(2)]
        by_sin = [sb(f"by_sin{p}", [P, 2, HALF]) for p in range(2)]
        rot = [sb(f"rot{p}", [P, 2, HALF]) for p in range(2)]
        kern = [sb(f"kern{p}", [P, 2, HALF]) for p in range(2)]
        kern_tail = [sb(f"kern_tail{j}", [64, HALF]) for j in range(2)]
        ukv = [sb(f"ukv{j}", [P, 2, HALF]) for j in range(2)]
        misc = ps("misc", [P, 2, 512])
        scores = [ps(f"scores{p}", [P, 2, 512]) for p in range(2)]
        kv = ps("kv", [P, 2, 512])
        (tables_in, cleared, qk_done, rot_done, sum_done, relu_done, kern_done, kv_done, gated, base_ps, base_sb,
         qk_ready, u_ps, u_sb, v_ps, v_sb, hs_ready, w2_ps, resid, plus_xn) = (sem(n) for n in (
            "tables", "cleared", "qk", "rot", "sum", "relu", "kern", "kv_done", "gated", "base_ps", "base_sb",
            "qk_ready", "u_ps", "u_sb", "v_ps", "v_sb", "hs_ready", "w2", "resid", "plus_xn"))
        met = sem("met")
        tail0, tail = MTILES[2]
        TAIL2 = 32
        W1, W2 = k["W1"], k["W2"]

        def col(name, n=0):
            at, _ = COLS[name]
            return k["cols"][:, at + n:at + n + 1]

        def batch(t, b):
            return t[:, bass.ds(b * S, S)]

        def half(t, b, j):
            return t[:, bass.ds(b * S + j * HALF, HALF)]

        block = st.enter_context(nc.Block())

        @block.sync
        def _(sp):
            sp.dma_start(cos[:], x["cos"]).then_inc(tables_in, 16)
            sp.dma_start(sin[:], x["sin"]).then_inc(tables_in, 16)

        @block.tensor
        def _(pe):
            def project_base(b):
                for j in range(2):
                    last = nc.tensor.matmul(misc[:, j, 0:HALF], W1[:, 2 * EXPAND:2 * EXPAND + P], half(HN, b, j), start=True, stop=True)
                last.then_inc(base_ps, 1)

            def project_u(b, e):
                if e == 0:
                    pe.wait_ge(base_sb, b + 1)
                else:
                    pe.wait_ge(u_sb, 2 * b + 1)
                for j in range(2):
                    last = nc.tensor.matmul(misc[:, j, 0:HALF], W1[:, e * P:(e + 1) * P], half(HN, b, j), start=True, stop=True)
                last.then_inc(u_ps, 1)

            def project_v(b, p, tails):
                if tails:
                    pe.wait_ge(v_sb, 2 * b + 1)
                    tiles = [(tail0, tail, 0, 0, 0), (ROPE + tail0, tail, TAIL2, 0, 0)]
                else:
                    pe.wait_ge(u_sb, 2 * b + 2)
                    pe.wait_ge(hs_ready, b + 1)
                    tiles = [(m0, P, 0, t // 2, t % 2) for t, m0 in enumerate((0, P, ROPE, ROPE + P))]
                for m0, rows, at, bank, side in tiles:
                    out = misc[at:at + rows, bank, side * EXPAND:(side + 1) * EXPAND]
                    nc.tensor.matmul(out, hs[p][:, m0:m0 + rows], W1[:, EXPAND:2 * EXPAND], start=True, stop=False)
                    last = nc.tensor.matmul(out, k["ones_bf"][:, 0:rows], k["b1_v3"][:], start=False, stop=True)
                last.then_inc(v_ps, 1)

            def down(b, first_wait):
                first_wait()
                pe.wait_ge(gated, 2 * b + 2)
                for j in range(2):
                    for e in range(2):
                        last = nc.tensor.matmul(misc[:, j, 0:HALF], W2[:, e, :], ukv[j][:, e, :], start=e == 0, stop=e == 1)
                last.then_inc(w2_ps, 1)

            def score(b, p, g, first=False):
                j, mt = divmod(g, 3)
                m0, rows = MTILES[mt]
                if g == 0:
                    pe.wait_ge(qk_ready, b + 1)
                if not first:
                    pe.wait_ge(rot_done, 6 * b + g - 1)
                for side in range(2):
                    last = nc.tensor.matmul(scores[g % 2][0:rows, side, 0:HALF],
                                            key[p][:, side * ROPE + m0:side * ROPE + m0 + rows],
                                            q[p][:, j * HALF:(j + 1) * HALF], start=True, stop=True)
                last.then_inc(qk_done, 1)

            def weigh(b, p, g, first=False):
                j, mt = divmod(g, 3)
                pe.wait_ge(kern_done, 6 * b + g + 1)
                if mt == 0 and not (first and j == 0):
                    pe.wait_ge(gated, 2 * b + j)
                if g == 0:
                    pe.wait_ge(v_sb, 2 * b + 2)
                for e in range(2):
                    if mt < 2:
                        for side in range(2):
                            last = nc.tensor.matmul(kv[:, e, 0:HALF], v[p][:, mt + 2 * side, e * P:(e + 1) * P],
                                                    kern[g % 2][:, side, :], start=mt == 0 and side == 0, stop=False)
                    else:
                        last = nc.tensor.matmul(kv[:, e, 0:HALF], v[p][0:TAIL2 + tail, 4, e * P:(e + 1) * P],
                                                kern_tail[j][0:TAIL2 + tail, :], start=False, stop=True)
                last.then_inc(kv_done, 1)

            def units(b, p, first=False, final=False):
                for g in range(6):
                    weigh(b, p, g, first)
                    if g < 4:
                        score(b, p, g + 2)
                    elif not final:
                        score(b + 1, 1 - p, g - 4)
                    if g == 0 and not first:
                        down(b - 1, lambda: pe.wait_ge(v_sb, 2 * b + 2))
                    if final:
                        continue
                    if g == 1:
                        if first:
                            pe.wait_ge(v_sb, 2)
                        else:
                            pe.wait_ge(resid, b)
                        project_base(b + 1)
                    if g in (2, 3):
                        project_u(b + 1, g - 2)
                    if g >= 4:
                        project_v(b + 1, 1 - p, g == 5)

            project_base(0)
            project_u(0, 0)
            project_u(0, 1)
            project_v(0, 0, False)
            project_v(0, 0, True)
            score(0, 0, 0, True)
            score(0, 0, 1, True)
            units(0, 0, first=True)
            with pe.Fori(0, (B - 2) // 2) as i:
                units(2 * i + 1, 1)
                units(2 * i + 2, 0)
            units(B - 1, 1, final=True)
            down(B - 1, lambda: pe.wait_ge(resid, B - 1))

        @block.scalar
        def _(act):
            def base_out(b, first=False):
                act.wait_ge(base_ps, b + 1)
                if not first:
                    act.wait_ge(qk_ready, b)
                nc.scalar.activation(base[:], misc[:, :, 0:HALF], ACT.Silu, bias=col("b1_base")).then_inc(base_sb, 1)

            def u_out(b, p, e, first=False):
                act.wait_ge(u_ps, 2 * b + e + 1)
                if e == 0 and not first:
                    act.wait_ge(gated, 2 * b - 2)
                nc.scalar.activation(u[p][:, e], misc[:, :, 0:HALF], ACT.Silu, bias=col("b1_u", e)).then_inc(u_sb, 1)

            def v_out(b, p, tails, first=False):
                act.wait_ge(v_ps, 2 * b + tails + 1)
                if not tails:
                    if not first:
                        act.wait_ge(kv_done, 6 * b - 6)
                    last = nc.scalar.activation(v[p][:, 0:4, :], misc[:].rearrange("p b (s n) -> p (b s) n", s=2), ACT.Silu)
                else:
                    for at in (0, TAIL2):
                        last = nc.scalar.activation(v[p][at:at + tail, 4, :], misc[at:at + tail, 0, 0:EXPAND], ACT.Silu)
                last.then_inc(v_sb, 1)

            def kernel_of(b, g, first=False):
                j, mt = divmod(g, 3)
                _, rows = MTILES[mt]
                n = 6 * b + g
                act.wait_ge(sum_done, n + 1)
                nc.scalar.activation(rot[g % 2][0:rows], rot[g % 2][0:rows], ACT.Relu).then_inc(relu_done, 1)
                act.wait_ge(relu_done, n + 1)
                if not first:
                    act.wait_ge(kv_done, n - 1)
                if mt < 2:
                    last = nc.scalar.activation(kern[g % 2][:], rot[g % 2][:], ACT.Square)
                else:
                    for side in range(2):
                        last = nc.scalar.activation(kern_tail[j][TAIL2 * side:TAIL2 * side + rows, :], rot[g % 2][0:rows, side, :], ACT.Square)
                last.then_inc(kern_done, 1)

            def units(b, p, first=False, final=False):
                for g in range(6):
                    if g < 5:
                        kernel_of(b, g + 1, first and g == 0)
                    elif not final:
                        kernel_of(b + 1, 0)
                    if final:
                        continue
                    if g == 1:
                        base_out(b + 1)
                    if g in (2, 3):
                        u_out(b + 1, 1 - p, g - 2, first)
                    if g >= 4:
                        v_out(b + 1, 1 - p, g == 5, first)

            act.wait_ge(cleared, 1)
            base_out(0, True)
            u_out(0, 0, 0, True)
            u_out(0, 0, 1, True)
            v_out(0, 0, False, True)
            v_out(0, 0, True, True)
            kernel_of(0, 0, True)
            units(0, 0, first=True)
            with act.Fori(0, (B - 2) // 2) as i:
                units(2 * i + 1, 1)
                units(2 * i + 2, 0)
            units(B - 1, 1, final=True)

        @block.gpsimd
        def _(pool):
            def keep_hn(b, p, first=False):
                if not first:
                    pool.wait_ge(v_ps, 2 * b - 2)
                nc.gpsimd.tensor_copy(hs[p][:], batch(HN, b)).then_inc(hs_ready, 1)

            def make_qk(b, p, first=False):
                pool.wait_ge(base_sb, b + 1)
                if not first:
                    pool.wait_ge(qk_done, 6 * b - 6)
                pool.sem_inc(met, 1)
                flat = base[:].rearrange("p a b -> p (a b)")
                nc.gpsimd.tensor_scalar(q[p][:], flat, col("gamma", 0), col("beta", 0), ALU.mult, ALU.add)
                nc.gpsimd.tensor_scalar(key[p][:], flat, col("gamma", 1), col("beta", 1), ALU.mult, ALU.add).then_inc(qk_ready, 1)

            def add(b, g, first=False):
                _, rows = MTILES[g % 3]
                n = 6 * b + g
                pool.wait_ge(rot_done, n + 1)
                if not first:
                    pool.wait_ge(kern_done, n - 1)
                a, c = by_cos[g % 2], by_sin[g % 2]
                nc.gpsimd.tensor_tensor(rot[g % 2][0:rows, 0], a[0:rows, 0], c[0:rows, 1], ALU.add)
                nc.gpsimd.tensor_tensor(rot[g % 2][0:rows, 1], a[0:rows, 1], c[0:rows, 0], ALU.add).then_inc(sum_done, 1)

            def units(b, p, first=False, final=False):
                for g in range(6):
                    if g < 5:
                        add(b, g + 1, first and g == 0)
                    elif not final:
                        add(b + 1, 0)
                    if g == 0:
                        nc.gpsimd.tensor_tensor(batch(H, b), batch(H, b), batch(XN, b), ALU.add).then_inc(plus_xn, 1)
                    if final:
                        continue
                    if g == 1:
                        keep_hn(b + 1, 1 - p, first)
                    if g == 2:
                        make_qk(b + 1, 1 - p, first)

            for j in range(2):
                nc.gpsimd.memset(kern_tail[j][:], 0.0)
            for p in range(2):
                last = nc.gpsimd.memset(v[p][:, 4, :], 0.0)
            last.then_inc(cleared, 1)
            keep_hn(0, 0, True)
            make_qk(0, 0, True)
            add(0, 0, True)
            units(0, 0, first=True)
            with pool.Fori(0, (B - 2) // 2) as i:
                units(2 * i + 1, 1)
                units(2 * i + 2, 0)
            units(B - 1, 1, final=True)

        @block.vector
        def _(dve):
            def rotate(b, g, first=False):
                j, mt = divmod(g, 3)
                _, rows = MTILES[mt]
                n = 6 * b + g
                dve.wait_ge(qk_done, n + 1)
                if not first:
                    dve.wait_ge(sum_done, n - 1)
                xs = scores[g % 2][0:rows, :, 0:HALF]
                cj = cos[0:rows, mt, j * HALF:(j + 1) * HALF].unsqueeze(1).broadcast_to([rows, 2, HALF])
                nc.vector.tensor_tensor(by_cos[g % 2][0:rows], xs, cj, ALU.mult)
                nc.vector.tensor_tensor(by_sin[g % 2][0:rows], xs, sin[0:rows, mt, :, j * HALF:(j + 1) * HALF], ALU.mult).then_inc(rot_done, 1)

            def gate(b, p, j, first=False):
                dve.wait_ge(kv_done, 6 * b + 3 * j + 3)
                if not first:
                    dve.wait_ge(w2_ps, b)
                nc.vector.tensor_tensor(ukv[j][:], kv[:, :, 0:HALF], u[p][:, :, j, :], ALU.mult).then_inc(gated, 1)

            def residual(b):
                dve.wait_ge(w2_ps, b + 1)
                dve.wait_ge(plus_xn, b + 1)
                hb = batch(H, b).rearrange("p (a b) -> p a b", a=2)
                nc.vector.scalar_tensor_tensor(hb, misc[:, :, 0:HALF], col("b2"), hb, ALU.add, ALU.add).then_inc(resid, 1)

            def units(b, p, first=False, final=False):
                for g in range(6):
                    if g < 5:
                        rotate(b, g + 1, first and g == 0)
                    elif not final:
                        rotate(b + 1, 0)
                    if g == 0 and not first:
                        residual(b - 1)
                    if g in (2, 5):
                        gate(b, p, g // 3, first)

            dve.wait_ge(tables_in, 32)
            rotate(0, 0, True)
            units(0, 0, first=True)
            with dve.Fori(0, (B - 2) // 2) as i:
                units(2 * i + 1, 1)
                units(2 * i + 2, 0)
            units(B - 1, 1, final=True)
            residual(B - 1)


def moe_first(nc, k, x, H):
    rows_d = nc.dram_tensor("token_rows", [NROWS, ROWW], F32, kind="Internal").ap()
    y_d = [nc.dram_tensor(f"moe_sums{p}", [NROWS, P], F32, kind="Internal").ap() for p in range(2)]
    slots_d = nc.dram_tensor("expert_slots", [NE * BLOCKS, BLK], I32, kind="Internal").ap()
    with ExitStack() as st:
        sb = lambda n, s, d=F32: st.enter_context(nc.sbuf_tensor(n, s, d))
        L = sb("router_logits", [P, SEGP])
        with ExitStack() as lnst:
            XN = lnst.enter_context(nc.sbuf_tensor("XN2", [P, NT], F32))
            layernorm(nc, k, H, [XN], [(1.0, 1e-5)], "ln2")
            token_rows(nc, k, x, XN, L, rows_d, y_d, slots_d)
        idx = sb("slot_tokens", [P, 3, NE], I32)
        choose_tokens(nc, k, x, L, rows_d, slots_d, idx)
        run_experts(nc, k, x, idx, rows_d, y_d)
    add_rows(nc, k, H, y_d)


def token_rows(nc, k, x, XN, L, rows_d, y_d, slots_d):
    with ExitStack() as st:
        sb = lambda n, s, d=F32: st.enter_context(nc.sbuf_tensor(f"tr_{n}", s, d))
        ps = lambda n, s: st.enter_context(nc.psum_tensor(f"tr_ps_{n}", s, F32))
        sem = lambda n: st.enter_context(nc.semaphore(f"tr_s_{n}"))
        xs = [sb(f"xs{p}", [P, S]) for p in range(2)]
        rows = [sb(f"rows{p}", [P, 5, P]) for p in range(2)]
        zeros = sb("zeros", [P, NROWS * P // P // 4])
        logit_ps = ps("logits", [P, 2, 512])
        row_ps = [ps(f"row{p}", [P, 2, 512]) for p in range(2)]
        kept, logits, logits_out, turned, copied, cleared, filled = (
            sem(n) for n in ("kept", "logits", "logits_out", "turned", "copied", "cleared", "filled"))
        stored = [sem(f"stored{p}") for p in range(2)]
        tail = S - 4 * P
        block = st.enter_context(nc.Block())

        @block.scalar
        def _(act):
            act.sem_inc(logits_out, 1)
            at, _ = COLS["router_b"]
            with act.Fori(0, NGRP) as i:
                for g in range(NGRP):
                    act.wait_ge(turned, 4 * i + g + 1)
                    nc.scalar.activation(xs[g % 2][:], XN[:, bass.ds((g * NGRP + i) * S, S)], ACT.Copy).then_inc(kept, 1)
                act.wait_ge(logits, i + 1)
                nc.scalar.activation(L[:, bass.ds(i * S, S)].rearrange("p (a b) -> p a b", a=2), logit_ps[:, :, 0:HALF],
                                     ACT.Identity, bias=k["cols"][:, at:at + 1]).then_inc(logits_out, 1)

        @block.tensor
        def _(pe):
            pe.sem_inc(turned, 2)
            with pe.Fori(0, NGRP) as i:
                for g in range(NGRP):
                    n = 4 * i + g
                    if g == 0:
                        pe.wait_ge(logits_out, i + 1)
                    pe.wait_ge(kept, n + 1)
                    for j in range(2):
                        last = nc.tensor.matmul(logit_ps[32 * g:32 * g + 32, j, 0:HALF], k["router"][:],
                                                xs[g % 2][:, j * HALF:(j + 1) * HALF], start=True, stop=True)
                    if g == NGRP - 1:
                        last.then_inc(logits, 1)
                    pe.wait_ge(copied, n + 1)
                    for t in range(4):
                        nc.tensor.transpose(row_ps[g % 2][:, 0, t * P:(t + 1) * P], xs[g % 2][:, t * P:(t + 1) * P], k["ident"][:])
                    nc.tensor.transpose(row_ps[g % 2][0:tail, 1, 0:P], xs[g % 2][:, 4 * P:S], k["ident"][:]).then_inc(turned, 1)

        @block.vector
        def _(dve):
            dve.sem_inc(copied, 2)
            nc.vector.memset(zeros[:], 0.0).then_inc(cleared, 1)
            nc.vector.memset(L[:, SEG:SEGP], 0.0)
            with dve.Fori(0, NGRP) as i:
                for g in range(NGRP):
                    n = 4 * i + g
                    dve.wait_ge(turned, n + 3)
                    dve.wait_ge(stored[g % 2], 32 * (2 * i + g // 2) + 16)
                    nc.vector.tensor_copy(rows[g % 2][:, 0:4, :], row_ps[g % 2][:, 0, :].rearrange("p (t d) -> p t d", t=4))
                    nc.vector.tensor_copy(rows[g % 2][0:tail, 4, :], row_ps[g % 2][0:tail, 1, 0:P]).then_inc(copied, 1)

        @block.sync
        def _(sp):
            for p in range(2):
                sp.sem_inc(stored[p], 16)
            with sp.Fori(0, NGRP) as i:
                for g in range(NGRP):
                    n = 4 * i + g
                    t0 = (g * NGRP + i) * S
                    sp.wait_ge(copied, n + 3)
                    sp.dma_start(rows_d[bass.ds(t0, 4 * P), 0:P].rearrange("(t p) d -> p t d", p=P), rows[g % 2][:, 0:4, :]).then_inc(stored[g % 2], 16)
                    sp.dma_start(rows_d[bass.ds(t0 + 4 * P, tail), 0:P], rows[g % 2][0:tail, 4, :]).then_inc(stored[g % 2], 16)
            for p in range(2):
                sp.wait_ge(stored[p], 16 * B + 16)

        @block.gpsimd
        def _(pool):
            pool.wait_ge(cleared, 1)
            w = NROWS * P // P // 4
            for sums in y_d:
                yv = sums.rearrange("(p r) d -> p (r d)", p=P)
                for c in range(4):
                    pool.dma_start(yv[:, c * w:(c + 1) * w], zeros[:]).then_inc(filled, 16)
            pool.dma_start(rows_d[NT:NROWS, :].rearrange("(p r) d -> p (r d)", p=64), zeros[0:64, 0:(NROWS - NT) * ROWW // 64]).then_inc(filled, 16)
            pool.dma_start(slots_d, x["empty_slots"]).then_inc(filled, 16)
            pool.wait_ge(filled, 16 * 10)


def choose_tokens(nc, k, x, L, rows_d, slots_d, idx):
    with ExitStack() as st:
        sb = lambda n, s, d=F32: st.enter_context(nc.sbuf_tensor(f"ct_{n}", s, d))
        ps = lambda n, s: st.enter_context(nc.psum_tensor(f"ct_ps_{n}", s, F32))
        sem = lambda n: st.enter_context(nc.semaphore(f"ct_s_{n}"))
        NB32 = SEGP // 32
        T = sb("turned", [P, SEGP])
        PR = sb("probs", [P, SEGP])
        V = sb("order", [P, SEGP])
        mark = sb("mark", [P, SEGP], BF16)
        desc_i = sb("desc_i", [P, SEGP], I32)
        desc = sb("desc", [P, SEGP])
        mx = sb("mx", [P, NB32])
        sm = sb("sm", [P, NB32])
        rs = sb("rs", [P, NB32])
        found, bit, cand, won = (sb(n, [P, 1], I32) for n in ("found", "bit", "cand", "won"))
        cnt, n_gt, n_ge, n_eq, take, room, n_blk, first_row, rnd = (
            sb(n, [P, 1]) for n in ("cnt", "n_gt", "n_ge", "n_eq", "take", "room", "n_blk", "first_row", "rnd"))
        blk_i = sb("blk_i", [P, 1], I32)
        pos = sb("pos", [P, BLK])
        dummy = sb("dummy", [P, BLK])
        top = [sb(f"top{p}", [P, BLK]) for p in range(2)]
        tok = sb("tok", [P, BLK])
        ok = sb("ok", [P, BLK])
        ids = [sb(f"ids{p}", [P, BLK], I32) for p in range(2)]
        row_f = sb("row_f", [P, 1])
        row = [sb(f"row{p}", [P, 1], I32) for p in range(2)]
        n_round_f = sb("n_round_f", [1, 1])
        n_round = sb("n_round", [1, 1], I32)
        lst_i = sb("lst_i", [NE, SLOTS], I32)
        lst = sb("lst", [NE, SLOTS])
        tot = ps("tot", [P, 4])
        blk_ps = ps("blk", [1, P])
        idx_ps = ps("idx", [P, 3, NE])
        (step, exps, counted, summed, probs_out, desc_done, rounds_known, id_ready, id_sent, lists_in, lists_f,
         turned, extra, met, id_free) = (sem(n) for n in ("step", "exps", "counted", "summed", "probs_out", "desc_done", "rounds_known",
                                            "id_ready", "id_sent", "lists_in", "lists_f", "turned", "extra", "met", "id_free"))
        T3 = T[:].rearrange("p (j e) -> p j e", e=32)
        group_row = k["group_row"]
        BITS = 30
        block = st.enter_context(nc.Block())

        @block.vector
        def _(dve):
            chain = [0]

            def link(ins):
                chain[0] += 1
                ins.then_inc(step, 1)
                dve.wait_ge(step, chain[0])

            dve.sem_inc(id_free, 2)
            nc.vector.memset(bit[:], 1 << (BITS - 1))
            nc.vector.memset(idx[:], 0)
            nc.vector.memset(found[:], 0)
            nc.vector.memset(rnd[:], 0.0)
            link(nc.vector.transpose(T[:], L[:]))
            link(nc.vector.tensor_reduce(mx[:], T3, AX.X, ALU.max))
            link(nc.vector.tensor_tensor(T3, T3, mx[:].unsqueeze(2).broadcast_to([P, NB32, 32]), ALU.subtract))
            dve.wait_ge(exps, 1)
            link(nc.vector.tensor_reduce(sm[:], T3, AX.X, ALU.add))
            link(nc.vector.reciprocal(rs[:], sm[:]))
            link(nc.vector.tensor_tensor(T3, T3, rs[:].unsqueeze(2).broadcast_to([P, NB32, 32]), ALU.mult))
            link(nc.vector.transpose(PR[:], T[:]))
            link(nc.vector.memset(PR[:, SEG:SEGP], -1.0))
            s0 = chain[0]
            with dve.Fori(0, BITS) as i:
                at = s0 + 4 * i
                nc.vector.tensor_tensor(cand[:], found[:], bit[:], ALU.bitwise_or).then_inc(step, 1)
                dve.wait_ge(step, at + 1)
                nc.vector.tensor_scalar(mark[:], PR[:], cand[:].bitcast(F32), None, ALU.is_ge, ALU.add, accum_out=cnt[:]).then_inc(counted, 1)
                dve.wait_ge(summed, i + 1)
                nc.vector.scalar_tensor_tensor(won[:], tot[:, 0:1], float(TOPK), bit[:], ALU.is_ge, ALU.mult).then_inc(step, 1)
                dve.wait_ge(step, at + 2)
                nc.vector.tensor_tensor(found[:], found[:], won[:], ALU.bitwise_or).then_inc(step, 1)
                nc.vector.tensor_single_scalar(bit[:], bit[:], 1, ALU.logical_shift_right).then_inc(step, 1)
                dve.wait_ge(step, at + 4)
            chain[0] += 4 * BITS
            thr = found[:].bitcast(F32)
            dve.wait_ge(desc_done, 1)
            link(nc.vector.tensor_copy(desc[:], desc_i[:]))
            link(nc.vector.tensor_scalar(mark[:], PR[:], thr, None, ALU.is_ge, ALU.add, accum_out=n_ge[:]))
            link(nc.vector.scalar_tensor_tensor(V[:], PR[:], thr, desc[:], ALU.is_ge, ALU.mult))
            nc.vector.tensor_scalar(mark[:], PR[:], thr, None, ALU.is_gt, ALU.add, accum_out=n_gt[:]).then_inc(counted, 1)
            dve.wait_ge(counted, BITS + 1)
            link(nc.vector.scalar_tensor_tensor(V[:], mark[:], 4096.0, V[:], ALU.mult, ALU.add))
            nc.vector.tensor_tensor(n_eq[:], n_ge[:], n_gt[:], ALU.subtract).then_inc(counted, 1)
            dve.wait_ge(summed, BITS + 1)
            link(nc.vector.tensor_scalar(room[:], tot[:, 1:2], -1.0, float(TOPK), ALU.mult, ALU.add))
            link(nc.vector.tensor_tensor(room[:], room[:], tot[:, 2:3], ALU.subtract))
            link(nc.vector.tensor_scalar(room[:], room[:], 0.0, n_eq[:], ALU.max, ALU.min))
            link(nc.vector.tensor_tensor(take[:], n_gt[:], room[:], ALU.add))
            link(nc.vector.tensor_scalar(blk_i[:], take[:], float(BLK - 1), None, ALU.add))
            link(nc.vector.tensor_single_scalar(blk_i[:], blk_i[:], 3, ALU.logical_shift_right))
            nc.vector.tensor_copy(n_blk[:], blk_i[:]).then_inc(counted, 1)
            dve.wait_ge(summed, BITS + 2)
            link(nc.vector.tensor_tensor(first_row[:], tot[:, 3:4], group_row[:, 2:3], ALU.add))
            link(nc.vector.reduce_max(n_round_f[:], blk_ps[:], AX.X))
            link(nc.vector.tensor_scalar(n_round[:], n_round_f[:], 1.0, None, ALU.add))
            link(nc.vector.tensor_single_scalar(n_round[:], n_round[:], 1, ALU.logical_shift_right))
            dve.sem_inc(rounds_known, 1)
            nc.vector.tensor_copy(pos[:], k["lanes"][:])
            link(nc.vector.tensor_scalar(dummy[:], k["lanes"][:], group_row[:, 1:2], float(TRASH), ALU.add, ALU.add))
            steps = nc.vector.value_load(n_round[0:1, 0:1], min_val=1, max_val=(ROUNDS + 1) // 2)
            s1 = chain[0]
            with dve.Fori(0, steps) as i:
                for p in range(2):
                    at = s1 + (i * 2 + p) * 6
                    nc.vector.max(top[p][:], V[:]).then_inc(step, 1)
                    dve.wait_ge(step, at + 1)
                    nc.vector.tensor_single_scalar(ok[:], top[p][:], 4096.0, ALU.is_gt)
                    nc.vector.match_replace(V[:], top[p][:], V[:], -1.0).then_inc(step, 1)
                    dve.wait_ge(step, at + 2)
                    nc.vector.scalar_tensor_tensor(tok[:], ok[:], 4096.0, top[p][:], ALU.mult, ALU.subtract).then_inc(step, 1)
                    dve.wait_ge(step, at + 3)
                    nc.vector.scalar_tensor_tensor(tok[:], tok[:], group_row[:, 0:1], dummy[:], ALU.add, ALU.subtract)
                    nc.vector.tensor_scalar(ok[:], pos[:], take[:], None, ALU.is_lt)
                    nc.vector.tensor_scalar(row_f[:], rnd[:], n_blk[:], 50000.0, ALU.is_ge, ALU.mult).then_inc(step, 1)
                    dve.wait_ge(step, at + 4)
                    nc.vector.scalar_tensor_tensor(row_f[:], rnd[:], first_row[:], row_f[:], ALU.add, ALU.add)
                    nc.vector.tensor_scalar_add(pos[:], pos[:], float(BLK))
                    nc.vector.scalar_tensor_tensor(tok[:], tok[:], 4096.0, ok[:], ALU.add, ALU.mult).then_inc(step, 1)
                    dve.wait_ge(id_free, 2 * i + p + 1)
                    dve.wait_ge(step, at + 5)
                    nc.vector.tensor_tensor(ids[p][:], tok[:], dummy[:], ALU.add)
                    nc.vector.tensor_copy(row[p][:], row_f[:])
                    nc.vector.tensor_scalar_add(rnd[:], rnd[:], 1.0).then_inc(step, 1)
                    dve.wait_ge(step, at + 6)
                    dve.sem_inc(id_ready, 1)
            dve.wait_ge(lists_in, 16)
            nc.vector.tensor_copy(lst[:], lst_i[:]).then_inc(lists_f, 1)
            dve.wait_ge(turned, 1)
            nc.vector.tensor_copy(idx[:, 0:2, :], idx_ps[:, 0:2, :])
            nc.vector.tensor_copy(idx[0:SLOTS - 256, 2, :], idx_ps[0:SLOTS - 256, 2, :]).then_inc(lists_f, 1)

        @block.scalar
        def _(act):
            act.wait_ge(step, 3)
            nc.scalar.activation(T[:], T[:], ACT.Exp).then_inc(exps, 1)

        @block.tensor
        def _(pe):
            with pe.Fori(0, BITS) as i:
                pe.wait_ge(counted, i + 1)
                nc.tensor.matmul(tot[:, 0:1], k["same_expert"][:], cnt[:], start=True, stop=True).then_inc(summed, 1)
            pe.wait_ge(counted, BITS + 2)
            nc.tensor.matmul(tot[:, 1:2], k["same_expert"][:], n_gt[:], start=True, stop=True)
            nc.tensor.matmul(tot[:, 2:3], k["earlier_group"][:], n_eq[:], start=True, stop=True).then_inc(summed, 1)
            pe.wait_ge(counted, BITS + 3)
            nc.tensor.matmul(tot[:, 3:4], k["earlier_group"][:], n_blk[:], start=True, stop=True)
            nc.tensor.matmul(blk_ps[:], n_blk[:], k["ident"][:], start=True, stop=True).then_inc(summed, 1)
            pe.wait_ge(lists_f, 1)
            for t, (s0, n) in enumerate(SLOT_TILES):
                last = nc.tensor.transpose(idx_ps[0:n, t, :], lst[:, s0:s0 + n], k["ident"][0:NE, 0:NE])
            last.then_inc(turned, 1)

        @block.sync
        def _(sp):
            sp.wait_ge(step, 6)
            whole = SEG // 32
            part = SEG - 32 * whole
            for g in range(NGRP):
                q0 = slice(32 * g, 32 * g + 32)
                sp.dma_start(rows_d[g * SEG:g * SEG + 32 * whole, P:ROWW].rearrange("(j t) e -> t j e", t=32),
                             T3[q0, 0:whole, :]).then_inc(probs_out, 16)
                sp.dma_start(rows_d[g * SEG + 32 * whole:(g + 1) * SEG, P:ROWW], T3[32 * g:32 * g + part, whole, :]).then_inc(probs_out, 16)
            sp.wait_ge(probs_out, 16 * 2 * NGRP)
            sp.wait_ge(extra, 1)
            sp.dma_start(lst_i[:], slots_d.rearrange("(e b) j -> e (b j)", e=NE)).then_inc(lists_in, 16)
            sp.wait_ge(lists_in, 16)

        @block.gpsimd
        def _(pool):
            nc.gpsimd.iota(desc_i[:], pattern=[[-1, SEGP]], base=4096, channel_multiplier=0).then_inc(desc_done, 1)
            pool.wait_ge(rounds_known, 1)
            steps = nc.gpsimd.value_load(n_round[0:1, 0:1], min_val=1, max_val=(ROUNDS + 1) // 2)
            with pool.Fori(0, steps) as i:
                for p in range(2):
                    pool.wait_ge(id_ready, 2 * i + p + 1)
                    pool.sem_inc(met, 1)
                    nc.gpsimd.indirect_dma_start(out=slots_d, out_offset=bass.IndirectOffsetOnAxis(ap=row[p][:], axis=0),
                                                 in_=ids[p][:], in_offset=None, bounds_check=NE * BLOCKS - 1,
                                                 oob_is_err=False).then_inc(id_sent, 16)
                    pool.wait_ge(id_sent, 16 * (2 * i + p + 1))
                    pool.sem_inc(id_free, 1)
            pool.sem_inc(extra, 1)


def run_experts(nc, k, x, idx, rows_d, y_d):
    with ExitStack() as st:
        sb = lambda n, s, d=F32: st.enter_context(nc.sbuf_tensor(f"ex_{n}", s, d))
        ps = lambda n, s: st.enter_context(nc.psum_tensor(f"ex_ps_{n}", s, F32))
        sem = lambda n: st.enter_context(nc.semaphore(f"ex_s_{n}"))
        ids = [sb(f"ids{p}", [P, 3], I32) for p in range(4)]
        rows = [sb(f"rows{p}", [P, 3, ROWW]) for p in range(4)]
        xt = [sb(f"xt{p}", [P, SLOTS]) for p in range(2)]
        hid = [sb(f"hid{p}", [P, 3, SLOTS]) for p in range(2)]
        down = [sb(f"down{p}", [P, 3, P]) for p in range(2)]
        up = [sb(f"up{p}", [P, DFF]) for p in range(2)]
        y = [sb(f"y{p}", [P, 3, P]) for p in range(4)]
        xt_ps = [ps(f"xt{p}", [P, 512]) for p in range(2)]
        up_ps = ps("up", [P, 3, 512])
        y_ps = [ps(f"y{p}", [P, 3, P]) for p in range(2)]
        up_in, down_in = ([sem(f"{n}{p}") for p in range(2)] for n in ("up_in", "down_in"))
        gathered = [sem(f"gathered{p}") for p in range(4)]
        added = [sem(f"added{p}") for p in range(2)]
        (turned, xt_out, up_done, hid_done, y_done, y_out, met, y_free, ids_kept) = (
            sem(n) for n in ("turned", "xt_out", "up_done", "hid_done", "y_done",
                             "y_out", "met", "y_free", "ids_kept"))
        met_act = sem("met_act")
        STEP = 8
        block = st.enter_context(nc.Block())

        @block.sync
        def _(sp):
            with sp.Fori(0, NE // STEP) as i:
                for m in range(STEP):
                    e = i * STEP + m
                    if m % 4 == 0:
                        sp.wait_ge(up_done, 3 * (e - 4) + 24)
                        sp.dma_start(up[m // 4][:], x["up"][bass.ds(i * 2 + m // 4, 1), :, :].rearrange("a h f -> h (a f)")).then_inc(up_in[m // 4], 16)
                    sp.wait_ge(y_done, e + 1)
                    sp.dma_start(down[m % 2][:], x["down"][bass.ds(e, 1)].rearrange("a p t d -> p (a t) d")).then_inc(down_in[m % 2], 16)

        @block.gpsimd
        def _(pool):
            def gather(e, p):
                nc.gpsimd.tensor_copy(ids[p][:], idx[:, :, bass.ds(e, 1)].rearrange("p t a -> p (t a)")).then_inc(ids_kept, 1)
                pool.wait_ge(ids_kept, e + 1)
                pool.sem_inc(met, 1)
                for t, (_, n) in enumerate(SLOT_TILES):
                    nc.gpsimd.indirect_dma_start(out=rows[p][0:n, t, :], out_offset=None, in_=rows_d,
                                                 in_offset=bass.IndirectOffsetOnAxis(ap=ids[p][0:n, t:t + 1], axis=0)).then_inc(gathered[p], 16)

            def freed(p, nth):
                if not (isinstance(nth, int) and nth == 0):
                    pool.wait_ge(added[p % 2], 48 * nth)
                pool.sem_inc(y_free, 1)

            def scatter(e, p):
                pool.wait_ge(y_out, 3 * e + 3 + 6)
                pool.sem_inc(met, 1)
                for t, (_, n) in enumerate(SLOT_TILES):
                    nc.gpsimd.indirect_dma_start(out=y_d[p % 2], out_offset=bass.IndirectOffsetOnAxis(ap=ids[p][0:n, t:t + 1], axis=0),
                                                 in_=y[p][0:n, t, :], in_offset=None, compute_op=ALU.add).then_inc(added[p % 2], 16)

            pool.sem_inc(y_free, 2)
            gather(0, 0)
            gather(1, 1)
            for e in range(4):
                freed(e, e // 2)
                gather(e + 2, (e + 2) % 4)
                scatter(e, e)
            with pool.Fori(0, NE // 4 - 2) as i:
                for m in range(4):
                    freed(m, 2 * i + 2 + m // 2)
                    gather(4 * i + m + 6, (m + 2) % 4)
                    scatter(4 * i + m + 4, m)
            for e in range(NE - 4, NE):
                freed(e, e // 2)
                if e + 2 < NE:
                    gather(e + 2, (e + 2) % 4)
                scatter(e, e % 4)
            for p in range(2):
                pool.wait_ge(added[p], 24 * NE)

        @block.tensor
        def _(pe):
            def turn(e, r, nth):
                p = r % 2
                pe.wait_ge(gathered[r], 48 * nth + 48)
                pe.wait_ge(xt_out, e + 1)
                for t, (s0, n) in enumerate(SLOT_TILES):
                    last = nc.tensor.transpose(xt_ps[p][:, s0:s0 + n], rows[r][0:n, t, 0:P], k["ident"][0:n, 0:n])
                last.then_inc(turned, 1)

            def project_up(e, p, w, nth):
                pe.wait_ge(up_in[w], 16 * nth + 16)
                pe.wait_ge(xt_out, e + 3)
                for f, (f0, m) in enumerate(FT):
                    pe.wait_ge(hid_done, 3 * e + f + 1)
                    nc.tensor.matmul(up_ps[0:m, f, 0:SLOTS], up[w][:, f0:f0 + m], xt[p][:], start=True, stop=True).then_inc(up_done, 1)

            def project_down(e, p, nth):
                pe.wait_ge(hid_done, 3 * e + 6)
                pe.wait_ge(down_in[p], 16 * nth + 16)
                pe.wait_ge(y_out, 3 * e + 3)
                for t, (s0, n) in enumerate(SLOT_TILES):
                    for f, (_, m) in enumerate(FT):
                        nc.tensor.matmul(y_ps[p][0:n, t, :], hid[p][0:m, f, s0:s0 + n], down[p][0:m, f, :], start=f == 0, stop=False)
                    last = nc.tensor.matmul(y_ps[p][0:n, t, :], k["ones_bf"][:, 0:n], k["down_b3"][:, bass.ds(e * P, P)], start=False, stop=True)
                last.then_inc(y_done, 1)

            pe.sem_inc(up_done, 24)
            pe.sem_inc(y_done, 2)
            turn(0, 0, 0)
            project_up(0, 0, 0, 0)
            with pe.Fori(0, NE // STEP - 1) as i:
                for m in range(STEP):
                    e = i * STEP + m
                    project_down(e, m % 2, 4 * i + m // 2)
                    turn(e + 1, (m + 1) % 4, 2 * i + (m + 1) // 4)
                    project_up(e + 1, (m + 1) % 2, (m + 1) // 4 % 2, i + (m + 1) // 8)
            for e in range(NE - STEP, NE):
                project_down(e, e % 2, e // 2)
                if e + 1 < NE:
                    turn(e + 1, (e + 1) % 4, (e + 1) // 4)
                    project_up(e + 1, (e + 1) % 2, (e + 1) // 4 % 2, (e + 1) // STEP)

        @block.scalar
        def _(act):
            act.sem_inc(hid_done, 3)
            act.sem_inc(xt_out, 2)
            at, _ = COLS["up_b"]
            with act.Fori(0, NE // STEP) as i:
                for m in range(STEP):
                    e = i * STEP + m
                    p = m % 2
                    act.wait_ge(turned, e + 1)
                    act.wait_ge(up_done, 3 * e - 3 + 24)
                    nc.scalar.activation(xt[p][:], xt_ps[p][:, 0:SLOTS], ACT.Copy).then_inc(xt_out, 1)
                    act.wait_ge(y_done, e + 1)
                    for f, (_, rows_f) in enumerate(FT):
                        act.wait_ge(up_done, 3 * e + f + 1 + 24)
                        bias = k["cols"][0:rows_f, bass.ds(at + (i * 2 + m // 4) * 3 + f, 1)]
                        act.sem_inc(met_act, 1)
                        nc.scalar.activation(hid[p][0:rows_f, f, :], up_ps[0:rows_f, f, 0:SLOTS], ACT.Silu, bias=bias).then_inc(hid_done, 1)

        @block.vector
        def _(dve):
            dve.sem_inc(y_out, 6)
            with dve.Fori(0, NE // 4) as i:
                for m in range(4):
                    e = 4 * i + m
                    p = m % 2
                    dve.wait_ge(y_done, e + 3)
                    dve.wait_ge(y_free, e + 1)
                    for t, (_, n) in enumerate(SLOT_TILES):
                        prob = rows[m][0:n, t, bass.ds(P + e, 1)]
                        nc.vector.tensor_scalar(y[m][0:n, t, :], y_ps[p][0:n, t, :], prob, None, ALU.mult).then_inc(y_out, 1)


def add_rows(nc, k, H, y_d):
    with ExitStack() as st:
        sem = lambda n: st.enter_context(nc.semaphore(f"ar_{n}"))
        NBUF = 4
        rows = [[st.enter_context(nc.sbuf_tensor(f"ar_rows{p}{q}", [P, 5, P], F32)) for q in range(2)] for p in range(NBUF)]
        out_ps = [st.enter_context(nc.psum_tensor(f"ar_ps{p}", [P, 2, 512], F32)) for p in range(NBUF)]
        turned, summed, joined = sem("turned"), sem("summed"), sem("joined")
        loaded = [sem(f"loaded{p}") for p in range(NBUF)]
        tail = S - 4 * P
        block = st.enter_context(nc.Block())

        @block.sync
        def _(sp):
            sp.sem_inc(turned, NBUF)
            with sp.Fori(0, B // NBUF) as i:
                for p in range(NBUF):
                    c = NBUF * i + p
                    sp.wait_ge(turned, c + 1)
                    for q in range(2):
                        at = c * S
                        sp.dma_start(rows[p][q][:, 0:4, :], y_d[q][bass.ds(at, 4 * P), :].rearrange("(t p) d -> p t d", p=P)).then_inc(loaded[p], 16)
                        sp.dma_start(rows[p][q][0:tail, 4, :], y_d[q][bass.ds(at + 4 * P, tail), :]).then_inc(loaded[p], 16)

        @block.gpsimd
        def _(pool):
            with pool.Fori(0, B // NBUF) as i:
                for p in range(NBUF):
                    pool.wait_ge(loaded[p], 64 * i + 64)
                    for n, t in ((P, slice(0, 4)), (tail, slice(4, 5))):
                        last = nc.gpsimd.tensor_tensor(rows[p][0][0:n, t], rows[p][0][0:n, t], rows[p][1][0:n, t], ALU.add)
                    last.then_inc(joined, 1)

        @block.tensor
        def _(pe):
            pe.sem_inc(summed, NBUF)
            with pe.Fori(0, B // NBUF) as i:
                for p in range(NBUF):
                    c = NBUF * i + p
                    pe.wait_ge(joined, c + 1)
                    pe.wait_ge(summed, c + 1)
                    for t in range(4):
                        nc.tensor.transpose(out_ps[p][:, 0, t * P:(t + 1) * P], rows[p][0][:, t, :], k["ident"][:])
                    nc.tensor.transpose(out_ps[p][:, 1, 0:tail], rows[p][0][0:tail, 4, :], k["ident"][0:tail, 0:tail]).then_inc(turned, 1)

        @block.vector
        def _(dve):
            with dve.Fori(0, B // NBUF) as i:
                for p in range(NBUF):
                    c = NBUF * i + p
                    dve.wait_ge(turned, NBUF + c + 1)
                    for at, n, bank in ((0, 4 * P, 0), (4 * P, tail, 1)):
                        hb = H[:, bass.ds(c * S + at, n)]
                        last = nc.vector.tensor_tensor(hb, hb, out_ps[p][:, bank, 0:n], ALU.add)
                    last.then_inc(summed, 1)


MAGIC = float(1 << 23)
UPWARD = 1.0 + 2.0 ** -23


def spiking_attention(nc, k, x, H):
    with ExitStack() as st:
        sb = lambda n, s, d=F32: st.enter_context(nc.sbuf_tensor(f"sa_{n}", s, d))
        QKV = sb("qkv", [P, 3, NT])
        scale = sb("scale", [P, 3])
        shift = sb("shift", [P, 3])
        with ExitStack() as lnst:
            XN = lnst.enter_context(nc.sbuf_tensor("XN3", [P, NT], F32))
            layernorm(nc, k, H, [XN], [(1.0, 1e-5)], "ln3")
            project_qkv(nc, k, x, XN, QKV, scale, shift)
        attend(nc, k, x, H, QKV, scale, shift)


def project_qkv(nc, k, x, XN, QKV, scale, shift):
    with ExitStack() as st:
        sb = lambda n, s, d=F32: st.enter_context(nc.sbuf_tensor(f"pq_{n}", s, d))
        sem = lambda n: st.enter_context(nc.semaphore(f"pq_s_{n}"))
        w = sb("w", [P, 3 * P])
        w3 = sb("w3", [P, 3, 3 * P], BF16)
        spikes = [sb(f"spikes{p}", [P, S], BF16) for p in range(2)]
        stats = sb("stats", [P, 3, 2 * B, 6])
        mv = sb("mv", [P, 3, 2])
        eps = sb("eps", [P, 1])
        tmp = sb("tmp", [P, 3])
        NQ = 4
        q_ps = [st.enter_context(nc.psum_tensor(f"pq_ps{n}", [P, 2, 512], F32)) for n in range(NQ)]
        w_in, cut, clipped, spiked, projected, kept, counted, met, stats_done, std_done = (
            sem(n) for n in ("w_in", "cut", "clipped", "spiked", "projected", "kept", "counted", "met", "stats", "std"))
        block = st.enter_context(nc.Block())

        @block.sync
        def _(sp):
            sp.dma_start(w[:], x["wqkv"]).then_inc(w_in, 16)

        @block.tensor
        def _(pe):
            pe.sem_inc(projected, 1)
            pe.wait_ge(cut, 7)
            with pe.Fori(0, B // NQ) as i:
                for m in range(NQ):
                    c = NQ * i + m
                    pe.wait_ge(spiked, 2 * c + 2)
                    for t in range(3):
                        n = 3 * c + t
                        pe.wait_ge(kept, n + 1)
                        for j in range(2):
                            for part in range(3):
                                last = nc.tensor.matmul(q_ps[(3 * m + t) % NQ][:, j, 0:HALF], w3[:, part, t * P:(t + 1) * P],
                                                        spikes[m % 2][:, j * HALF:(j + 1) * HALF], start=part == 0, stop=part == 2)
                        last.then_inc(projected, 1)

        @block.scalar
        def _(act):
            act.sem_inc(kept, NQ)
            with act.Fori(0, B // NQ) as i:
                for m in range(NQ):
                    for t in range(3):
                        n = 3 * (NQ * i + m) + t
                        act.wait_ge(projected, n + 2)
                        act.sem_inc(met, 1)
                        nc.scalar.activation(QKV[:, t, bass.ds((NQ * i + m) * S, S)].rearrange("p (a b) -> p a b", a=2),
                                             q_ps[(3 * m + t) % NQ][:, :, 0:HALF], ACT.Copy).then_inc(kept, 1)
            act.wait_ge(stats_done, 1)
            nc.scalar.activation(tmp[:], mv[:, :, 1], ACT.Sqrt, bias=eps[:], scale=1.0).then_inc(std_done, 1)

        @block.vector
        def _(dve):
            dve.wait_ge(w_in, 16)
            for part in range(3):
                nc.vector.tensor_copy(w3[:, part, :], w[:]).then_inc(cut, 1)
                dve.wait_ge(cut, 2 * part + 1)
                nc.vector.tensor_tensor(w[:], w[:], w3[:, part, :], ALU.subtract).then_inc(cut, 1)
                dve.wait_ge(cut, 2 * part + 2)
            nc.vector.memset(eps[:], 1e-5).then_inc(cut, 1)

            def spike(c, p):
                xb = XN[:, bass.ds(c * S, S)]
                nc.vector.tensor_scalar(xb, xb, 4.0, 0.0, ALU.min, ALU.max).then_inc(clipped, 1)
                dve.wait_ge(clipped, c + 1)
                dve.wait_ge(projected, 3 * c - 2)
                dve.sem_inc(met, 1)
                nc.vector.tensor_scalar(xb, xb, UPWARD, MAGIC, ALU.mult, ALU.add).then_inc(spiked, 1)
                dve.wait_ge(spiked, 2 * c + 1)
                nc.vector.tensor_scalar(spikes[p][:], xb, MAGIC, None, ALU.subtract).then_inc(spiked, 1)

            def count(c, m):
                for t in range(3):
                    n = 3 * c + t
                    dve.wait_ge(kept, NQ + n + 1)
                    dve.sem_inc(met, 1)
                    for j in range(2):
                        last = nc.vector.bn_stats(stats[:, t, bass.ds(2 * c + j, 1), :].rearrange("p a b -> p (a b)"),
                                                  QKV[:, t, bass.ds(c * S + j * HALF, HALF)])
                    last.then_inc(counted, 1)

            def first_spike(c, p):
                xb = XN[:, c * S:(c + 1) * S]
                nc.vector.tensor_scalar(xb, xb, 4.0, 0.0, ALU.min, ALU.max).then_inc(clipped, 1)
                dve.wait_ge(clipped, c + 1)
                nc.vector.tensor_scalar(xb, xb, UPWARD, MAGIC, ALU.mult, ALU.add).then_inc(spiked, 1)
                dve.wait_ge(spiked, 2 * c + 1)
                nc.vector.tensor_scalar(spikes[p][:], xb, MAGIC, None, ALU.subtract).then_inc(spiked, 1)

            first_spike(0, 0)
            with dve.Fori(0, B // NQ - 1) as i:
                for m in range(NQ):
                    spike(NQ * i + m + 1, (m + 1) % 2)
                    count(NQ * i + m, m)
            for m in range(NQ):
                c = B - NQ + m
                if c + 1 < B:
                    spike(c + 1, (m + 1) % 2)
                count(c, m)
            dve.wait_ge(counted, 3 * B)
            for t in range(3):
                nc.vector.bn_aggr(mv[:, t, :], stats[:, t].rearrange("p a b -> p (a b)")).then_inc(stats_done, 1) if t == 2 else \
                    nc.vector.bn_aggr(mv[:, t, :], stats[:, t].rearrange("p a b -> p (a b)"))
            dve.wait_ge(std_done, 1)
            g0, b0 = COLS["bn_gamma"][0], COLS["bn_beta"][0]
            nc.vector.reciprocal(tmp[:], tmp[:]).then_inc(cut, 1)
            dve.wait_ge(cut, 8)
            nc.vector.tensor_tensor(scale[:], tmp[:], k["cols"][:, g0:g0 + 3], ALU.mult).then_inc(cut, 1)
            dve.wait_ge(cut, 9)
            nc.vector.tensor_tensor(tmp[:], mv[:, :, 0], scale[:], ALU.mult).then_inc(cut, 1)
            dve.wait_ge(cut, 10)
            nc.vector.tensor_tensor(shift[:], k["cols"][:, b0:b0 + 3], tmp[:], ALU.subtract).then_inc(cut, 1)


def attend(nc, k, x, H, QKV, scale, shift):
    with ExitStack() as st:
        sb = lambda n, s, d=F32: st.enter_context(nc.sbuf_tensor(f"at_{n}", s, d))
        sem = lambda n: st.enter_context(nc.semaphore(f"at_s_{n}"))
        relu = [sb(f"relu{n}", [P, S]) for n in range(3)]
        vs = sb("vs", [P, S], BF16)
        qs = sb("qs", [P, S], BF16)
        ks = [sb(f"ks{p}", [P, S], BF16) for p in range(2)]
        qm = [sb(f"qm{p}", [P, HEADS, S], BF16) for p in range(2)]
        ve = [sb(f"ve{p}", [P, 5, 4, 32], BF16) for p in range(2)]
        vo = [sb(f"vo{p}", [P, 5, 4, 32], BF16) for p in range(2)]
        clip = [[sb(f"clip{p}{u}", [P, 2, HALF], BF16) for u in range(4)] for p in range(2)]
        fours = sb("fours", [P, HALF], BF16)
        ident = sb("ident", [P, P], BF16)
        out_r = [sb(f"out_r{j}", [P, HALF]) for j in range(2)]
        out_s = [sb(f"out_s{j}", [P, HALF], BF16) for j in range(2)]
        w = sb("w", [P, P])
        w3 = sb("w3", [P, 3, P], BF16)
        headmask = sb("headmask", [P, HEADS])
        four = sb("four", [P, 1])
        slot = [st.enter_context(nc.psum_tensor(f"at_slot{n}", [P, 2, 512], F32)) for n in range(3)]
        out_ps = [st.enter_context(nc.psum_tensor(f"at_out{j}", [P, 512], F32)) for j in range(2)]
        (w_in, cut, relu_done, steps, spiked, masked, s_ps, by_dve, by_act, o_done, vt_ps, ve_done, vo_done, out_relu,
         out_spiked, proj_ps, resid, met, ready) = (sem(n) for n in (
            "w_in", "cut", "relu", "steps", "spiked", "masked", "scores", "by_dve", "by_act", "o_done", "vt", "ve", "vo",
            "out_relu", "out_spiked", "proj", "resid", "met", "ready"))
        met_pe = sem("met_pe")
        TAIL = S - 4 * P
        PAIRS = [(0, 2), (1, 3), (4, 6), (5, 7)]
        SLOT = [[0, 1, 2, 0], [1, 2, 0, 1]]
        V, Q, K = range(3)
        WHERE = [2, 0, 1]
        rows_of = lambda t: P if t < 4 else TAIL
        vt_view = out_ps[0][:, 0:5 * P // 2].bitcast(BF16).rearrange("p (t h d) -> p t h d", t=5, d=32)
        block = st.enter_context(nc.Block())

        @block.sync
        def _(sp):
            sp.dma_start(w[:], x["wproj"]).then_inc(w_in, 16)
            sp.dma_start(headmask[:], x["headmask"]).then_inc(w_in, 16)

        @block.tensor
        def _(pe):
            def score(b, p, T, units, first=False):
                j, t = divmod(T, 5)
                TT = 10 * b + T
                if T == 0 and units[0] == 0:
                    pe.wait_ge(masked, b + 1)
                    pe.wait_ge(spiked, 3 * b + 3)
                for u in units:
                    heads = PAIRS[u]
                    if T % 2 == 0:
                        last_use = [(by_dve, 2 * TT), (by_act, 2 * TT), (by_act, 2 * TT - 1), (by_dve, 2 * TT + 1)][u]
                    else:
                        last_use = [(by_act, 2 * TT - 1), (by_dve, 2 * TT), (by_act, 2 * TT), (by_dve, 2 * TT + 1)][u]
                    if not (first and u < 3):
                        pe.wait_ge(*last_use)
                    for s, h in enumerate(heads):
                        last = nc.tensor.matmul(slot[SLOT[T % 2][u]][0:rows_of(t), s, 0:HALF], ks[p][:, t * P:t * P + rows_of(t)],
                                                qm[p][:, h, j * HALF:(j + 1) * HALF], start=True, stop=True)
                    last.then_inc(s_ps, 1)

            def weigh(b, p, T):
                j, t = divmod(T, 5)
                TT = 10 * b + T
                r = rows_of(t)
                pe.wait_ge(by_dve, 2 * TT + 2)
                if T == 0:
                    pe.wait_ge(ve_done, b + 1)
                    pe.wait_ge(vo_done, b + 1)
                if T == 5:
                    pe.wait_ge(resid, 2 * b)
                pe.sem_inc(met_pe, 1)
                for h in range(0, HEADS, 2):
                    u, s = (0 if h < 4 else 2), h // 2 % 2
                    nc.tensor.matmul(out_ps[j][16 * h:16 * h + 32, 0:HALF], ve[p][0:r, t, h // 2, :], clip[T % 2][u][0:r, s, :],
                                     start=t == 0, stop=False)
                nc.tensor.matmul(out_ps[j][:, 0:HALF], vo[p][0:r, t].rearrange("p h d -> p (h d)"), fours[0:r, :],
                                 start=False, stop=False)
                pe.wait_ge(by_act, 2 * TT + 2)
                pe.sem_inc(met_pe, 1)
                for h in range(1, HEADS, 2):
                    u, s = (1 if h < 4 else 3), h // 2 % 2
                    last = nc.tensor.matmul(out_ps[j][16 * h - 16:16 * h + 16, 0:HALF], vo[p][0:r, t, h // 2, :],
                                            clip[T % 2][u][0:r, s, :], start=False, stop=t == 4)
                last.then_inc(o_done, 1)

            def project(b, j):
                pe.wait_ge(out_spiked, 2 * b + j + 2)
                for part in range(3):
                    last = nc.tensor.matmul(out_ps[j][:, 0:HALF], w3[:, part, :], out_s[j][:], start=part == 0, stop=part == 2)
                last.then_inc(proj_ps, 1)

            def turn_values(b, first=False):
                pe.wait_ge(spiked, 3 * b + 1)
                if not first:
                    pe.wait_ge(resid, 2 * b - 1)
                flat = out_ps[0][:, 0:5 * P // 2].bitcast(BF16)
                for t in range(5):
                    last = nc.tensor.transpose(flat[0:rows_of(t), t * P:(t + 1) * P], vs[:, t * P:t * P + rows_of(t)], ident[:])
                last.then_inc(vt_ps, 1)

            def steps_of(b, p, first=False, final=False):
                for T in range(10):
                    ahead = (b, p, T + 1) if T < 9 else (b + 1, 1 - p, 0)
                    if T < 9 or not final:
                        score(*ahead, range(3))
                    if T == 2 and not first:
                        project(b - 1, 1)
                    weigh(b, p, T)
                    if T < 9 or not final:
                        score(*ahead, range(3, 4))
                    if T == 7:
                        project(b, 0)
                    if T == 8 and not final:
                        turn_values(b + 1)

            pe.sem_inc(proj_ps, 1)
            pe.wait_ge(ready, 2)
            turn_values(0, True)
            score(0, 0, 0, range(4), True)
            steps_of(0, 0, first=True)
            with pe.Fori(0, (B - 2) // 2) as i:
                steps_of(2 * i + 1, 1)
                steps_of(2 * i + 2, 0)
            steps_of(B - 1, 1, final=True)
            project(B - 1, 1)

        @block.scalar
        def _(act):
            def rectify(b, n, first=False):
                if not first:
                    act.wait_ge(spiked, 3 * b + n - 2)
                    act.sem_inc(met, 1)
                c = WHERE[n]
                nc.scalar.activation(relu[n][:], QKV[:, c, bass.ds(b * S, S)], ACT.Relu, bias=shift[:, c:c + 1],
                                     scale=scale[:, c:c + 1]).then_inc(relu_done, 1)

            def clip_odd(b, T, first=False):
                TT = 10 * b + T
                r = rows_of(T % 5)
                for u in (1, 3):
                    act.wait_ge(s_ps, 4 * TT + u + 1)
                    if not first:
                        act.wait_ge(o_done, TT - 1)
                    nc.scalar.activation(clip[T % 2][u][0:r], slot[SLOT[T % 2][u]][0:r, :, 0:HALF], ACT.Relu,
                                         bias=four[0:r], scale=-1.0).then_inc(by_act, 1)

            def out_rectify(b, j):
                act.wait_ge(o_done, 10 * b + 5 * j + 5)
                if not (isinstance(b, int) and b == 0):
                    act.wait_ge(out_spiked, 2 * b + j)
                nc.scalar.activation(out_r[j][:], out_ps[j][:, 0:HALF], ACT.Relu, scale=float(HD) ** -0.5).then_inc(out_relu, 1)

            def odd_values(b, p):
                act.wait_ge(ve_done, b + 1)
                for t0, t1, r in ((0, 4, P), (4, 5, TAIL)):
                    last = nc.scalar.activation(vo[p][0:r, t0:t1, :, HD:32], vt_view[0:r, t0:t1, :, HD:32], ACT.Copy, scale=-1.0)
                last.then_inc(vo_done, 1)

            def steps_of(b, p, first=False, final=False):
                for T in range(10):
                    if T < 9:
                        clip_odd(b, T + 1, first and T == 0)
                    elif not final:
                        clip_odd(b + 1, 0)
                    if T == 0 and not first:
                        out_rectify(b - 1, 1)
                    if T < 3 and not final:
                        rectify(b + 1, T)
                    if T == 5:
                        out_rectify(b, 0)
                    if T == 9 and not final:
                        odd_values(b + 1, 1 - p)

            act.wait_ge(ready, 1)
            for n in range(3):
                rectify(0, n, True)
            odd_values(0, 0)
            clip_odd(0, 0, True)
            steps_of(0, 0, first=True)
            with act.Fori(0, (B - 2) // 2) as i:
                steps_of(2 * i + 1, 1)
                steps_of(2 * i + 2, 0)
            steps_of(B - 1, 1, final=True)
            out_rectify(B - 1, 1)

        @block.gpsimd
        def _(pool):
            def mask(b, p, first=False):
                pool.wait_ge(spiked, 3 * b + 2)
                if not first:
                    pool.wait_ge(s_ps, 40 * b - 40)
                pool.sem_inc(met, 1)
                for h in range(HEADS):
                    last = nc.gpsimd.tensor_scalar(qm[p][:, h, :], qs[:], headmask[:, h:h + 1], 1.0, ALU.mult, ALU.mult)
                last.then_inc(masked, 1)

            pool.wait_ge(w_in, 32)
            mask(0, 0, True)
            mask(1, 1, True)
            with pool.Fori(0, (B - 2) // 2) as i:
                mask(2 * i + 2, 0)
                mask(2 * i + 3, 1)

        @block.vector
        def _(dve):
            def clip_even(b, T, first=False):
                TT = 10 * b + T
                r = rows_of(T % 5)
                for u in (0, 2):
                    dve.wait_ge(s_ps, 4 * TT + u + 1)
                    if not first:
                        dve.wait_ge(o_done, TT - 1)
                    nc.vector.tensor_scalar(clip[T % 2][u][0:r], slot[SLOT[T % 2][u]][0:r, :, 0:HALF], 4.0, None,
                                            ALU.min).then_inc(by_dve, 1)

            def spike(dst, r, n, done):
                dve.sem_inc(met, 1)
                nc.vector.tensor_scalar(r, r, 4.0, UPWARD, ALU.min, ALU.mult).then_inc(steps, 1)
                dve.wait_ge(steps, n + 1)
                dve.sem_inc(met, 1)
                nc.vector.tensor_scalar(dst, r, MAGIC, MAGIC, ALU.add, ALU.subtract).then_inc(done, 1)

            def spikes_of(b, p, n, order, first=False):
                dve.wait_ge(relu_done, 3 * b + n + 1)
                if not first:
                    if n == V:
                        dve.wait_ge(vt_ps, b)
                    elif n == Q:
                        dve.wait_ge(masked, b)
                    else:
                        dve.wait_ge(s_ps, 40 * b - 40)
                spike((vs, qs, ks[p])[n][:], relu[n][:], order, spiked)

            def out_spikes(b, j, order):
                dve.wait_ge(out_relu, 2 * b + j + 1)
                if not (isinstance(b, int) and b == 0):
                    dve.wait_ge(proj_ps, 2 * b + j)
                spike(out_s[j][:], out_r[j][:], order, out_spiked)

            def residual(b, j):
                dve.wait_ge(proj_ps, 2 * b + j + 2)
                hb = H[:, bass.ds(b * S + j * HALF, HALF)]
                at, _ = COLS["proj_b"]
                dve.sem_inc(met, 1)
                nc.vector.scalar_tensor_tensor(hb, out_ps[j][:, 0:HALF], k["cols"][:, at:at + 1], hb, ALU.add, ALU.add).then_inc(resid, 1)

            def even_values(b, p):
                dve.wait_ge(vt_ps, b + 1)
                for t0, t1, r in ((0, 4, P), (4, 5, TAIL)):
                    last = nc.vector.tensor_copy(ve[p][0:r, t0:t1, :, 0:HD], vt_view[0:r, t0:t1, :, 0:HD])
                last.then_inc(ve_done, 1)

            def steps_of(b, p, first=False, final=False):
                for T in range(10):
                    if T < 9:
                        clip_even(b, T + 1, first and T == 0)
                    elif not final:
                        clip_even(b + 1, 0)
                    n = 5 * b + 2
                    if T == 1 and not first:
                        out_spikes(b - 1, 1, n)
                    if T in (2, 4, 5) and not final:
                        at = (2, 4, 5).index(T)
                        spikes_of(b + 1, 1 - p, at, n + 1 + at, first)
                    if T == 3 and not first:
                        residual(b - 1, 1)
                    if T == 6:
                        out_spikes(b, 0, n + 1 if final else n + 4)
                    if T == 8:
                        residual(b, 0)
                    if T == 9 and not final:
                        even_values(b + 1, 1 - p)

            nc.vector.memset(four[:], 4.0).then_inc(ready, 1)
            nc.vector.memset(fours[:], -4.0)
            for p in range(2):
                nc.vector.memset(ve[p][:], 0.0)
                nc.vector.memset(vo[p][:], 0.0)
            nc.vector.tensor_copy(ident[:], k["ident"][:])
            dve.wait_ge(w_in, 32)
            for part in range(3):
                nc.vector.tensor_copy(w3[:, part, :], w[:]).then_inc(cut, 1)
                dve.wait_ge(cut, 2 * part + 1)
                nc.vector.tensor_tensor(w[:], w[:], w3[:, part, :], ALU.subtract).then_inc(cut, 1)
                dve.wait_ge(cut, 2 * part + 2)
            dve.sem_inc(ready, 1)
            dve.sem_inc(out_spiked, 1)
            for n in range(3):
                spikes_of(0, 0, n, n, True)
            even_values(0, 0)
            clip_even(0, 0, True)
            steps_of(0, 0, first=True)
            with dve.Fori(0, (B - 2) // 2) as i:
                steps_of(2 * i + 1, 1)
                steps_of(2 * i + 2, 0)
            steps_of(B - 1, 1, final=True)
            out_spikes(B - 1, 1, 5 * (B - 1) + 4)
            residual(B - 1, 1)


def last_ffn(nc, k, x, H):
    with ExitStack() as st:
        sb = lambda n, s, d=F32: st.enter_context(nc.sbuf_tensor(f"ff_{n}", s, d))
        F = sb("tokens", [P, NTP])
        layernorm(nc, k, H, [F], [(1.0 + 1e-5, 1e-10)], "ln4")
        comb = sb("comb", [P, TILES, NEX])
        cnt = sb("cnt", [P, TILES, NEX + 1])
        route_tokens(nc, k, x, F, comb, cnt)
        mix_experts(nc, k, x, H, F, comb, cnt)


def route_tokens(nc, k, x, F, comb, cnt):
    with ExitStack() as st:
        sb = lambda n, s, d=F32: st.enter_context(nc.sbuf_tensor(f"rt_{n}", s, d))
        sem = lambda n: st.enter_context(nc.semaphore(f"rt_s_{n}"))
        gates = sb("gates", [P, 10])
        fb = [sb(f"chunk{p}", [P, CH]) for p in range(2)]
        GL = sb("logits", [P, TILES, 10])
        s, ns, mx, tot = (sb(n, [P, TILES]) for n in ("second", "first", "max", "total"))
        es, tmp, pr, sel = (sb(n, [P, TILES, 4]) for n in ("chosen", "tmp", "probs", "sel"))
        beats = sb("beats", [P, TILES, 6])
        gl_ps = [st.enter_context(nc.psum_tensor(f"rt_ps{p}", [P, 512], F32)) for p in range(2)]
        gates_in, scaled, kept, gated, copied, step, shifted, exps, met = (
            sem(n) for n in ("gates_in", "scaled", "kept", "gated", "copied", "step", "shifted", "exps", "met"))
        GLW = CT * 10
        block = st.enter_context(nc.Block())

        @block.sync
        def _(sp):
            sp.dma_start(gates[:], x["gates"]).then_inc(gates_in, 16)

        @block.scalar
        def _(act):
            def keep(c, p):
                act.wait_ge(gated, c + 1)
                act.sem_inc(met, 1)
                nc.scalar.activation(fb[p][:], F[:, bass.ds(c * CH, CH)], ACT.Copy).then_inc(kept, 1)

            act.wait_ge(scaled, 1)
            with act.Fori(0, CHUNKS // 2) as i:
                keep(2 * i, 0)
                keep(2 * i + 1, 1)
            keep(CHUNKS - 1, 0)
            act.wait_ge(shifted, 1)
            nc.scalar.activation(es[:], es[:], ACT.Exp).then_inc(exps, 1)

        @block.tensor
        def _(pe):
            def gate(c, p):
                pe.wait_ge(kept, c + 1)
                pe.wait_ge(copied, c + 1)
                for t in range(CT):
                    last = nc.tensor.matmul(gl_ps[p][:, 10 * t:10 * t + 10], fb[p][:, t * P:(t + 1) * P], gates[:],
                                            start=True, stop=True)
                last.then_inc(gated, 1)

            pe.sem_inc(gated, 2)
            pe.wait_ge(gates_in, 16)
            with pe.Fori(0, CHUNKS // 2) as i:
                gate(2 * i, 0)
                gate(2 * i + 1, 1)
            gate(CHUNKS - 1, 0)

        @block.vector
        def _(dve):
            def copy(c, p):
                dve.wait_ge(gated, c + 3)
                nc.vector.tensor_copy(GL[:, bass.ds(c * CT, CT), :].rearrange("p t e -> p (t e)"), gl_ps[p][:, 0:GLW]).then_inc(copied, 1)

            chain = [0]

            def link(ins):
                chain[0] += 1
                ins.then_inc(step, 1)
                dve.wait_ge(step, chain[0])

            wide = lambda a, n: a[:].unsqueeze(2).broadcast_to([P, TILES, n])
            link(nc.vector.memset(F[:, NT:NTP], 0.0))
            at, bt, gt = COLS["ln_scale"][0], COLS["ln_bias"][0], COLS["gate_b"][0]
            nc.vector.tensor_scalar(F[:], F[:], k["cols"][:, at:at + 1], k["cols"][:, bt:bt + 1], ALU.mult, ALU.add).then_inc(scaled, 1)
            dve.sem_inc(copied, 2)
            with dve.Fori(0, CHUNKS // 2) as i:
                copy(2 * i, 0)
                copy(2 * i + 1, 1)
            copy(CHUNKS - 1, 0)
            dve.wait_ge(copied, CHUNKS + 2)
            link(nc.vector.tensor_tensor(GL[:], GL[:], k["cols"][:, gt:gt + 10].unsqueeze(1).broadcast_to([P, TILES, 10]), ALU.add))
            link(nc.vector.tensor_tensor(s[:], GL[:, :, 1], GL[:, :, 0], ALU.is_gt))
            link(nc.vector.tensor_scalar(ns[:], s[:], -1.0, 1.0, ALU.mult, ALU.add))
            nc.vector.tensor_tensor(tmp[:], GL[:, :, 6:10], wide(s, 4), ALU.mult)
            link(nc.vector.tensor_tensor(es[:], GL[:, :, 2:6], wide(ns, 4), ALU.mult))
            link(nc.vector.tensor_tensor(es[:], es[:], tmp[:], ALU.add))
            link(nc.vector.tensor_reduce(mx[:], es[:], AX.X, ALU.max))
            nc.vector.tensor_tensor(es[:], es[:], wide(mx, 4), ALU.subtract).then_inc(shifted, 1)
            dve.wait_ge(exps, 1)
            link(nc.vector.tensor_reduce(tot[:], es[:], AX.X, ALU.add))
            link(nc.vector.reciprocal(tot[:], tot[:]))
            link(nc.vector.tensor_tensor(pr[:], es[:], wide(tot, 4), ALU.mult))
            pairs = [(i, j) for i in range(4) for j in range(i + 1, 4)]
            for n, (i, j) in enumerate(pairs):
                last = nc.vector.tensor_tensor(beats[:, :, n], pr[:, :, i], pr[:, :, j], ALU.is_ge)
            link(last)
            won = [beats[:, :, n] for n in range(6)]
            nc.vector.tensor_tensor(sel[:, :, 3], won[2], won[4], ALU.add)
            nc.vector.tensor_tensor(sel[:, :, 2], won[1], won[3], ALU.add)
            nc.vector.tensor_tensor(sel[:, :, 1], won[0], won[3], ALU.subtract)
            link(nc.vector.tensor_tensor(sel[:, :, 0], won[0], won[1], ALU.add))
            nc.vector.tensor_tensor(sel[:, :, 3], sel[:, :, 3], won[5], ALU.add)
            nc.vector.tensor_tensor(sel[:, :, 2], sel[:, :, 2], won[5], ALU.subtract)
            nc.vector.tensor_tensor(sel[:, :, 1], sel[:, :, 1], won[4], ALU.subtract)
            link(nc.vector.tensor_tensor(sel[:, :, 0], sel[:, :, 0], won[2], ALU.add))
            nc.vector.tensor_scalar(sel[:, :, 3], sel[:, :, 3], 2.0, None, ALU.is_lt)
            nc.vector.tensor_scalar(sel[:, :, 2], sel[:, :, 2], 1.0, None, ALU.is_lt)
            nc.vector.tensor_scalar(sel[:, :, 1], sel[:, :, 1], 0.0, None, ALU.is_lt)
            link(nc.vector.tensor_scalar(sel[:, :, 0], sel[:, :, 0], 1.0, None, ALU.is_gt))
            link(nc.vector.tensor_tensor(pr[:], pr[:], sel[:], ALU.mult))
            link(nc.vector.tensor_reduce(tot[:], pr[:], AX.X, ALU.add))
            link(nc.vector.tensor_scalar(tot[:], tot[:], 1e-8, None, ALU.add))
            link(nc.vector.reciprocal(tot[:], tot[:]))
            link(nc.vector.tensor_tensor(pr[:], pr[:], wide(tot, 4), ALU.mult))
            nc.vector.tensor_tensor(comb[:, :, 0:4], pr[:], wide(ns, 4), ALU.mult)
            nc.vector.tensor_tensor(comb[:, :, 4:8], pr[:], wide(s, 4), ALU.mult)
            nc.vector.tensor_tensor(cnt[:, :, 0:4], sel[:], wide(ns, 4), ALU.mult)
            nc.vector.tensor_tensor(cnt[:, :, 4:8], sel[:], wide(s, 4), ALU.mult)
            nc.vector.memset(cnt[:, :, 8:9], 1.0)


def mix_experts(nc, k, x, H, F, comb, cnt):
    with ExitStack() as st:
        sb = lambda n, s, d=F32: st.enter_context(nc.sbuf_tensor(f"mx_{n}", s, d))
        sem = lambda n: st.enter_context(nc.semaphore(f"mx_s_{n}"))
        weights = {"expert_in": sb("expert_in", [P, 4 * P]), "shared_in": sb("shared_in", [P, 4 * P]),
                   "expert_out": sb("expert_out", [P, 2, NEX * P]), "shared_out": sb("shared_out", [P, 2, P])}
        high = {n: sb(f"{n}_high", list(t.shape), F32R) for n, t in weights.items()}
        low = {n: sb(f"{n}_low", list(t.shape), F32R) for n, t in weights.items()}
        out_bias = sb("out_bias", [NEX + 1, P])
        silu = {s: sb(f"silu_{s}", [P, 2, CH]) for s in "ES"}
        hid = {s: sb(f"hid_{s}", [P, 2, CH]) for s in "ES"}
        h = {s: [[sb(f"h_{s}{p}{q}", [P, 2, CH], F32R) for q in range(2)] for p in range(2)] for s in "ES"}
        f_parts = [[sb(f"f{p}{q}", [P, CH], F32R) for q in range(2)] for p in range(2)]
        weighted = sb("weighted", [P, NEX, P])
        R = [[sb(f"routed{p}{t}", [P, P]) for t in range(CT)] for p in range(2)]
        cnt_b = sb("cnt_chunk", [P, CT, NEX + 1])
        cnt_t = sb("cnt_turned", [NEX + 1, CH])
        a_ps = st.enter_context(nc.psum_tensor("mx_a", [P, 2, 512], F32))
        b_ps = st.enter_context(nc.psum_tensor("mx_b", [P, 2, 512], F32))
        e_ps = [st.enter_context(nc.psum_tensor(f"mx_e{n}", [P, 512], F32)) for n in range(2)]
        y_ps = st.enter_context(nc.psum_tensor("mx_y", [P, 512], F32))
        r_ps = st.enter_context(nc.psum_tensor("mx_r", [P, 512], F32))
        high_done, low_done, f_high, f_low, w_high, w_low = (sem(n) for n in ("high", "low", "f_high", "f_low", "w_high", "w_low"))
        (loaded, projected, silu_done, hidden, expert_done, weighed, reduced, cnt_kept, cnt_ps, cnt_out, y_done,
         added) = (sem(n) for n in (
             "loaded", "projected", "silu", "hidden", "expert", "weighed", "reduced", "cnt_kept", "cnt_ps", "cnt_out",
             "y_done", "added"))
        block = st.enter_context(nc.Block())

        def ahead(c):
            return not isinstance(c, int) or c + 2 < CHUNKS

        def loop(eng, body):
            body(0, 0, True, False)
            with eng.Fori(0, (CHUNKS - 3) // 2) as i:
                body(2 * i + 1, 1, False, False)
                body(2 * i + 2, 0, False, False)
            body(CHUNKS - 2, 1, False, False)
            body(CHUNKS - 1, 0, False, True)

        @block.sync
        def _(sp):
            for name in weights:
                sp.dma_start(weights[name][:], x[name]).then_inc(loaded, 16)
            sp.dma_start(out_bias[:], x["out_bias"]).then_inc(loaded, 16)

        @block.tensor
        def _(pe):
            def project(c, p, s):
                if s == "E":
                    pe.wait_ge(hidden, 2 * c)
                else:
                    pe.wait_ge(hidden, 2 * c + 1)
                pe.wait_ge(f_low, c + 1)
                name = "expert_in" if s == "E" else "shared_in"
                for ps, at in ((a_ps, 0), (b_ps, 2)):
                    for f in range(2):
                        cols = slice((at + f) * P, (at + f + 1) * P)
                        last = split_matmul(nc, ps[:, f, 0:CH], (high[name][:, cols], low[name][:, cols]),
                                            (f_parts[p][0][:], f_parts[p][1][:]), True, True)
                last.then_inc(projected, 1)

            def experts(c, p, t):
                if t == 0:
                    pe.wait_ge(low_done, 2 * c + 1)
                tokens = slice(t * P, (t + 1) * P)
                for a in range(2):
                    pe.wait_ge(weighed, 6 * c + 2 * t + a + 1)
                    for f in range(2):
                        cols = slice(a * 512, (a + 1) * 512)
                        last = split_matmul(nc, e_ps[a][:], [part[:, f, tokens] for part in h["E"][p]],
                                            (high["expert_out"][:, f, cols], low["expert_out"][:, f, cols]), f == 0, f == 1)
                    last.then_inc(expert_done, 1)

            def turn_cnt(c):
                pe.wait_ge(cnt_kept, c + 1)
                pe.wait_ge(added, 2 * c + 1)
                for t in range(CT):
                    last = nc.tensor.transpose(r_ps[0:NEX + 1, t * P:(t + 1) * P], cnt_b[:, t, :], k["ident"][:])
                last.then_inc(cnt_ps, 1)

            def finish(c, p):
                pe.wait_ge(low_done, 2 * c + 2)
                pe.wait_ge(added, 2 * c + 1)
                for f in range(2):
                    split_matmul(nc, y_ps[:, 0:CH], (high["shared_out"][:, f, :], low["shared_out"][:, f, :]),
                                 [part[:, f, :] for part in h["S"][p]], f == 0, False)
                pe.wait_ge(cnt_out, c + 1)
                nc.tensor.matmul(y_ps[:, 0:CH], out_bias[:], cnt_t[:], start=False, stop=True)
                pe.wait_ge(reduced, CT * c + CT)
                for t in range(CT):
                    last = nc.tensor.transpose(r_ps[:, t * P:(t + 1) * P], R[p][t][:], k["ident"][:])
                last.then_inc(y_done, 1)

            def body(c, p, first, final):
                experts(c, p, 0)
                if not first:
                    finish(c - 1, 1 - p)
                if not final:
                    project(c + 1, 1 - p, "E")
                experts(c, p, 1)
                turn_cnt(c)
                if not final:
                    project(c + 1, 1 - p, "S")
                experts(c, p, 2)

            pe.sem_inc(cnt_ps, 1)
            pe.wait_ge(loaded, 80)
            pe.wait_ge(w_low, len(weights))
            project(0, 0, "E")
            project(0, 0, "S")
            loop(pe, body)
            finish(CHUNKS - 1, 0)

        @block.scalar
        def _(act):
            def swish(c, s):
                act.wait_ge(projected, 2 * c + 1 + (s == "S"))
                nc.scalar.activation(silu[s][:], a_ps[:, :, 0:CH], ACT.Silu).then_inc(silu_done, 1)

            def body(c, p, first, final):
                if not final:
                    swish(c + 1, "E")
                act.wait_ge(cnt_ps, c + 2)
                nc.scalar.activation(cnt_t[:], r_ps[0:NEX + 1, 0:CH], ACT.Copy).then_inc(cnt_out, 1)
                if not final:
                    swish(c + 1, "S")

            swish(0, "E")
            swish(0, "S")
            loop(act, body)

        @block.gpsimd
        def _(pool):
            def keep(c):
                pool.wait_ge(cnt_ps, c + 1)
                nc.gpsimd.tensor_copy(cnt_b[:], cnt[:, bass.ds(c * CT, CT), :]).then_inc(cnt_kept, 1)

            def f_low_part(c, p):
                pool.wait_ge(f_high, c + 1)
                nc.gpsimd.tensor_tensor(f_parts[p][1][:], F[:, bass.ds(c * CH, CH)], f_parts[p][0][:], ALU.subtract).then_inc(f_low, 1)

            def hid_low_part(c, p, s):
                pool.wait_ge(high_done, 2 * c + 1 + (s == "S"))
                nc.gpsimd.tensor_tensor(h[s][p][1][:], hid[s][:], h[s][p][0][:], ALU.subtract).then_inc(low_done, 1)

            def body(c, p, first, final):
                keep(c)
                if not final:
                    hid_low_part(c + 1, 1 - p, "E")
                if ahead(c):
                    f_low_part(c + 2, p)
                if not final:
                    hid_low_part(c + 1, 1 - p, "S")

            f_low_part(0, 0)
            f_low_part(1, 1)
            for n, name in enumerate(weights):
                pool.wait_ge(w_high, n + 1)
                nc.gpsimd.tensor_tensor(low[name][:], weights[name][:], high[name][:], ALU.subtract).then_inc(w_low, 1)
            hid_low_part(0, 0, "E")
            hid_low_part(0, 0, "S")
            loop(pool, body)

        @block.vector
        def _(dve):
            def f_high_part(c, p):
                if not (isinstance(c, int) and c < 2):
                    dve.wait_ge(projected, 2 * c - 2)
                nc.vector.tensor_copy(f_parts[p][0][:], F[:, bass.ds(c * CH, CH)]).then_inc(f_high, 1)

            def hide(c, p, s):
                dve.wait_ge(silu_done, 2 * c + 1 + (s == "S"))
                if not (isinstance(c, int) and c == 0):
                    dve.wait_ge(low_done, 2 * c - 1 + (s == "S"))
                nc.vector.tensor_tensor(hid[s][:], silu[s][:], b_ps[:, :, 0:CH], ALU.mult).then_inc(hidden, 1)
                dve.wait_ge(hidden, 2 * c + 1 + (s == "S"))
                nc.vector.tensor_copy(h[s][p][0][:], hid[s][:]).then_inc(high_done, 1)

            def weigh(c, p, t):
                n = 6 * c + 2 * t
                for a in range(2):
                    dve.wait_ge(expert_done, n + a + 1)
                    by = comb[:, bass.ds(CT * c + t, 1), 4 * a:4 * a + 4].rearrange("p o e -> p (o e)").unsqueeze(2).broadcast_to([P, 4, P])
                    nc.vector.tensor_tensor(weighted[:, 4 * a:4 * a + 4, :], e_ps[a][:].rearrange("p (e d) -> p e d", e=4),
                                            by, ALU.mult).then_inc(weighed, 1)
                dve.wait_ge(weighed, n + 4)
                nc.vector.tensor_reduce(R[p][t][:], weighted[:].rearrange("p e d -> p d e"), AX.X, ALU.add).then_inc(reduced, 1)
                dve.wait_ge(reduced, CT * c + t + 1)

            def add(c):
                dve.wait_ge(y_done, c + 1)
                hc = H[:, bass.ds(c * CH, CH)]
                nc.vector.tensor_tensor(hc, hc, y_ps[:, 0:CH], ALU.add).then_inc(added, 1)
                dve.wait_ge(added, 2 * c + 2)
                nc.vector.tensor_tensor(hc, hc, r_ps[:, 0:CH], ALU.add).then_inc(added, 1)

            def body(c, p, first, final):
                weigh(c, p, 0)
                if not first:
                    add(c - 1)
                if not final:
                    hide(c + 1, 1 - p, "E")
                if ahead(c):
                    f_high_part(c + 2, p)
                weigh(c, p, 1)
                if not final:
                    hide(c + 1, 1 - p, "S")
                weigh(c, p, 2)

            dve.sem_inc(weighed, 2)
            dve.sem_inc(added, 1)
            f_high_part(0, 0)
            f_high_part(1, 1)
            dve.wait_ge(loaded, 16 * (len(weights) + 1))
            for name in weights:
                nc.vector.tensor_copy(high[name][:], weights[name][:]).then_inc(w_high, 1)
            hide(0, 0, "E")
            hide(0, 0, "S")
            loop(dve, body)
            add(CHUNKS - 1)


def build(nc, x, out):
    with ExitStack() as ctx:
        sb = lambda n, s, d=F32: ctx.enter_context(nc.sbuf_tensor(n, s, d))
        H = sb("H", [P, NTP])
        k = {"center": sb("center_sb", [P, P]), "mean32": sb("mean32_sb", [P, 32]), "pick_row": sb("pick_row_sb", [P, P]),
             "cols": sb("cols_sb", [P, NCOLS]), "ident": sb("ident_sb", [P, P]), "W1": sb("W1_sb", [P, 640]),
             "W2": sb("W2_sb", [P, 2, P]), "ones_bf": sb("ones_bf", [P, P], BF16), "b1_v3": sb("b1_v3", [P, EXPAND], BF16),
             "down_b3": sb("down_b3", [P, 4096], BF16), "rowmask": sb("rowmask_sb", [P, 3]),
             "same_expert": sb("same_expert_sb", [P, P]), "earlier_group": sb("earlier_group_sb", [P, P]),
             "router": sb("router_sb", [P, NE]), "group_row": sb("group_row_sb", [P, 4]), "lanes": sb("lanes_sb", [P, BLK])}
        k["ln_sems"] = {n: [ctx.enter_context(nc.semaphore(f"ln_{n}")), 0] for n in LN_TOTALS}
        load_inputs(nc, x, k, H)
        with ExitStack() as st:
            HN = st.enter_context(nc.sbuf_tensor("HN", [P, NT], F32))
            XN = st.enter_context(nc.sbuf_tensor("XN", [P, NT], F32))
            layernorm(nc, k, H, [HN, XN], [(1.0, 1e-5), (1.0 + 1e-6, 1e-11)], "ln1")
            scale_norm(nc, k, HN)
            gated_attention(nc, k, x, H, HN, XN)
        moe_first(nc, k, x, H)
        with ExitStack() as st:
            spiking_attention(nc, k, x, H)
        last_ffn(nc, k, x, H)
        store(nc, H, out)


def scale_norm(nc, k, HN):
    with ExitStack() as st:
        done = st.enter_context(nc.semaphore("norm_scaled"))
        block = st.enter_context(nc.Block())
        at, _ = COLS["norm"]

        @block.vector
        def _(dve):
            nc.vector.tensor_scalar(HN[:], HN[:], k["cols"][:, at:at + 1], None, ALU.mult).then_inc(done, 1)


def store(nc, H, out):
    with ExitStack() as st:
        stored = st.enter_context(nc.semaphore("stored"))
        block = st.enter_context(nc.Block())

        @block.sync
        def _(sp):
            sp.dma_start(out, H[:, 0:NT]).then_inc(stored, 16)
            sp.wait_ge(stored, 16)


def _arrays(inp):
    f = np.float32
    a = {}
    img = np.asarray(inp["x"]).reshape(B, 3, 6, 16, 6, 16).transpose(1, 3, 5, 0, 2, 4)
    a["patches"] = img.reshape(TOK_K, P, B * PATCHES)
    a["text"] = np.asarray(inp["txt"]).transpose(2, 0, 1)
    a["tok_w"] = np.asarray(inp["L0_tok_w"]).T.reshape(TOK_K, P, P)
    a["W1"] = np.asarray(inp["L0_attn_W1"])
    a["W2"] = np.asarray(inp["L0_attn_W2"]).reshape(2, P, P).transpose(1, 0, 2)
    b1 = np.asarray(inp["L0_attn_b1"])
    a["b1_v"] = b1[EXPAND:2 * EXPAND].reshape(1, EXPAND)
    a["down_b"] = np.asarray(inp["L0_ffn_b_down"]).reshape(1, NE * P)
    a["router"] = np.asarray(inp["L0_ffn_W_router"])
    up_b = np.zeros((8, 3 * P), f)
    up_b[:, :DFF] = np.asarray(inp["L0_ffn_b_up"])
    gate_b = np.concatenate([np.asarray(inp["L1_ffn_group_bias"]), np.asarray(inp["L1_ffn_expert_bias"])])
    parts = {
        "tok_b": np.asarray(inp["L0_tok_b"])[:, None], "b2": np.asarray(inp["L0_attn_b2"])[:, None],
        "gamma": np.asarray(inp["L0_attn_gamma"]).T, "beta": np.asarray(inp["L0_attn_beta"]).T,
        "norm": np.broadcast_to(np.asarray(inp["L0_attn_norm_scale"]).reshape(1, 1), (P, 1)),
        "b1_base": b1[2 * EXPAND:][:, None], "b1_u": b1[:EXPAND].reshape(2, P).T,
        "router_b": np.tile(np.asarray(inp["L0_ffn_b_router"]), NGRP)[:, None],
        "bn_gamma": np.asarray(inp["L1_attn_gamma"]).reshape(3, P).T, "bn_beta": np.asarray(inp["L1_attn_beta"]).reshape(3, P).T,
        "proj_b": np.asarray(inp["L1_attn_bproj"])[:, None], "ln_scale": np.asarray(inp["L1_ffn_ln_scale"])[:, None],
        "ln_bias": np.asarray(inp["L1_ffn_ln_bias"])[:, None],
        "up_b": up_b.reshape(24, P).T, "gate_b": np.broadcast_to(gate_b[None], (P, 10)),
    }
    a["cols"] = np.concatenate([parts[n] for n in COLS], axis=1)
    a["wqkv"] = np.asarray(inp["L1_attn_Wqkv"]).T
    a["wproj"] = np.asarray(inp["L1_attn_Wproj"]).T
    up = np.asarray(inp["L0_ffn_W_up"])
    a["up"] = up
    down = np.zeros((NE, 3 * P, P), f)
    down[:, :DFF] = np.asarray(inp["L0_ffn_W_down"])
    a["down"] = down.reshape(NE, 3, P, P).transpose(0, 2, 1, 3)
    a["shared_in"] = np.asarray(inp["L1_ffn_shared_in_w"]).T
    a["expert_in"] = np.asarray(inp["L1_ffn_expert_in_w"]).T
    a["shared_out"] = np.asarray(inp["L1_ffn_shared_out_w"]).T.reshape(2, P, P).transpose(1, 0, 2)
    a["expert_out"] = np.asarray(inp["L1_ffn_expert_out_weight"]).transpose(2, 0, 1).reshape(2, P, NEX * P).transpose(1, 0, 2)
    a["out_bias"] = np.concatenate([np.asarray(inp["L1_ffn_expert_out_bias"]), np.asarray(inp["L1_ffn_shared_out_b"])[None]], 0)
    a["gates"] = np.concatenate([np.asarray(inp["L1_ffn_group_gate_w"]), np.asarray(inp["L1_ffn_expert_gate_w"])], 0).T
    a["center"] = (np.eye(P) - 1.0 / P).astype(f)
    a["mean32"] = np.full((P, 32), 1.0 / P, f)
    a["pick_row"] = np.where(np.arange(P)[:, None] % 32 == 0, 1.0, 0.0).astype(f) * np.ones((1, P), f)
    a["ident"] = np.eye(P, dtype=f)
    lane = np.arange(P)
    a["same_expert"] = (lane[:, None] % NE == lane[None] % NE).astype(f)
    a["earlier_group"] = ((lane[:, None] % NE == lane[None] % NE) & (lane[:, None] // NE < lane[None] // NE)).astype(f)
    a["group_row"] = np.stack([lane // NE * SEG, lane // NE * BLK, lane % NE * BLOCKS, lane % 2 * 0], 1).astype(f)
    a["lanes"] = np.broadcast_to(np.arange(BLK, dtype=f), (P, BLK))
    a["empty_slots"] = (TRASH + BLK * NGRP + np.arange(NE * SLOTS) % SLOTS).reshape(-1, BLK).astype(np.int32)
    a["headmask"] = (lane[:, None] // HD == np.arange(HEADS)[None]).astype(f)
    a["rowmask"] = (lane[:, None] == 32 * np.arange(3)[None]).astype(f)
    inv_freq = (10000.0 ** (-np.arange(ROPE) / ROPE)).astype(f)
    angle = (np.arange(S, dtype=f)[None] * inv_freq[:, None]).astype(f).astype(np.float64)
    cos, sin = (fn(angle) / 128 for fn in (np.cos, np.sin))
    ct, stt = np.zeros((P, 3, S), f), np.zeros((P, 3, 2, S), f)
    for t, (m0, rows) in enumerate(MTILES):
        ct[:rows, t] = cos[m0:m0 + rows]
        stt[:rows, t, 0] = sin[m0:m0 + rows]
        stt[:rows, t, 1] = -sin[m0:m0 + rows]
    a["cos"], a["sin"] = ct, stt
    return {n: np.ascontiguousarray(v) for n, v in a.items()}


def kernel(**inputs):
    import concourse.bacc as _bacc
    from concourse.bass_utils import run_bass_kernel_spmd as _run

    nc = _bacc.Bacc("TRN2", target_bir_lowering=False, num_devices=1)
    arrays = _arrays(inputs)
    x = {n: nc.dram_tensor(f"in_{n}", a.shape, mybir.dt.from_np(a.dtype), kind="ExternalInput").ap() for n, a in arrays.items()}
    out = nc.dram_tensor("out_h", (P, NT), F32, kind="ExternalOutput").ap()
    build(nc, x, out)
    r = _run(nc, [{f"in_{n}": a for n, a in arrays.items()}], core_ids=[0])
    return r.results[0]["out_h"].reshape(P, B, S).transpose(1, 2, 0)
```

```python
import concourse.bass as bass
from concourse import mybir
from contextlib import ExitStack
import numpy as np

F32 = mybir.dt.float32
BF16 = mybir.dt.bfloat16
I32 = mybir.dt.int32
F32R = mybir.dt.float32r
ALU = mybir.AluOpType
ACT = mybir.ActivationFunctionType
AX = mybir.AxisListType

B = 16
P = 128
TEXT = 512
PATCHES = 36
S = TEXT + PATCHES
NT = B * S
HALF = S // 2
ROPE = S // 2
EXPAND = 256
TOK_K = 768 // P
NE = 32
NGRP = 4
SEG = NT // NGRP
SEGP = -(-SEG // 32) * 32
TOPK = NT // NE
BLK = 8
BLOCKS = -(-TOPK // BLK) + NGRP - 1
SLOTS = BLOCKS * BLK
SLOT_TILES = [(0, 128), (128, 128), (256, SLOTS - 256)]
ROUNDS = -(-TOPK // BLK)
TRASH = NT
NROWS = NT + 448
ROWW = P + NE
DFF = 341
FT = [(0, 128), (128, 128), (256, DFF - 256)]
HEADS = 8
HD = 16
CT = 3
CH = CT * P
TILES = -(-NT // CH) * CT
CHUNKS = TILES // CT
NTP = TILES * P
NEX = 8

BIAS_ROWS = NE + EXPAND // P

COLS = {}


def _columns():
    at = 0
    for name, n in [("tok_b", 1), ("b2", 1), ("gamma", 2), ("beta", 2), ("norm", 1), ("b1_base", 1), ("b1_u", 2),
                    ("router_b", 1), ("bn_gamma", 3), ("bn_beta", 3), ("proj_b", 1), ("ln_scale", 1), ("ln_bias", 1),
                    ("up_b", 8 * 3), ("gate_b", 10)]:
        COLS[name] = (at, n)
        at += n
    return at


NCOLS = _columns()
MTILES = [(0, 128), (128, 128), (256, ROPE - 256)]


LN_TOTALS = {"centred": lambda n: 8 * NGRP, "evacuated": lambda n: 8 * NGRP + 2, "squared": lambda n: 2 * NGRP,
             "var": lambda n: 4 * NGRP + 1, "std": lambda n: NGRP * n + 1, "rstd": lambda n: 3 * NGRP * n,
             "bc": lambda n: 4 * NGRP * n, "scaled": lambda n: 4 * NGRP * n + 2, "joined": lambda n: (4 * NGRP + 2) * (n - 1), "eps": lambda n: n}


def split_matmul(nc, out, weights, moving, start, stop):
    nc.tensor.matmul(out, weights[0], moving[0], start=start, stop=False)
    nc.tensor.matmul(out, weights[0], moving[1], start=False, stop=False)
    return nc.tensor.matmul(out, weights[1], moving[0], start=False, stop=stop)


def layernorm(nc, k, H, XN, variants, tag, gain=None):
    sets = NGRP
    with ExitStack() as st:
        sb = lambda n, s, d: st.enter_context(nc.sbuf_tensor(f"{tag}_{n}", s, d))
        ps = lambda n, s: st.enter_context(nc.psum_tensor(f"{tag}_{n}", s, F32))
        nv = len(variants)
        sq = [sb(f"square{g}", [P, S], F32) for g in range(NGRP)]
        rstd = [sb(f"rstd{v}", [P, 2, HALF], F32) for v in range(nv)]
        rstd_parts = [[sb(f"rstd{v}{part}", [P, 2, HALF], F32R) for part in range(2)] for v in range(nv)]
        eps = [sb(f"eps{v}", [P, 1], F32) for v in range(nv)]
        xc_ps = [ps(f"centred{j}", [P, 512]) for j in range(2)]
        var_ps = ps("var", [P, 2, 512])
        bc_ps = [ps(f"bcast{j}", [P, 2, 512]) for j in range(2)]
        centred, evacuated, squared, var_done, std_done, rstd_done, bc_done, scaled, joined, eps_set = (
            k["ln_sems"][n][0] for n in LN_TOTALS)
        (centred0, evacuated0, squared0, var0, std0, rstd0, bc0, scaled0, joined0, eps0) = (k["ln_sems"][n][1] for n in LN_TOTALS)
        for n, total in LN_TOTALS.items():
            k["ln_sems"][n][1] += total(nv)
        for_h = [sb(f"for_h{j}", [P, S], F32) for j in range(2)] if nv == 2 else None
        base = XN
        block = st.enter_context(nc.Block())

        def tokens(t, i, g, j):
            return t[:, bass.ds(((g * NGRP) + i) * S + j * HALF, HALF)]

        def whole(t, i, g):
            return t[:, bass.ds(((g * NGRP) + i) * S, S)]

        @block.tensor
        def _(pe):
            def center(i):
                for g in range(NGRP):
                    for j in range(2):
                        pe.wait_ge(evacuated, evacuated0 + 8 * i + 2 * g + j + 1)
                        nc.tensor.matmul(xc_ps[j][:, 0:HALF], k["center"][:], tokens(H, i, g, j),
                                         start=True, stop=True).then_inc(centred, 1)

            def variance(i):
                for g in range(NGRP):
                    if g % 2 == 0:
                        pe.wait_ge(squared, squared0 + 2 * i + g // 2 + 1)
                    else:
                        pe.wait_ge(evacuated, evacuated0 + 8 * i + 2 * g + 2 + 2)
                    if g == 0:
                        pe.wait_ge(std_done, std0 + nv * i + 1)
                    for j in range(2):
                        last = nc.tensor.matmul(var_ps[32 * g:32 * g + 32, j, 0:HALF], k["mean32"][:],
                                                sq[g][:, j * HALF:(j + 1) * HALF], start=True, stop=True)
                    last.then_inc(var_done, 1)

            def broadcast(i, which=range(nv * NGRP)):
                for vg in which:
                    v, g = divmod(vg, NGRP)
                    if g == 0:
                        pe.wait_ge(rstd_done, rstd0 + 3 * (nv * i + v) + 3)
                    n = (4 * v + g) % 2
                    pe.wait_ge(scaled, scaled0 + 4 * nv * i + 4 * v + g + 1)
                    for j in range(2):
                        for part in range(2):
                            last = nc.tensor.matmul(bc_ps[n][:, j, 0:HALF], k["pick_row_r"][32 * g:32 * g + 32, :],
                                                    rstd_parts[v][part][32 * g:32 * g + 32, j, :], start=part == 0, stop=part == 1)
                    last.then_inc(bc_done, 1)

            pe.sem_inc(var_done, 1)
            center(0)
            variance(0)
            with pe.Fori(0, sets - 1) as i:
                center(i + 1)
                broadcast(i, range(2))
                variance(i + 1)
                broadcast(i, range(2, nv * NGRP))
            broadcast(sets - 1)

        @block.scalar
        def _(act):
            act.sem_inc(evacuated, 2)
            act.sem_inc(std_done, 1)
            act.wait_ge(eps_set, eps0 + nv)

            def evacuate(i):
                for g in range(NGRP):
                    for j in range(2):
                        act.wait_ge(centred, centred0 + 8 * i + 2 * g + j + 1)
                        last = nc.scalar.activation(tokens(base, i, g, j), xc_ps[j][:, 0:HALF], ACT.Copy)
                        if g % 2 == 1:
                            last = nc.scalar.activation(sq[g][:, j * HALF:(j + 1) * HALF], xc_ps[j][:, 0:HALF], ACT.Square)
                        last.then_inc(evacuated, 1)

            def std(i):
                act.wait_ge(var_done, var0 + 4 * i + 5)
                if not (isinstance(i, int) and i == 0):
                    act.wait_ge(rstd_done, rstd0 + 3 * nv * i)
                for v, (a, _) in enumerate(variants):
                    nc.scalar.activation(rstd[v][:], var_ps[:, :, 0:HALF], ACT.Sqrt, bias=eps[v][:], scale=a).then_inc(std_done, 1)

            evacuate(0)
            std(0)
            with act.Fori(0, sets - 1) as i:
                evacuate(i + 1)
                std(i + 1)

        @block.gpsimd
        def _(pool):
            def square(i):
                for g in range(0, NGRP, 2):
                    pool.wait_ge(evacuated, evacuated0 + 8 * i + 2 * g + 2 + 2)
                    pool.wait_ge(var_done, var0 + 4 * i + 1)
                    nc.gpsimd.tensor_tensor(sq[g][:], whole(base, i, g), whole(base, i, g), ALU.mult).then_inc(squared, 1)

            def add_to_h(i):
                for g in range(NGRP):
                    pool.wait_ge(scaled, scaled0 + 4 * nv * i + g + 3)
                    nc.gpsimd.tensor_tensor(whole(H, i, g), whole(H, i, g), for_h[g % 2][:], ALU.add).then_inc(joined, 1)

            square(0)
            with pool.Fori(0, sets - 1) as i:
                square(i + 1)
                if nv == 2:
                    add_to_h(i)
            if nv == 2:
                add_to_h(sets - 1)

        @block.vector
        def _(dve):
            dve.sem_inc(scaled, 2)
            if nv == 2:
                dve.sem_inc(joined, 2)
            for v, (_, b) in enumerate(variants):
                nc.vector.memset(eps[v][:], b).then_inc(eps_set, 1)
            with dve.Fori(0, sets) as i:
                for v in range(nv):
                    dve.wait_ge(std_done, std0 + nv * i + v + 2)
                    n = rstd0 + 3 * (nv * i + v)
                    nc.vector.reciprocal(rstd[v][:], rstd[v][:]).then_inc(rstd_done, 1)
                    dve.wait_ge(rstd_done, n + 1)
                    high, low = rstd_parts[v]
                    if gain is not None and v == nv - 1:
                        nc.vector.tensor_scalar(high[:], rstd[v][:], gain, None, ALU.mult).then_inc(rstd_done, 1)
                        dve.wait_ge(rstd_done, n + 2)
                        nc.vector.scalar_tensor_tensor(low[:], rstd[v][:], gain, high[:], ALU.mult, ALU.subtract).then_inc(rstd_done, 1)
                    else:
                        nc.vector.tensor_copy(high[:], rstd[v][:]).then_inc(rstd_done, 1)
                        dve.wait_ge(rstd_done, n + 2)
                        nc.vector.tensor_tensor(low[:], rstd[v][:], high[:], ALU.subtract).then_inc(rstd_done, 1)
                for v in range(nv):
                    for g in range(NGRP):
                        n = (4 * v + g) % 2
                        dve.wait_ge(bc_done, bc0 + 4 * nv * i + 4 * v + g + 1)
                        if v == 0 and g % 2 == 0:
                            dve.wait_ge(squared, squared0 + 2 * i + g // 2 + 1)
                        dst = whole(XN, i, g)
                        if v < nv - 1:
                            dst = for_h[g % 2][:]
                            dve.wait_ge(joined, joined0 + 4 * i + g + 1)
                        nc.vector.tensor_tensor(
                            dst.rearrange("p (a b) -> p a b", a=2),
                            whole(base, i, g).rearrange("p (a b) -> p a b", a=2),
                            bc_ps[n][:, :, 0:HALF], ALU.mult).then_inc(scaled, 1)


def load_inputs(nc, x, k, H):
    with ExitStack() as st:
        sem = lambda n: st.enter_context(nc.semaphore(f"in_{n}"))
        patches = st.enter_context(nc.sbuf_tensor("patches", [P, TOK_K, B * PATCHES], F32))
        tok_w = st.enter_context(nc.sbuf_tensor("tok_w_sb", [P, TOK_K, P], F32))
        emb = [st.enter_context(nc.psum_tensor(f"embedding{j}", [P, 512], F32)) for j in range(2)]
        parts_d = nc.dram_tensor("bias_parts", [3, BIAS_ROWS, P], BF16, kind="Internal").ap()
        bias_rest = st.enter_context(nc.sbuf_tensor("bias_rest", [BIAS_ROWS, P], F32))
        bias_part = [st.enter_context(nc.sbuf_tensor(f"bias_part{n}", [BIAS_ROWS, P], BF16)) for n in range(3)]
        img_in, text_in, const_in, embedded, evacuated, bias_in, cut, laid = (
            sem(n) for n in ("image", "text", "const", "embedded", "evacuated", "bias", "cut", "laid"))
        half = B * PATCHES // 2
        Hb = H[:, 0:NT].rearrange("p (b s) -> p b s", b=B)
        block = st.enter_context(nc.Block())
        consts = [("center", "center"), ("mean32", "mean32"), ("pick_row", "pick_row"), ("cols", "cols"),
                  ("ident", "ident"), ("W1", "W1"), ("W2", "W2"), ("same_expert", "same_expert"),
                  ("earlier_group", "earlier_group"), ("router", "router"), ("group_row", "group_row"), ("lanes", "lanes")]

        @block.sync
        def _(sp):
            sp.dma_start(bias_rest[:], x["bias_rows"]).then_inc(bias_in, 16)
            sp.dma_start(patches[:], x["patches"].rearrange("k p n -> p k n")).then_inc(img_in, 16)
            sp.dma_start(tok_w[:], x["tok_w"].rearrange("k p n -> p k n")).then_inc(img_in, 16)
            sp.dma_start(Hb[:, :, PATCHES:S], x["text"]).then_inc(text_in, 16)
            sp.wait_ge(cut, 6)
            for part in range(3):
                sp.dma_start(parts_d[part], bias_part[part][:]).then_inc(laid, 16)
            sp.wait_ge(laid, 48)
            for part in range(3):
                r = slice(32 * part, 32 * part + 1)
                sp.dma_start(k["down_b3"][r, :], parts_d[part:part + 1, 0:NE, :].rearrange("o e d -> o (e d)")).then_inc(laid, 16)
                sp.dma_start(k["b1_v3"][r, :], parts_d[part:part + 1, NE:BIAS_ROWS, :].rearrange("o e d -> o (e d)")).then_inc(laid, 16)
            sp.wait_ge(laid, 144)
            sp.wait_ge(img_in, 32)
            sp.wait_ge(text_in, 16)

        @block.scalar
        def _(act):
            for name, src in consts:
                act.dma_start(k[name][:], x[src]).then_inc(const_in, 16)
            act.wait_ge(const_in, 16 * len(consts))
            at, _ = COLS["tok_b"]
            for j in range(2):
                act.wait_ge(embedded, j + 1)
                nc.scalar.activation(Hb[:, 8 * j:8 * j + 8, 0:PATCHES],
                                     emb[j][:, 0:half].rearrange("p (b s) -> p b s", b=8),
                                     ACT.Identity, bias=k["cols"][:, at:at + 1]).then_inc(evacuated, 1)

        @block.tensor
        def _(pe):
            pe.wait_ge(img_in, 32)
            for j in range(2):
                for t in range(TOK_K):
                    last = nc.tensor.matmul(emb[j][:, 0:half], tok_w[:, t, :], patches[:, t, j * half:(j + 1) * half],
                                            start=t == 0, stop=t == TOK_K - 1)
                last.then_inc(embedded, 1)

        @block.vector
        def _(dve):
            nc.vector.memset(k["b1_v3"][:], 0.0)
            nc.vector.memset(k["down_b3"][:], 0.0).then_inc(cut, 1)
            dve.wait_ge(bias_in, 16)
            for part in range(3):
                nc.vector.tensor_copy(bias_part[part][:], bias_rest[:]).then_inc(cut, 1)
                dve.wait_ge(cut, 2 * part + 2)
                if part < 2:
                    nc.vector.tensor_tensor(bias_rest[:], bias_rest[:], bias_part[part][:], ALU.subtract).then_inc(cut, 1)
                    dve.wait_ge(cut, 2 * part + 3)
            nc.vector.memset(k["ones_bf"][:], 1.0)
            nc.vector.memset(H[:, NT:NTP], 0.0)
            dve.wait_ge(const_in, 16 * len(consts))
            nc.vector.tensor_copy(k["pick_row_r"][:], k["pick_row"][:])


def gated_attention(nc, k, x, H, HN, moe_d):
    with ExitStack() as st:
        sb = lambda n, s, d=F32: st.enter_context(nc.sbuf_tensor(f"ga_{n}", s, d))
        ps = lambda n, s: st.enter_context(nc.psum_tensor(f"ga_{n}", s, F32))
        sem = lambda n: st.enter_context(nc.semaphore(f"ga_{n}"))
        cos = sb("cos", [P, 3, S])
        sin = sb("sin", [P, 3, 2, S])
        hs = [[sb(f"hs{p}{part}", [P, S], F32R) for part in range(2)] for p in range(2)]
        q_parts = [[sb(f"q{p}{part}", [P, S], F32R) for part in range(2)] for p in range(2)]
        key_parts = [[sb(f"k{p}{part}", [P, S], F32R) for part in range(2)] for p in range(2)]
        W1p = [sb(f"W1_{part}", [P, 5 * P], F32R) for part in range(2)]
        base = sb("base", [P, 2, HALF])
        q = sb("q", [P, S])
        key = sb("k", [P, S])
        u = [sb(f"u{p}", [P, 2, 2, HALF]) for p in range(2)]
        v = [sb(f"v{p}", [P, 5, EXPAND]) for p in range(2)]
        by_cos = [sb(f"by_cos{p}", [P, 2, HALF]) for p in range(2)]
        by_sin = [sb(f"by_sin{p}", [P, 2, HALF]) for p in range(2)]
        rot = [sb(f"rot{p}", [P, 2, HALF]) for p in range(2)]
        kern = [sb(f"kern{p}", [P, 2, HALF]) for p in range(2)]
        kern_tail = [sb(f"kern_tail{j}", [64, HALF]) for j in range(2)]
        zeros = sb("zeros", [P, NROWS // 4])
        zeros_set, filled = sem("zeros_set"), sem("filled")
        ukv = [sb(f"ukv{j}", [P, 2, HALF]) for j in range(2)]
        misc = ps("misc", [P, 2, 512])
        scores = [ps(f"scores{p}", [P, 2, 512]) for p in range(2)]
        kv = ps("kv", [P, 2, 512])
        (tables_in, cleared, qk_done, rot_done, sum_done, relu_done, kern_done, kv_done, gated, base_ps, base_sb,
         qk_ready, u_ps, u_sb, v_ps, v_sb, hs_ready, w2_ps, resid) = (sem(n) for n in (
            "tables", "cleared", "qk", "rot", "sum", "relu", "kern", "kv_done", "gated", "base_ps", "base_sb",
            "qk_ready", "u_ps", "u_sb", "v_ps", "v_sb", "hs_ready", "w2", "resid"))
        met, hs_low, qk_low, w_cut = sem("met"), sem("hs_low"), sem("qk_low"), sem("w_cut")
        tail0, tail = MTILES[2]
        TAIL2 = 32
        W1, W2 = k["W1"], k["W2"]

        def col(name, n=0):
            at, _ = COLS[name]
            return k["cols"][:, at + n:at + n + 1]

        def batch(t, b):
            return t[:, bass.ds(b * S, S)]

        def half(t, b, j):
            return t[:, bass.ds(b * S + j * HALF, HALF)]

        block = st.enter_context(nc.Block())

        @block.sync
        def _(sp):
            sp.dma_start(cos[:], x["cos"]).then_inc(tables_in, 16)
            sp.dma_start(sin[:], x["sin"]).then_inc(tables_in, 16)
            rows_d, y_d, slots_d = moe_d
            sp.wait_ge(zeros_set, 1)
            w = NROWS // 4
            for sums in y_d:
                yv = sums.rearrange("(p r) d -> p (r d)", p=P)
                for c in range(4):
                    sp.dma_start(yv[:, c * w:(c + 1) * w], zeros[:]).then_inc(filled, 16)
            sp.dma_start(rows_d[NT:NROWS, :].rearrange("(p r) d -> p (r d)", p=64), zeros[0:64, 0:(NROWS - NT) * ROWW // 64]).then_inc(filled, 16)
            sp.dma_start(slots_d, x["empty_slots"]).then_inc(filled, 16)
            sp.wait_ge(filled, 16 * 10)

        @block.tensor
        def _(pe):
            def project(p, col0):
                for j in range(2):
                    last = split_matmul(nc, misc[:, j, 0:HALF], [w[:, col0:col0 + P] for w in W1p],
                                        [part[:, j * HALF:(j + 1) * HALF] for part in hs[p]], True, True)
                return last

            def project_base(b, p):
                pe.wait_ge(hs_low, b + 1)
                project(p, 2 * EXPAND).then_inc(base_ps, 1)

            def project_u(b, p, e):
                if e == 0:
                    pe.wait_ge(base_sb, b + 1)
                else:
                    pe.wait_ge(u_sb, 2 * b + 1)
                project(p, e * P).then_inc(u_ps, 1)

            def project_v(b, p, tails):
                if tails:
                    pe.wait_ge(v_sb, 2 * b + 1)
                    tiles = [(tail0, tail, 0, 0), (ROPE + tail0, tail, 0, 1)]
                else:
                    pe.wait_ge(u_sb, 2 * b + 2)
                    tiles = [(m0, P, t // 2, t % 2) for t, m0 in enumerate((0, P, ROPE, ROPE + P))]
                for m0, rows, bank, side in tiles:
                    out = misc[0:rows, bank, side * EXPAND:(side + 1) * EXPAND]
                    split_matmul(nc, out, [part[:, m0:m0 + rows] for part in hs[p]],
                                 [w[:, EXPAND:2 * EXPAND] for w in W1p], True, False)
                    last = nc.tensor.matmul(out, k["ones_bf"][:, 0:rows], k["b1_v3"][:], start=False, stop=True)
                last.then_inc(v_ps, 1)

            def down(b, first_wait):
                first_wait()
                pe.wait_ge(gated, 2 * b + 2)
                for j in range(2):
                    for e in range(2):
                        last = nc.tensor.matmul(misc[:, j, 0:HALF], W2[:, e, :], ukv[j][:, e, :], start=e == 0, stop=e == 1)
                last.then_inc(w2_ps, 1)

            def score(b, p, g, first=False):
                j, mt = divmod(g, 3)
                m0, rows = MTILES[mt]
                if g == 0:
                    pe.wait_ge(qk_low, 2 * b + 2)
                if not first:
                    pe.wait_ge(rot_done, 6 * b + g - 1)
                for side in range(2):
                    m = slice(side * ROPE + m0, side * ROPE + m0 + rows)
                    last = split_matmul(nc, scores[g % 2][0:rows, side, 0:HALF], [part[:, m] for part in key_parts[p]],
                                        [part[:, j * HALF:(j + 1) * HALF] for part in q_parts[p]], True, True)
                last.then_inc(qk_done, 1)

            def weigh(b, p, g, first=False):
                j, mt = divmod(g, 3)
                pe.wait_ge(kern_done, 6 * b + g + 1)
                if mt == 0 and not (first and j == 0):
                    pe.wait_ge(gated, 2 * b + j)
                if g == 0:
                    pe.wait_ge(v_sb, 2 * b + 2)
                for e in range(2):
                    if mt < 2:
                        for side in range(2):
                            last = nc.tensor.matmul(kv[:, e, 0:HALF], v[p][:, mt + 2 * side, e * P:(e + 1) * P],
                                                    kern[g % 2][:, side, :], start=mt == 0 and side == 0, stop=False)
                    else:
                        last = nc.tensor.matmul(kv[:, e, 0:HALF], v[p][0:TAIL2 + tail, 4, e * P:(e + 1) * P],
                                                kern_tail[j][0:TAIL2 + tail, :], start=False, stop=True)
                last.then_inc(kv_done, 1)

            def units(b, p, first=False, final=False):
                for g in range(6):
                    if g < 4:
                        score(b, p, g + 2)
                    if g >= 4:
                        weigh(b, p, g, first)
                    if g >= 4 and not final:
                        score(b + 1, 1 - p, g - 4)
                    if g < 4:
                        weigh(b, p, g, first)
                    if g == 0 and not first:
                        down(b - 1, lambda: pe.wait_ge(v_sb, 2 * b + 2))
                    if final:
                        continue
                    if g == 1:
                        if first:
                            pe.wait_ge(v_sb, 2)
                        else:
                            pe.wait_ge(resid, b)
                        project_base(b + 1, 1 - p)
                    if g in (2, 3):
                        project_u(b + 1, 1 - p, g - 2)
                    if g >= 4:
                        project_v(b + 1, 1 - p, g == 5)

            pe.wait_ge(w_cut, 2)
            project_base(0, 0)
            project_u(0, 0, 0)
            project_u(0, 0, 1)
            project_v(0, 0, False)
            project_v(0, 0, True)
            score(0, 0, 0, True)
            score(0, 0, 1, True)
            units(0, 0, first=True)
            with pe.Fori(0, (B - 2) // 2) as i:
                units(2 * i + 1, 1)
                units(2 * i + 2, 0)
            units(B - 1, 1, final=True)
            down(B - 1, lambda: pe.wait_ge(resid, B - 1))

        @block.scalar
        def _(act):
            def base_out(b, first=False):
                act.wait_ge(base_ps, b + 1)
                if not first:
                    act.wait_ge(qk_ready, 2 * b)
                nc.scalar.activation(base[:], misc[:, :, 0:HALF], ACT.Silu, bias=col("b1_base")).then_inc(base_sb, 1)

            def u_out(b, p, e, first=False):
                act.wait_ge(u_ps, 2 * b + e + 1)
                if e == 0 and not first:
                    act.wait_ge(gated, 2 * b - 2)
                nc.scalar.activation(u[p][:, e], misc[:, :, 0:HALF], ACT.Silu, bias=col("b1_u", e)).then_inc(u_sb, 1)

            def v_out(b, p, tails, first=False):
                act.wait_ge(v_ps, 2 * b + tails + 1)
                if not tails:
                    if not first:
                        act.wait_ge(kv_done, 6 * b - 6)
                    last = nc.scalar.activation(v[p][:, 0:4, :], misc[:].rearrange("p b (s n) -> p (b s) n", s=2), ACT.Silu)
                else:
                    for side in range(2):
                        last = nc.scalar.activation(v[p][TAIL2 * side:TAIL2 * side + tail, 4, :],
                                                    misc[0:tail, 0, side * EXPAND:(side + 1) * EXPAND], ACT.Silu)
                last.then_inc(v_sb, 1)

            def kernel_of(b, g, first=False):
                j, mt = divmod(g, 3)
                _, rows = MTILES[mt]
                n = 6 * b + g
                for side in range(2):
                    act.wait_ge(sum_done, 2 * n + side + 1)
                    last = nc.scalar.activation(rot[g % 2][0:rows, side], rot[g % 2][0:rows, side], ACT.Relu)
                last.then_inc(relu_done, 1)
                act.wait_ge(relu_done, n + 1)
                if not first:
                    act.wait_ge(kv_done, n - 1)
                if mt < 2:
                    last = nc.scalar.activation(kern[g % 2][:], rot[g % 2][:], ACT.Square)
                else:
                    for side in range(2):
                        last = nc.scalar.activation(kern_tail[j][TAIL2 * side:TAIL2 * side + rows, :], rot[g % 2][0:rows, side, :], ACT.Square)
                last.then_inc(kern_done, 1)

            def units(b, p, first=False, final=False):
                for g in range(6):
                    if g < 5:
                        kernel_of(b, g + 1, first and g == 0)
                    elif not final:
                        kernel_of(b + 1, 0)
                    if final:
                        continue
                    if g == 1:
                        base_out(b + 1)
                    if g in (2, 3):
                        u_out(b + 1, 1 - p, g - 2, first)
                    if g >= 4:
                        v_out(b + 1, 1 - p, g == 5, first)

            act.wait_ge(cleared, 1)
            base_out(0, True)
            u_out(0, 0, 0, True)
            u_out(0, 0, 1, True)
            v_out(0, 0, False, True)
            v_out(0, 0, True, True)
            kernel_of(0, 0, True)
            units(0, 0, first=True)
            with act.Fori(0, (B - 2) // 2) as i:
                units(2 * i + 1, 1)
                units(2 * i + 2, 0)
            units(B - 1, 1, final=True)

        @block.gpsimd
        def _(pool):
            def keep_hn(b, p, first=False):
                if not first:
                    pool.wait_ge(v_ps, 2 * b - 2)
                nc.gpsimd.tensor_copy(hs[p][0][:], batch(HN, b)).then_inc(hs_ready, 1)

            def make(b, p, n, first=False):
                pool.wait_ge(base_sb, b + 1)
                if not first:
                    pool.wait_ge(qk_done, 6 * b - 6)
                    pool.wait_ge(qk_low, 2 * b)
                pool.sem_inc(met, 1)
                flat = base[:].rearrange("p a b -> p (a b)")
                for dst in ((q, q_parts[p][0]), (key, key_parts[p][0]))[n]:
                    last = nc.gpsimd.tensor_scalar(dst[:], flat, col("gamma", n), col("beta", n), ALU.mult, ALU.add)
                last.then_inc(qk_ready, 1)

            def add(b, g, first=False):
                _, rows = MTILES[g % 3]
                n = 6 * b + g
                pool.wait_ge(rot_done, n + 1)
                if not first:
                    pool.wait_ge(kern_done, n - 1)
                a, c = by_cos[g % 2], by_sin[g % 2]
                nc.gpsimd.tensor_tensor(rot[g % 2][0:rows, 0], a[0:rows, 0], c[0:rows, 1], ALU.add).then_inc(sum_done, 1)
                nc.gpsimd.tensor_tensor(rot[g % 2][0:rows, 1], a[0:rows, 1], c[0:rows, 0], ALU.add).then_inc(sum_done, 1)

            def units(b, p, first=False, final=False):
                for g in range(6):
                    if g < 5:
                        add(b, g + 1, first and g == 0)
                    elif not final:
                        add(b + 1, 0)
                    if g == 0 and not final:
                        keep_hn(b + 1, 1 - p, first)
                    if final:
                        continue
                    if g in (2, 3):
                        make(b + 1, 1 - p, g - 2, first)

            for j in range(2):
                nc.gpsimd.memset(kern_tail[j][:], 0.0)
            for p in range(2):
                last = nc.gpsimd.memset(v[p][:, 4, :], 0.0)
            last.then_inc(cleared, 1)
            keep_hn(0, 0, True)
            make(0, 0, 0, True)
            make(0, 0, 1, True)
            add(0, 0, True)
            units(0, 0, first=True)
            with pool.Fori(0, (B - 2) // 2) as i:
                units(2 * i + 1, 1)
                units(2 * i + 2, 0)
            units(B - 1, 1, final=True)

        @block.vector
        def _(dve):
            def rotate(b, g, first=False):
                j, mt = divmod(g, 3)
                _, rows = MTILES[mt]
                n = 6 * b + g
                dve.wait_ge(qk_done, n + 1)
                if not first:
                    dve.wait_ge(sum_done, 2 * n - 2)
                xs = scores[g % 2][0:rows, :, 0:HALF]
                cj = cos[0:rows, mt, j * HALF:(j + 1) * HALF].unsqueeze(1).broadcast_to([rows, 2, HALF])
                nc.vector.tensor_tensor(by_cos[g % 2][0:rows], xs, cj, ALU.mult)
                nc.vector.tensor_tensor(by_sin[g % 2][0:rows], xs, sin[0:rows, mt, :, j * HALF:(j + 1) * HALF], ALU.mult).then_inc(rot_done, 1)

            def tokens_low(b, p):
                dve.wait_ge(hs_ready, b + 1)
                nc.vector.tensor_tensor(hs[p][1][:], batch(HN, b), hs[p][0][:], ALU.subtract).then_inc(hs_low, 1)

            def low_of(b, p, n):
                whole, parts = ((q, q_parts[p]), (key, key_parts[p]))[n]
                dve.wait_ge(qk_ready, 2 * b + n + 1)
                nc.vector.tensor_tensor(parts[1][:], whole[:], parts[0][:], ALU.subtract).then_inc(qk_low, 1)

            def gate(b, p, j, first=False):
                dve.wait_ge(kv_done, 6 * b + 3 * j + 3)
                if not first:
                    dve.wait_ge(w2_ps, b)
                nc.vector.tensor_tensor(ukv[j][:], kv[:, :, 0:HALF], u[p][:, :, j, :], ALU.mult).then_inc(gated, 1)

            def residual(b):
                dve.wait_ge(w2_ps, b + 1)
                hb = batch(H, b).rearrange("p (a b) -> p a b", a=2)
                nc.vector.scalar_tensor_tensor(hb, misc[:, :, 0:HALF], col("b2"), hb, ALU.add, ALU.add).then_inc(resid, 1)

            def units(b, p, first=False, final=False):
                for g in range(6):
                    if g < 5:
                        rotate(b, g + 1, first and g == 0)
                    elif not final:
                        rotate(b + 1, 0)
                    if g == 0 and not final:
                        tokens_low(b + 1, 1 - p)
                    if g == 1 and not first:
                        residual(b - 1)
                    if g in (2, 5):
                        gate(b, p, g // 3, first)
                    if g in (3, 4) and not final:
                        low_of(b + 1, 1 - p, g - 3)

            nc.vector.memset(zeros[:], 0.0).then_inc(zeros_set, 1)
            nc.vector.tensor_copy(W1p[0][:], W1[:]).then_inc(w_cut, 1)
            dve.wait_ge(w_cut, 1)
            nc.vector.tensor_tensor(W1p[1][:], W1[:], W1p[0][:], ALU.subtract).then_inc(w_cut, 1)
            tokens_low(0, 0)
            low_of(0, 0, 0)
            low_of(0, 0, 1)
            dve.wait_ge(tables_in, 32)
            rotate(0, 0, True)
            units(0, 0, first=True)
            with dve.Fori(0, (B - 2) // 2) as i:
                units(2 * i + 1, 1)
                units(2 * i + 2, 0)
            units(B - 1, 1, final=True)
            residual(B - 1)


def moe_first(nc, k, x, H, moe_d):
    rows_d, y_d, slots_d = moe_d
    with ExitStack() as st:
        sb = lambda n, s, d=F32: st.enter_context(nc.sbuf_tensor(n, s, d))
        L = sb("router_logits", [P, SEGP])
        with ExitStack() as lnst:
            XN = lnst.enter_context(nc.sbuf_tensor("XN2", [P, NT], F32))
            layernorm(nc, k, H, XN, [(1.0, 1e-5)], "ln2")
            token_rows(nc, k, XN, L, rows_d)
        idx = sb("slot_tokens", [P, 3, NE], I32)
        choose_tokens(nc, k, x, L, rows_d, slots_d, idx)
        run_experts(nc, k, x, idx, rows_d, y_d)
    add_rows(nc, k, H, y_d)


def token_rows(nc, k, XN, L, rows_d):
    with ExitStack() as st:
        sb = lambda n, s, d=F32: st.enter_context(nc.sbuf_tensor(f"tr_{n}", s, d))
        ps = lambda n, s: st.enter_context(nc.psum_tensor(f"tr_ps_{n}", s, F32))
        sem = lambda n: st.enter_context(nc.semaphore(f"tr_s_{n}"))
        xs = [sb(f"xs{p}", [P, S]) for p in range(2)]
        rows = [sb(f"rows{p}", [P, 5, P]) for p in range(2)]
        logit_ps = ps("logits", [P, 2, 512])
        row_ps = [ps(f"row{p}", [P, 2, 512]) for p in range(2)]
        kept, logits, logits_out, turned, copied = (
            sem(n) for n in ("kept", "logits", "logits_out", "turned", "copied"))
        stored = [sem(f"stored{p}") for p in range(2)]
        tail = S - 4 * P
        block = st.enter_context(nc.Block())

        @block.scalar
        def _(act):
            act.sem_inc(logits_out, 1)
            at, _ = COLS["router_b"]
            with act.Fori(0, NGRP) as i:
                for g in range(NGRP):
                    act.wait_ge(turned, 4 * i + g + 1)
                    nc.scalar.activation(xs[g % 2][:], XN[:, bass.ds((g * NGRP + i) * S, S)], ACT.Copy).then_inc(kept, 1)
                act.wait_ge(logits, i + 1)
                nc.scalar.activation(L[:, bass.ds(i * S, S)].rearrange("p (a b) -> p a b", a=2), logit_ps[:, :, 0:HALF],
                                     ACT.Identity, bias=k["cols"][:, at:at + 1]).then_inc(logits_out, 1)

        @block.tensor
        def _(pe):
            pe.sem_inc(turned, 2)
            with pe.Fori(0, NGRP) as i:
                for g in range(NGRP):
                    n = 4 * i + g
                    if g == 0:
                        pe.wait_ge(logits_out, i + 1)
                    pe.wait_ge(kept, n + 1)
                    for j in range(2):
                        last = nc.tensor.matmul(logit_ps[32 * g:32 * g + 32, j, 0:HALF], k["router"][:],
                                                xs[g % 2][:, j * HALF:(j + 1) * HALF], start=True, stop=True)
                    if g == NGRP - 1:
                        last.then_inc(logits, 1)
                    pe.wait_ge(copied, n + 1)
                    for t in range(4):
                        nc.tensor.transpose(row_ps[g % 2][:, 0, t * P:(t + 1) * P], xs[g % 2][:, t * P:(t + 1) * P], k["ident"][:])
                    nc.tensor.transpose(row_ps[g % 2][0:tail, 1, 0:P], xs[g % 2][:, 4 * P:S], k["ident"][:]).then_inc(turned, 1)

        @block.vector
        def _(dve):
            dve.sem_inc(copied, 2)
            nc.vector.memset(L[:, SEG:SEGP], 0.0)
            with dve.Fori(0, NGRP) as i:
                for g in range(NGRP):
                    n = 4 * i + g
                    dve.wait_ge(turned, n + 3)
                    dve.wait_ge(stored[g % 2], 32 * (2 * i + g // 2) + 16)
                    nc.vector.tensor_copy(rows[g % 2][:, 0:4, :], row_ps[g % 2][:, 0, :].rearrange("p (t d) -> p t d", t=4))
                    nc.vector.tensor_copy(rows[g % 2][0:tail, 4, :], row_ps[g % 2][0:tail, 1, 0:P]).then_inc(copied, 1)

        @block.sync
        def _(sp):
            for p in range(2):
                sp.sem_inc(stored[p], 16)
            with sp.Fori(0, NGRP) as i:
                for g in range(NGRP):
                    n = 4 * i + g
                    t0 = (g * NGRP + i) * S
                    sp.wait_ge(copied, n + 3)
                    sp.dma_start(rows_d[bass.ds(t0, 4 * P), 0:P].rearrange("(t p) d -> p t d", p=P), rows[g % 2][:, 0:4, :]).then_inc(stored[g % 2], 16)
                    sp.dma_start(rows_d[bass.ds(t0 + 4 * P, tail), 0:P], rows[g % 2][0:tail, 4, :]).then_inc(stored[g % 2], 16)
            for p in range(2):
                sp.wait_ge(stored[p], 16 * B + 16)


def choose_tokens(nc, k, x, L, rows_d, slots_d, idx):
    with ExitStack() as st:
        sb = lambda n, s, d=F32: st.enter_context(nc.sbuf_tensor(f"ct_{n}", s, d))
        ps = lambda n, s: st.enter_context(nc.psum_tensor(f"ct_ps_{n}", s, F32))
        sem = lambda n: st.enter_context(nc.semaphore(f"ct_s_{n}"))
        NB32 = SEGP // 32
        T = sb("turned", [P, SEGP])
        PR = sb("probs", [P, SEGP])
        V = sb("order", [P, SEGP])
        mark = sb("mark", [P, SEGP], BF16)
        desc_i = sb("desc_i", [P, SEGP], I32)
        desc = sb("desc", [P, SEGP])
        mx = sb("mx", [P, NB32])
        sm = sb("sm", [P, NB32])
        rs = sb("rs", [P, NB32])
        found, bit, cand, won = (sb(n, [P, 1], I32) for n in ("found", "bit", "cand", "won"))
        cnt, n_gt, n_ge, n_eq, take, room, n_blk, first_row, rnd = (
            sb(n, [P, 1]) for n in ("cnt", "n_gt", "n_ge", "n_eq", "take", "room", "n_blk", "first_row", "rnd"))
        blk_i = sb("blk_i", [P, 1], I32)
        pos = sb("pos", [P, BLK])
        dummy = sb("dummy", [P, BLK])
        top = [sb(f"top{p}", [P, BLK]) for p in range(2)]
        tok = sb("tok", [P, BLK])
        ok = sb("ok", [P, BLK])
        ids = [sb(f"ids{p}", [P, BLK], I32) for p in range(2)]
        row_f = sb("row_f", [P, 1])
        row = [sb(f"row{p}", [P, 1], I32) for p in range(2)]
        open_ = sb("open", [P, 1])
        n_left_f = sb("n_left_f", [1, 1])
        n_left = sb("n_left", [1, 1], I32)
        n_round_f = sb("n_round_f", [1, 1])
        n_round = sb("n_round", [1, 1], I32)
        lst_i = sb("lst_i", [NE, SLOTS], I32)
        lst = sb("lst", [NE, SLOTS])
        tot = ps("tot", [P, 4])
        blk_ps = ps("blk", [1, P])
        idx_ps = ps("idx", [P, 3, NE])
        (step, exps, counted, summed, probs_out, desc_done, rounds_known, id_ready, id_sent, lists_in, lists_f,
         turned, extra, met, id_free) = (sem(n) for n in ("step", "exps", "counted", "summed", "probs_out", "desc_done", "rounds_known",
                                            "id_ready", "id_sent", "lists_in", "lists_f", "turned", "extra", "met", "id_free"))
        step2, counted2, summed2, left_known = (sem(n) for n in ("step2", "counted2", "summed2", "left_known"))
        T3 = T[:].rearrange("p (j e) -> p j e", e=32)
        group_row = k["group_row"]
        BITS = 30
        EARLY = 21
        N1 = EARLY + 2
        block = st.enter_context(nc.Block())

        @block.vector
        def _(dve):
            chain = [0]

            def link(ins):
                chain[0] += 1
                ins.then_inc(step, 1)
                dve.wait_ge(step, chain[0])

            dve.sem_inc(id_free, 2)
            nc.vector.memset(bit[:], 1 << (BITS - 1))
            nc.vector.memset(idx[:], 0)
            nc.vector.memset(found[:], 0)
            nc.vector.memset(rnd[:], 0.0)
            link(nc.vector.transpose(T[:], L[:]))
            link(nc.vector.tensor_reduce(mx[:], T3, AX.X, ALU.max))
            link(nc.vector.tensor_tensor(T3, T3, mx[:].unsqueeze(2).broadcast_to([P, NB32, 32]), ALU.subtract))
            dve.wait_ge(exps, 1)
            link(nc.vector.tensor_reduce(sm[:], T3, AX.X, ALU.add))
            link(nc.vector.reciprocal(rs[:], sm[:]))
            link(nc.vector.tensor_tensor(T3, T3, rs[:].unsqueeze(2).broadcast_to([P, NB32, 32]), ALU.mult))
            link(nc.vector.transpose(PR[:], T[:]))
            link(nc.vector.memset(PR[:, SEG:SEGP], -1.0))
            def narrow(i, at, step, counted, summed):
                nc.vector.tensor_tensor(cand[:], found[:], bit[:], ALU.bitwise_or).then_inc(step, 1)
                dve.wait_ge(step, at + 1)
                nc.vector.tensor_scalar(mark[:], PR[:], cand[:].bitcast(F32), None, ALU.is_ge, ALU.add, accum_out=cnt[:]).then_inc(counted, 1)
                dve.wait_ge(summed, i + 1)
                nc.vector.scalar_tensor_tensor(won[:], tot[:, 0:1], float(TOPK), bit[:], ALU.is_ge, ALU.mult).then_inc(step, 1)
                dve.wait_ge(step, at + 2)
                nc.vector.tensor_tensor(found[:], found[:], won[:], ALU.bitwise_or).then_inc(step, 1)
                nc.vector.tensor_single_scalar(bit[:], bit[:], 1, ALU.logical_shift_right).then_inc(step, 1)
                dve.wait_ge(step, at + 4)

            s0 = chain[0]
            with dve.Fori(0, EARLY) as i:
                narrow(i, s0 + 4 * i, step, counted, summed)
            chain[0] += 4 * EARLY
            nc.vector.tensor_scalar(mark[:], PR[:], found[:].bitcast(F32), None, ALU.is_ge, ALU.add, accum_out=cnt[:]).then_inc(counted, 1)
            dve.wait_ge(summed, EARLY + 1)
            nc.vector.tensor_scalar(open_[:], tot[:, 0:1], float(TOPK), None, ALU.is_gt).then_inc(counted, 1)
            dve.wait_ge(summed, EARLY + 2)
            link(nc.vector.reduce_max(n_left_f[:], blk_ps[:], AX.X))
            link(nc.vector.tensor_scalar(n_left[:], n_left_f[:], float(BITS - EARLY - 1), 1.0, ALU.mult, ALU.add))
            dve.sem_inc(left_known, 1)
            left = nc.vector.value_load(n_left[0:1, 0:1], min_val=1, max_val=BITS - EARLY)
            with dve.Fori(0, left) as i:
                narrow(i, 4 * i, step2, counted2, summed2)
            thr = found[:].bitcast(F32)
            dve.wait_ge(desc_done, 1)
            link(nc.vector.tensor_copy(desc[:], desc_i[:]))
            link(nc.vector.tensor_scalar(mark[:], PR[:], thr, None, ALU.is_ge, ALU.add, accum_out=n_ge[:]))
            link(nc.vector.scalar_tensor_tensor(V[:], PR[:], thr, desc[:], ALU.is_ge, ALU.mult))
            nc.vector.tensor_scalar(mark[:], PR[:], thr, None, ALU.is_gt, ALU.add, accum_out=n_gt[:]).then_inc(counted, 1)
            dve.wait_ge(counted, N1 + 1)
            link(nc.vector.scalar_tensor_tensor(V[:], mark[:], 4096.0, V[:], ALU.mult, ALU.add))
            nc.vector.tensor_tensor(n_eq[:], n_ge[:], n_gt[:], ALU.subtract).then_inc(counted, 1)
            dve.wait_ge(summed, N1 + 1)
            link(nc.vector.tensor_scalar(room[:], tot[:, 1:2], -1.0, float(TOPK), ALU.mult, ALU.add))
            link(nc.vector.tensor_tensor(room[:], room[:], tot[:, 2:3], ALU.subtract))
            link(nc.vector.tensor_scalar(room[:], room[:], 0.0, n_eq[:], ALU.max, ALU.min))
            link(nc.vector.tensor_tensor(take[:], n_gt[:], room[:], ALU.add))
            link(nc.vector.tensor_scalar(blk_i[:], take[:], float(BLK - 1), None, ALU.add))
            link(nc.vector.tensor_single_scalar(blk_i[:], blk_i[:], 3, ALU.logical_shift_right))
            nc.vector.tensor_copy(n_blk[:], blk_i[:]).then_inc(counted, 1)
            dve.wait_ge(summed, N1 + 2)
            link(nc.vector.tensor_tensor(first_row[:], tot[:, 3:4], group_row[:, 2:3], ALU.add))
            link(nc.vector.reduce_max(n_round_f[:], blk_ps[:], AX.X))
            link(nc.vector.tensor_scalar(n_round[:], n_round_f[:], 1.0, None, ALU.add))
            link(nc.vector.tensor_single_scalar(n_round[:], n_round[:], 1, ALU.logical_shift_right))
            dve.sem_inc(rounds_known, 1)
            nc.vector.tensor_copy(pos[:], k["lanes"][:])
            link(nc.vector.tensor_scalar(dummy[:], k["lanes"][:], group_row[:, 1:2], float(TRASH), ALU.add, ALU.add))
            steps = nc.vector.value_load(n_round[0:1, 0:1], min_val=1, max_val=(ROUNDS + 1) // 2)
            s1 = chain[0]
            with dve.Fori(0, steps) as i:
                for p in range(2):
                    at = s1 + (i * 2 + p) * 6
                    nc.vector.max(top[p][:], V[:]).then_inc(step, 1)
                    dve.wait_ge(step, at + 1)
                    nc.vector.tensor_single_scalar(ok[:], top[p][:], 4096.0, ALU.is_gt)
                    nc.vector.match_replace(V[:], top[p][:], V[:], -1.0).then_inc(step, 1)
                    dve.wait_ge(step, at + 2)
                    nc.vector.scalar_tensor_tensor(tok[:], ok[:], 4096.0, top[p][:], ALU.mult, ALU.subtract).then_inc(step, 1)
                    dve.wait_ge(step, at + 3)
                    nc.vector.scalar_tensor_tensor(tok[:], tok[:], group_row[:, 0:1], dummy[:], ALU.add, ALU.subtract)
                    nc.vector.tensor_scalar(ok[:], pos[:], take[:], None, ALU.is_lt)
                    nc.vector.tensor_scalar(row_f[:], rnd[:], n_blk[:], 50000.0, ALU.is_ge, ALU.mult).then_inc(step, 1)
                    dve.wait_ge(step, at + 4)
                    nc.vector.scalar_tensor_tensor(row_f[:], rnd[:], first_row[:], row_f[:], ALU.add, ALU.add)
                    nc.vector.tensor_scalar_add(pos[:], pos[:], float(BLK))
                    nc.vector.scalar_tensor_tensor(tok[:], tok[:], 4096.0, ok[:], ALU.add, ALU.mult).then_inc(step, 1)
                    dve.wait_ge(id_free, 2 * i + p + 1)
                    dve.wait_ge(step, at + 5)
                    nc.vector.tensor_tensor(ids[p][:], tok[:], dummy[:], ALU.add)
                    nc.vector.tensor_copy(row[p][:], row_f[:])
                    nc.vector.tensor_scalar_add(rnd[:], rnd[:], 1.0).then_inc(step, 1)
                    dve.wait_ge(step, at + 6)
                    dve.sem_inc(id_ready, 1)
            dve.wait_ge(lists_in, 16)
            nc.vector.tensor_copy(lst[:], lst_i[:]).then_inc(lists_f, 1)
            dve.wait_ge(turned, 1)
            nc.vector.tensor_copy(idx[:, 0:2, :], idx_ps[:, 0:2, :])
            nc.vector.tensor_copy(idx[0:SLOTS - 256, 2, :], idx_ps[0:SLOTS - 256, 2, :]).then_inc(lists_f, 1)

        @block.scalar
        def _(act):
            act.wait_ge(step, 3)
            nc.scalar.activation(T[:], T[:], ACT.Exp).then_inc(exps, 1)

        @block.tensor
        def _(pe):
            def total(i, counted, summed):
                pe.wait_ge(counted, i + 1)
                nc.tensor.matmul(tot[:, 0:1], k["same_expert"][:], cnt[:], start=True, stop=True).then_inc(summed, 1)

            with pe.Fori(0, EARLY) as i:
                total(i, counted, summed)
            total(EARLY, counted, summed)
            pe.wait_ge(counted, EARLY + 2)
            nc.tensor.matmul(blk_ps[:], open_[:], k["ident"][:], start=True, stop=True).then_inc(summed, 1)
            pe.wait_ge(left_known, 1)
            left = nc.tensor.value_load(n_left[0:1, 0:1], min_val=1, max_val=BITS - EARLY)
            with pe.Fori(0, left) as i:
                total(i, counted2, summed2)
            pe.wait_ge(counted, N1 + 2)
            nc.tensor.matmul(tot[:, 1:2], k["same_expert"][:], n_gt[:], start=True, stop=True)
            nc.tensor.matmul(tot[:, 2:3], k["earlier_group"][:], n_eq[:], start=True, stop=True).then_inc(summed, 1)
            pe.wait_ge(counted, N1 + 3)
            nc.tensor.matmul(tot[:, 3:4], k["earlier_group"][:], n_blk[:], start=True, stop=True)
            nc.tensor.matmul(blk_ps[:], n_blk[:], k["ident"][:], start=True, stop=True).then_inc(summed, 1)
            pe.wait_ge(lists_f, 1)
            for t, (s0, n) in enumerate(SLOT_TILES):
                last = nc.tensor.transpose(idx_ps[0:n, t, :], lst[:, s0:s0 + n], k["ident"][0:NE, 0:NE])
            last.then_inc(turned, 1)

        @block.sync
        def _(sp):
            sp.wait_ge(step, 6)
            whole = SEG // 32
            part = SEG - 32 * whole
            for g in range(NGRP):
                q0 = slice(32 * g, 32 * g + 32)
                sp.dma_start(rows_d[g * SEG:g * SEG + 32 * whole, P:ROWW].rearrange("(j t) e -> t j e", t=32),
                             T3[q0, 0:whole, :]).then_inc(probs_out, 16)
                sp.dma_start(rows_d[g * SEG + 32 * whole:(g + 1) * SEG, P:ROWW], T3[32 * g:32 * g + part, whole, :]).then_inc(probs_out, 16)
            sp.wait_ge(probs_out, 16 * 2 * NGRP)
            sp.wait_ge(extra, 1)
            sp.dma_start(lst_i[:], slots_d.rearrange("(e b) j -> e (b j)", e=NE)).then_inc(lists_in, 16)
            sp.wait_ge(lists_in, 16)

        @block.gpsimd
        def _(pool):
            nc.gpsimd.iota(desc_i[:], pattern=[[-1, SEGP]], base=4096, channel_multiplier=0).then_inc(desc_done, 1)
            pool.wait_ge(rounds_known, 1)
            steps = nc.gpsimd.value_load(n_round[0:1, 0:1], min_val=1, max_val=(ROUNDS + 1) // 2)
            with pool.Fori(0, steps) as i:
                for p in range(2):
                    pool.wait_ge(id_ready, 2 * i + p + 1)
                    pool.sem_inc(met, 1)
                    nc.gpsimd.indirect_dma_start(out=slots_d, out_offset=bass.IndirectOffsetOnAxis(ap=row[p][:], axis=0),
                                                 in_=ids[p][:], in_offset=None, bounds_check=NE * BLOCKS - 1,
                                                 oob_is_err=False).then_inc(id_sent, 16)
                    pool.wait_ge(id_sent, 16 * (2 * i + p + 1))
                    pool.sem_inc(id_free, 1)
            pool.sem_inc(extra, 1)


def run_experts(nc, k, x, idx, rows_d, y_d):
    with ExitStack() as st:
        sb = lambda n, s, d=F32: st.enter_context(nc.sbuf_tensor(f"ex_{n}", s, d))
        ps = lambda n, s: st.enter_context(nc.psum_tensor(f"ex_ps_{n}", s, F32))
        sem = lambda n: st.enter_context(nc.semaphore(f"ex_s_{n}"))
        ids = [sb(f"ids{p}", [P, 3], I32) for p in range(4)]
        rows = [sb(f"rows{p}", [P, 3, ROWW]) for p in range(4)]
        xt = [sb(f"xt{p}", [P, SLOTS]) for p in range(2)]
        hid = [sb(f"hid{p}", [P, 3, SLOTS]) for p in range(2)]
        down = [sb(f"down{p}", [P, 3, P]) for p in range(2)]
        up = [sb(f"up{p}", [P, DFF]) for p in range(2)]
        y = [sb(f"y{p}", [P, 3, P]) for p in range(4)]
        xt_ps = [ps(f"xt{p}", [P, 512]) for p in range(2)]
        up_ps = ps("up", [P, 3, 512])
        y_ps = [ps(f"y{p}", [P, 3, P]) for p in range(2)]
        up_in, down_in = ([sem(f"{n}{p}") for p in range(2)] for n in ("up_in", "down_in"))
        gathered = [sem(f"gathered{p}") for p in range(4)]
        added = [sem(f"added{p}") for p in range(2)]
        (turned, xt_out, up_done, hid_done, y_done, y_out, met, y_free, ids_kept) = (
            sem(n) for n in ("turned", "xt_out", "up_done", "hid_done", "y_done",
                             "y_out", "met", "y_free", "ids_kept"))
        met_act = sem("met_act")
        STEP = 8
        block = st.enter_context(nc.Block())

        @block.sync
        def _(sp):
            with sp.Fori(0, NE // STEP) as i:
                for m in range(STEP):
                    e = i * STEP + m
                    if m % 4 == 0:
                        sp.wait_ge(up_done, 3 * (e - 4) + 24)
                        sp.dma_start(up[m // 4][:], x["up"][bass.ds(i * 2 + m // 4, 1), :, :].rearrange("a h f -> h (a f)")).then_inc(up_in[m // 4], 16)
                    sp.wait_ge(y_done, e + 1)
                    sp.dma_start(down[m % 2][:], x["down"][bass.ds(e, 1)].rearrange("a p t d -> p (a t) d")).then_inc(down_in[m % 2], 16)

        @block.gpsimd
        def _(pool):
            def gather(e, p):
                nc.gpsimd.tensor_copy(ids[p][:], idx[:, :, bass.ds(e, 1)].rearrange("p t a -> p (t a)")).then_inc(ids_kept, 1)
                pool.wait_ge(ids_kept, e + 1)
                pool.sem_inc(met, 1)
                for t, (_, n) in enumerate(SLOT_TILES):
                    nc.gpsimd.indirect_dma_start(out=rows[p][0:n, t, :], out_offset=None, in_=rows_d,
                                                 in_offset=bass.IndirectOffsetOnAxis(ap=ids[p][0:n, t:t + 1], axis=0)).then_inc(gathered[p], 16)

            def freed(p, nth):
                if not (isinstance(nth, int) and nth == 0):
                    pool.wait_ge(added[p % 2], 48 * nth)
                pool.sem_inc(y_free, 1)

            def scatter(e, p):
                pool.wait_ge(y_out, 3 * e + 3 + 6)
                pool.sem_inc(met, 1)
                for t, (_, n) in enumerate(SLOT_TILES):
                    nc.gpsimd.indirect_dma_start(out=y_d[p % 2], out_offset=bass.IndirectOffsetOnAxis(ap=ids[p][0:n, t:t + 1], axis=0),
                                                 in_=y[p][0:n, t, :], in_offset=None, compute_op=ALU.add).then_inc(added[p % 2], 16)

            pool.sem_inc(y_free, 2)
            gather(0, 0)
            gather(1, 1)
            for e in range(4):
                freed(e, e // 2)
                gather(e + 2, (e + 2) % 4)
                scatter(e, e)
            with pool.Fori(0, NE // 4 - 2) as i:
                for m in range(4):
                    freed(m, 2 * i + 2 + m // 2)
                    gather(4 * i + m + 6, (m + 2) % 4)
                    scatter(4 * i + m + 4, m)
            for e in range(NE - 4, NE):
                freed(e, e // 2)
                if e + 2 < NE:
                    gather(e + 2, (e + 2) % 4)
                scatter(e, e % 4)
            for p in range(2):
                pool.wait_ge(added[p], 24 * NE)

        @block.tensor
        def _(pe):
            def turn(e, r, nth):
                p = r % 2
                pe.wait_ge(gathered[r], 48 * nth + 48)
                pe.wait_ge(xt_out, e + 1)
                for t, (s0, n) in enumerate(SLOT_TILES):
                    last = nc.tensor.transpose(xt_ps[p][:, s0:s0 + n], rows[r][0:n, t, 0:P], k["ident"][0:n, 0:n])
                last.then_inc(turned, 1)

            def project_up(e, p, w, nth):
                pe.wait_ge(up_in[w], 16 * nth + 16)
                pe.wait_ge(xt_out, e + 3)
                for f, (f0, m) in enumerate(FT):
                    pe.wait_ge(hid_done, 3 * e + f + 1)
                    nc.tensor.matmul(up_ps[0:m, f, 0:SLOTS], up[w][:, f0:f0 + m], xt[p][:], start=True, stop=True).then_inc(up_done, 1)

            def project_down(e, p, nth):
                pe.wait_ge(hid_done, 3 * e + 6)
                pe.wait_ge(down_in[p], 16 * nth + 16)
                pe.wait_ge(y_out, 3 * e + 3)
                for t, (s0, n) in enumerate(SLOT_TILES):
                    for f, (_, m) in enumerate(FT):
                        nc.tensor.matmul(y_ps[p][0:n, t, :], hid[p][0:m, f, s0:s0 + n], down[p][0:m, f, :], start=f == 0, stop=False)
                    last = nc.tensor.matmul(y_ps[p][0:n, t, :], k["ones_bf"][:, 0:n], k["down_b3"][:, bass.ds(e * P, P)], start=False, stop=True)
                last.then_inc(y_done, 1)

            pe.sem_inc(up_done, 24)
            pe.sem_inc(y_done, 2)
            turn(0, 0, 0)
            project_up(0, 0, 0, 0)
            with pe.Fori(0, NE // STEP - 1) as i:
                for m in range(STEP):
                    e = i * STEP + m
                    project_down(e, m % 2, 4 * i + m // 2)
                    turn(e + 1, (m + 1) % 4, 2 * i + (m + 1) // 4)
                    project_up(e + 1, (m + 1) % 2, (m + 1) // 4 % 2, i + (m + 1) // 8)
            for e in range(NE - STEP, NE):
                project_down(e, e % 2, e // 2)
                if e + 1 < NE:
                    turn(e + 1, (e + 1) % 4, (e + 1) // 4)
                    project_up(e + 1, (e + 1) % 2, (e + 1) // 4 % 2, (e + 1) // STEP)

        @block.scalar
        def _(act):
            act.sem_inc(hid_done, 3)
            act.sem_inc(xt_out, 2)
            at, _ = COLS["up_b"]
            with act.Fori(0, NE // STEP) as i:
                for m in range(STEP):
                    e = i * STEP + m
                    p = m % 2
                    act.wait_ge(turned, e + 1)
                    act.wait_ge(up_done, 3 * e - 3 + 24)
                    nc.scalar.activation(xt[p][:], xt_ps[p][:, 0:SLOTS], ACT.Copy).then_inc(xt_out, 1)
                    act.wait_ge(y_done, e + 1)
                    for f, (_, rows_f) in enumerate(FT):
                        act.wait_ge(up_done, 3 * e + f + 1 + 24)
                        bias = k["cols"][0:rows_f, bass.ds(at + (i * 2 + m // 4) * 3 + f, 1)]
                        act.sem_inc(met_act, 1)
                        nc.scalar.activation(hid[p][0:rows_f, f, :], up_ps[0:rows_f, f, 0:SLOTS], ACT.Silu, bias=bias).then_inc(hid_done, 1)

        @block.vector
        def _(dve):
            dve.sem_inc(y_out, 6)
            with dve.Fori(0, NE // 4) as i:
                for m in range(4):
                    e = 4 * i + m
                    p = m % 2
                    dve.wait_ge(y_done, e + 3)
                    dve.wait_ge(y_free, e + 1)
                    for t, (_, n) in enumerate(SLOT_TILES):
                        prob = rows[m][0:n, t, bass.ds(P + e, 1)]
                        nc.vector.tensor_scalar(y[m][0:n, t, :], y_ps[p][0:n, t, :], prob, None, ALU.mult).then_inc(y_out, 1)


def add_rows(nc, k, H, y_d):
    with ExitStack() as st:
        sem = lambda n: st.enter_context(nc.semaphore(f"ar_{n}"))
        NBUF = 4
        rows = [[st.enter_context(nc.sbuf_tensor(f"ar_rows{p}{q}", [P, 5, P], F32)) for q in range(2)] for p in range(NBUF)]
        out_ps = [st.enter_context(nc.psum_tensor(f"ar_ps{p}", [P, 2, 512], F32)) for p in range(NBUF)]
        turned, summed, joined = sem("turned"), sem("summed"), sem("joined")
        loaded = [sem(f"loaded{p}") for p in range(NBUF)]
        tail = S - 4 * P
        block = st.enter_context(nc.Block())

        @block.sync
        def _(sp):
            sp.sem_inc(turned, NBUF)
            with sp.Fori(0, B // NBUF) as i:
                for p in range(NBUF):
                    c = NBUF * i + p
                    sp.wait_ge(turned, c + 1)
                    for q in range(2):
                        at = c * S
                        sp.dma_start(rows[p][q][:, 0:4, :], y_d[q][bass.ds(at, 4 * P), :].rearrange("(t p) d -> p t d", p=P)).then_inc(loaded[p], 16)
                        sp.dma_start(rows[p][q][0:tail, 4, :], y_d[q][bass.ds(at + 4 * P, tail), :]).then_inc(loaded[p], 16)

        @block.gpsimd
        def _(pool):
            with pool.Fori(0, B // NBUF) as i:
                for p in range(NBUF):
                    pool.wait_ge(loaded[p], 64 * i + 64)
                    for n, t in ((P, slice(0, 4)), (tail, slice(4, 5))):
                        last = nc.gpsimd.tensor_tensor(rows[p][0][0:n, t], rows[p][0][0:n, t], rows[p][1][0:n, t], ALU.add)
                    last.then_inc(joined, 1)

        @block.tensor
        def _(pe):
            pe.sem_inc(summed, NBUF)
            with pe.Fori(0, B // NBUF) as i:
                for p in range(NBUF):
                    c = NBUF * i + p
                    pe.wait_ge(joined, c + 1)
                    pe.wait_ge(summed, c + 1)
                    for t in range(4):
                        nc.tensor.transpose(out_ps[p][:, 0, t * P:(t + 1) * P], rows[p][0][:, t, :], k["ident"][:])
                    nc.tensor.transpose(out_ps[p][:, 1, 0:tail], rows[p][0][0:tail, 4, :], k["ident"][0:tail, 0:tail]).then_inc(turned, 1)

        @block.vector
        def _(dve):
            with dve.Fori(0, B // NBUF) as i:
                for p in range(NBUF):
                    c = NBUF * i + p
                    dve.wait_ge(turned, NBUF + c + 1)
                    for at, n, bank in ((0, 4 * P, 0), (4 * P, tail, 1)):
                        hb = H[:, bass.ds(c * S + at, n)]
                        last = nc.vector.tensor_tensor(hb, hb, out_ps[p][:, bank, 0:n], ALU.add)
                    last.then_inc(summed, 1)


MAGIC = float(1 << 23)
UPWARD = 1.0 + 2.0 ** -23


def spiking_attention(nc, k, x, H):
    with ExitStack() as st:
        sb = lambda n, s, d=F32: st.enter_context(nc.sbuf_tensor(f"sa_{n}", s, d))
        QKV = sb("qkv", [P, 3, NT])
        scale = sb("scale", [P, 3])
        shift = sb("shift", [P, 3])
        with ExitStack() as lnst:
            XN = lnst.enter_context(nc.sbuf_tensor("XN3", [P, NT], F32))
            layernorm(nc, k, H, XN, [(1.0, 1e-5)], "ln3")
            project_qkv(nc, k, x, XN, QKV, scale, shift)
        attend(nc, k, x, H, QKV, scale, shift)


def project_qkv(nc, k, x, XN, QKV, scale, shift):
    with ExitStack() as st:
        sb = lambda n, s, d=F32: st.enter_context(nc.sbuf_tensor(f"pq_{n}", s, d))
        sem = lambda n: st.enter_context(nc.semaphore(f"pq_s_{n}"))
        w = sb("w", [P, 3 * P])
        w3 = sb("w3", [P, 3, 3 * P], BF16)
        spikes = [sb(f"spikes{p}", [P, S], BF16) for p in range(2)]
        stats = sb("stats", [P, 3, 2 * B, 6])
        mv = sb("mv", [P, 3, 2])
        eps = sb("eps", [P, 1])
        tmp = sb("tmp", [P, 3])
        NQ = 4
        q_ps = [st.enter_context(nc.psum_tensor(f"pq_ps{n}", [P, 2, 512], F32)) for n in range(NQ)]
        w_in, cut, clipped, spiked, projected, kept, counted, met, stats_done, std_done = (
            sem(n) for n in ("w_in", "cut", "clipped", "spiked", "projected", "kept", "counted", "met", "stats", "std"))
        block = st.enter_context(nc.Block())

        @block.sync
        def _(sp):
            sp.dma_start(w[:], x["wqkv"]).then_inc(w_in, 16)

        @block.tensor
        def _(pe):
            pe.sem_inc(projected, 1)
            pe.wait_ge(cut, 7)
            with pe.Fori(0, B // NQ) as i:
                for m in range(NQ):
                    c = NQ * i + m
                    pe.wait_ge(spiked, 2 * c + 2)
                    for t in range(3):
                        n = 3 * c + t
                        pe.wait_ge(kept, n + 1)
                        for j in range(2):
                            for part in range(3):
                                last = nc.tensor.matmul(q_ps[(3 * m + t) % NQ][:, j, 0:HALF], w3[:, part, t * P:(t + 1) * P],
                                                        spikes[m % 2][:, j * HALF:(j + 1) * HALF], start=part == 0, stop=part == 2)
                        last.then_inc(projected, 1)

        @block.scalar
        def _(act):
            act.sem_inc(kept, NQ)
            with act.Fori(0, B // NQ) as i:
                for m in range(NQ):
                    for t in range(3):
                        n = 3 * (NQ * i + m) + t
                        act.wait_ge(projected, n + 2)
                        act.sem_inc(met, 1)
                        nc.scalar.activation(QKV[:, t, bass.ds((NQ * i + m) * S, S)].rearrange("p (a b) -> p a b", a=2),
                                             q_ps[(3 * m + t) % NQ][:, :, 0:HALF], ACT.Copy).then_inc(kept, 1)
            act.wait_ge(stats_done, 1)
            nc.scalar.activation(tmp[:], mv[:, :, 1], ACT.Sqrt, bias=eps[:], scale=1.0).then_inc(std_done, 1)

        @block.vector
        def _(dve):
            dve.wait_ge(w_in, 16)
            for part in range(3):
                nc.vector.tensor_copy(w3[:, part, :], w[:]).then_inc(cut, 1)
                dve.wait_ge(cut, 2 * part + 1)
                nc.vector.tensor_tensor(w[:], w[:], w3[:, part, :], ALU.subtract).then_inc(cut, 1)
                dve.wait_ge(cut, 2 * part + 2)
            nc.vector.memset(eps[:], 1e-5).then_inc(cut, 1)

            def spike(c, p):
                xb = XN[:, bass.ds(c * S, S)]
                nc.vector.tensor_scalar(xb, xb, 4.0, 0.0, ALU.min, ALU.max).then_inc(clipped, 1)
                dve.wait_ge(clipped, c + 1)
                dve.wait_ge(projected, 3 * c - 2)
                dve.sem_inc(met, 1)
                nc.vector.tensor_scalar(xb, xb, UPWARD, MAGIC, ALU.mult, ALU.add).then_inc(spiked, 1)
                dve.wait_ge(spiked, 2 * c + 1)
                nc.vector.tensor_scalar(spikes[p][:], xb, MAGIC, None, ALU.subtract).then_inc(spiked, 1)

            def count(c, m):
                for t in range(3):
                    n = 3 * c + t
                    dve.wait_ge(kept, NQ + n + 1)
                    dve.sem_inc(met, 1)
                    for j in range(2):
                        last = nc.vector.bn_stats(stats[:, t, bass.ds(2 * c + j, 1), :].rearrange("p a b -> p (a b)"),
                                                  QKV[:, t, bass.ds(c * S + j * HALF, HALF)])
                    last.then_inc(counted, 1)

            def first_spike(c, p):
                xb = XN[:, c * S:(c + 1) * S]
                nc.vector.tensor_scalar(xb, xb, 4.0, 0.0, ALU.min, ALU.max).then_inc(clipped, 1)
                dve.wait_ge(clipped, c + 1)
                nc.vector.tensor_scalar(xb, xb, UPWARD, MAGIC, ALU.mult, ALU.add).then_inc(spiked, 1)
                dve.wait_ge(spiked, 2 * c + 1)
                nc.vector.tensor_scalar(spikes[p][:], xb, MAGIC, None, ALU.subtract).then_inc(spiked, 1)

            first_spike(0, 0)
            with dve.Fori(0, B // NQ - 1) as i:
                for m in range(NQ):
                    spike(NQ * i + m + 1, (m + 1) % 2)
                    count(NQ * i + m, m)
            for m in range(NQ):
                c = B - NQ + m
                if c + 1 < B:
                    spike(c + 1, (m + 1) % 2)
                count(c, m)
            dve.wait_ge(counted, 3 * B)
            for t in range(3):
                last = nc.vector.bn_aggr(mv[:, t, :], stats[:, t].rearrange("p a b -> p (a b)"))
            last.then_inc(stats_done, 1)
            dve.wait_ge(std_done, 1)
            g0, b0 = COLS["bn_gamma"][0], COLS["bn_beta"][0]
            nc.vector.reciprocal(tmp[:], tmp[:]).then_inc(cut, 1)
            dve.wait_ge(cut, 8)
            nc.vector.tensor_tensor(scale[:], tmp[:], k["cols"][:, g0:g0 + 3], ALU.mult).then_inc(cut, 1)
            dve.wait_ge(cut, 9)
            nc.vector.tensor_tensor(tmp[:], mv[:, :, 0], scale[:], ALU.mult).then_inc(cut, 1)
            dve.wait_ge(cut, 10)
            nc.vector.tensor_tensor(shift[:], k["cols"][:, b0:b0 + 3], tmp[:], ALU.subtract).then_inc(cut, 1)


def attend(nc, k, x, H, QKV, scale, shift):
    with ExitStack() as st:
        sb = lambda n, s, d=F32: st.enter_context(nc.sbuf_tensor(f"at_{n}", s, d))
        sem = lambda n: st.enter_context(nc.semaphore(f"at_s_{n}"))
        relu = [sb(f"relu{n}", [P, S]) for n in range(3)]
        vs = sb("vs", [P, S], BF16)
        qs = sb("qs", [P, S], BF16)
        ks = [sb(f"ks{p}", [P, S], BF16) for p in range(2)]
        qm = [sb(f"qm{p}", [P, HEADS, S], BF16) for p in range(2)]
        ve = [sb(f"ve{p}", [P, 5, 4, 32], BF16) for p in range(2)]
        vo = [sb(f"vo{p}", [P, 5, 4, 32], BF16) for p in range(2)]
        clip = [[sb(f"clip{p}{u}", [P, 2, HALF], BF16) for u in range(4)] for p in range(2)]
        fours = sb("fours", [P, HALF], BF16)
        ident = sb("ident", [P, P], BF16)
        out_r = [sb(f"out_r{j}", [P, HALF]) for j in range(2)]
        out_s = [sb(f"out_s{j}", [P, HALF], BF16) for j in range(2)]
        w = sb("w", [P, P])
        w3 = sb("w3", [P, 3, P], BF16)
        headmask = sb("headmask", [P, HEADS])
        four = sb("four", [P, 1])
        slot = [st.enter_context(nc.psum_tensor(f"at_slot{n}", [P, 2, 512], F32)) for n in range(3)]
        out_ps = [st.enter_context(nc.psum_tensor(f"at_out{j}", [P, 512], F32)) for j in range(2)]
        (w_in, cut, relu_done, steps, spiked, masked, s_ps, by_dve, by_act, o_done, vt_ps, ve_done, vo_done, out_relu,
         out_spiked, proj_ps, resid, met, ready) = (sem(n) for n in (
            "w_in", "cut", "relu", "steps", "spiked", "masked", "scores", "by_dve", "by_act", "o_done", "vt", "ve", "vo",
            "out_relu", "out_spiked", "proj", "resid", "met", "ready"))
        met_pe = sem("met_pe")
        TAIL = S - 4 * P
        PAIRS = [(0, 2), (1, 3), (4, 6), (5, 7)]
        SLOT = [[0, 1, 2, 0], [1, 2, 0, 1]]
        V, Q, K = range(3)
        WHERE = [2, 0, 1]
        rows_of = lambda t: P if t < 4 else TAIL
        vt_view = out_ps[0][:, 0:5 * P // 2].bitcast(BF16).rearrange("p (t h d) -> p t h d", t=5, d=32)
        block = st.enter_context(nc.Block())

        @block.sync
        def _(sp):
            sp.dma_start(w[:], x["wproj"]).then_inc(w_in, 16)
            sp.dma_start(headmask[:], x["headmask"]).then_inc(w_in, 16)

        @block.tensor
        def _(pe):
            def score(b, p, T, units, first=False):
                j, t = divmod(T, 5)
                TT = 10 * b + T
                if T == 0 and units[0] == 0:
                    pe.wait_ge(masked, b + 1)
                    pe.wait_ge(spiked, 3 * b + 3)
                for u in units:
                    heads = PAIRS[u]
                    if T % 2 == 0:
                        last_use = [(by_dve, 2 * TT), (by_act, 2 * TT), (by_act, 2 * TT - 1), (by_dve, 2 * TT + 1)][u]
                    else:
                        last_use = [(by_act, 2 * TT - 1), (by_dve, 2 * TT), (by_act, 2 * TT), (by_dve, 2 * TT + 1)][u]
                    if not (first and u < 3):
                        pe.wait_ge(*last_use)
                    for s, h in enumerate(heads):
                        last = nc.tensor.matmul(slot[SLOT[T % 2][u]][0:rows_of(t), s, 0:HALF], ks[p][:, t * P:t * P + rows_of(t)],
                                                qm[p][:, h, j * HALF:(j + 1) * HALF], start=True, stop=True)
                    last.then_inc(s_ps, 1)

            def weigh(b, p, T):
                j, t = divmod(T, 5)
                TT = 10 * b + T
                r = rows_of(t)
                pe.wait_ge(by_dve, 2 * TT + 2)
                if T == 0:
                    pe.wait_ge(ve_done, b + 1)
                    pe.wait_ge(vo_done, b + 1)
                if T == 5:
                    pe.wait_ge(resid, 2 * b)
                pe.sem_inc(met_pe, 1)
                for h in range(0, HEADS, 2):
                    u, s = (0 if h < 4 else 2), h // 2 % 2
                    nc.tensor.matmul(out_ps[j][16 * h:16 * h + 32, 0:HALF], ve[p][0:r, t, h // 2, :], clip[T % 2][u][0:r, s, :],
                                     start=t == 0, stop=False)
                nc.tensor.matmul(out_ps[j][:, 0:HALF], vo[p][0:r, t].rearrange("p h d -> p (h d)"), fours[0:r, :],
                                 start=False, stop=False)
                pe.wait_ge(by_act, 2 * TT + 2)
                pe.sem_inc(met_pe, 1)
                for h in range(1, HEADS, 2):
                    u, s = (1 if h < 4 else 3), h // 2 % 2
                    last = nc.tensor.matmul(out_ps[j][16 * h - 16:16 * h + 16, 0:HALF], vo[p][0:r, t, h // 2, :],
                                            clip[T % 2][u][0:r, s, :], start=False, stop=t == 4)
                last.then_inc(o_done, 1)

            def project(b, j):
                pe.wait_ge(out_spiked, 2 * b + j + 2)
                for part in range(3):
                    last = nc.tensor.matmul(out_ps[j][:, 0:HALF], w3[:, part, :], out_s[j][:], start=part == 0, stop=part == 2)
                last.then_inc(proj_ps, 1)

            def turn_values(b, first=False):
                pe.wait_ge(spiked, 3 * b + 1)
                if not first:
                    pe.wait_ge(resid, 2 * b - 1)
                flat = out_ps[0][:, 0:5 * P // 2].bitcast(BF16)
                for t in range(5):
                    last = nc.tensor.transpose(flat[0:rows_of(t), t * P:(t + 1) * P], vs[:, t * P:t * P + rows_of(t)], ident[:])
                last.then_inc(vt_ps, 1)

            def steps_of(b, p, first=False, final=False):
                for T in range(10):
                    ahead = (b, p, T + 1) if T < 9 else (b + 1, 1 - p, 0)
                    if T < 9 or not final:
                        score(*ahead, range(3))
                    if T == 2 and not first:
                        project(b - 1, 1)
                    weigh(b, p, T)
                    if T < 9 or not final:
                        score(*ahead, range(3, 4))
                    if T == 7:
                        project(b, 0)
                    if T == 8 and not final:
                        turn_values(b + 1)

            pe.sem_inc(proj_ps, 1)
            pe.wait_ge(ready, 2)
            turn_values(0, True)
            score(0, 0, 0, range(4), True)
            steps_of(0, 0, first=True)
            with pe.Fori(0, (B - 2) // 2) as i:
                steps_of(2 * i + 1, 1)
                steps_of(2 * i + 2, 0)
            steps_of(B - 1, 1, final=True)
            project(B - 1, 1)

        @block.scalar
        def _(act):
            def rectify(b, n, first=False):
                if not first:
                    act.wait_ge(spiked, 3 * b + n - 2)
                    act.sem_inc(met, 1)
                c = WHERE[n]
                nc.scalar.activation(relu[n][:], QKV[:, c, bass.ds(b * S, S)], ACT.Relu, bias=shift[:, c:c + 1],
                                     scale=scale[:, c:c + 1]).then_inc(relu_done, 1)

            def clip_odd(b, T, first=False):
                TT = 10 * b + T
                r = rows_of(T % 5)
                for u in (1, 3):
                    act.wait_ge(s_ps, 4 * TT + u + 1)
                    if not first:
                        act.wait_ge(o_done, TT - 1)
                    nc.scalar.activation(clip[T % 2][u][0:r], slot[SLOT[T % 2][u]][0:r, :, 0:HALF], ACT.Relu,
                                         bias=four[0:r], scale=-1.0).then_inc(by_act, 1)

            def out_rectify(b, j):
                act.wait_ge(o_done, 10 * b + 5 * j + 5)
                if not (isinstance(b, int) and b == 0):
                    act.wait_ge(out_spiked, 2 * b + j)
                nc.scalar.activation(out_r[j][:], out_ps[j][:, 0:HALF], ACT.Relu, scale=float(HD) ** -0.5).then_inc(out_relu, 1)

            def odd_values(b, p):
                act.wait_ge(ve_done, b + 1)
                for t0, t1, r in ((0, 4, P), (4, 5, TAIL)):
                    last = nc.scalar.activation(vo[p][0:r, t0:t1, :, HD:32], vt_view[0:r, t0:t1, :, HD:32], ACT.Copy, scale=-1.0)
                last.then_inc(vo_done, 1)

            def steps_of(b, p, first=False, final=False):
                for T in range(10):
                    if T < 9:
                        clip_odd(b, T + 1, first and T == 0)
                    elif not final:
                        clip_odd(b + 1, 0)
                    if T == 0 and not first:
                        out_rectify(b - 1, 1)
                    if T < 3 and not final:
                        rectify(b + 1, T)
                    if T == 5:
                        out_rectify(b, 0)
                    if T == 9 and not final:
                        odd_values(b + 1, 1 - p)

            act.wait_ge(ready, 1)
            for n in range(3):
                rectify(0, n, True)
            odd_values(0, 0)
            clip_odd(0, 0, True)
            steps_of(0, 0, first=True)
            with act.Fori(0, (B - 2) // 2) as i:
                steps_of(2 * i + 1, 1)
                steps_of(2 * i + 2, 0)
            steps_of(B - 1, 1, final=True)
            out_rectify(B - 1, 1)

        @block.gpsimd
        def _(pool):
            def mask(b, p, first=False):
                pool.wait_ge(spiked, 3 * b + 2)
                if not first:
                    pool.wait_ge(s_ps, 40 * b - 40)
                pool.sem_inc(met, 1)
                for h in range(HEADS):
                    last = nc.gpsimd.tensor_scalar(qm[p][:, h, :], qs[:], headmask[:, h:h + 1], 1.0, ALU.mult, ALU.mult)
                last.then_inc(masked, 1)

            pool.wait_ge(w_in, 32)
            mask(0, 0, True)
            mask(1, 1, True)
            with pool.Fori(0, (B - 2) // 2) as i:
                mask(2 * i + 2, 0)
                mask(2 * i + 3, 1)

        @block.vector
        def _(dve):
            def clip_even(b, T, first=False):
                TT = 10 * b + T
                r = rows_of(T % 5)
                for u in (0, 2):
                    dve.wait_ge(s_ps, 4 * TT + u + 1)
                    if not first:
                        dve.wait_ge(o_done, TT - 1)
                    nc.vector.tensor_scalar(clip[T % 2][u][0:r], slot[SLOT[T % 2][u]][0:r, :, 0:HALF], 4.0, None,
                                            ALU.min).then_inc(by_dve, 1)

            def spike(dst, r, n, done):
                dve.sem_inc(met, 1)
                nc.vector.tensor_scalar(r, r, 4.0, UPWARD, ALU.min, ALU.mult).then_inc(steps, 1)
                dve.wait_ge(steps, n + 1)
                dve.sem_inc(met, 1)
                nc.vector.tensor_scalar(dst, r, MAGIC, MAGIC, ALU.add, ALU.subtract).then_inc(done, 1)

            def spikes_of(b, p, n, order, first=False):
                dve.wait_ge(relu_done, 3 * b + n + 1)
                if not first:
                    if n == V:
                        dve.wait_ge(vt_ps, b)
                    elif n == Q:
                        dve.wait_ge(masked, b)
                    else:
                        dve.wait_ge(s_ps, 40 * b - 40)
                spike((vs, qs, ks[p])[n][:], relu[n][:], order, spiked)

            def out_spikes(b, j, order):
                dve.wait_ge(out_relu, 2 * b + j + 1)
                if not (isinstance(b, int) and b == 0):
                    dve.wait_ge(proj_ps, 2 * b + j)
                spike(out_s[j][:], out_r[j][:], order, out_spiked)

            def residual(b, j):
                dve.wait_ge(proj_ps, 2 * b + j + 2)
                hb = H[:, bass.ds(b * S + j * HALF, HALF)]
                at, _ = COLS["proj_b"]
                dve.sem_inc(met, 1)
                nc.vector.scalar_tensor_tensor(hb, out_ps[j][:, 0:HALF], k["cols"][:, at:at + 1], hb, ALU.add, ALU.add).then_inc(resid, 1)

            def even_values(b, p):
                dve.wait_ge(vt_ps, b + 1)
                for t0, t1, r in ((0, 4, P), (4, 5, TAIL)):
                    last = nc.vector.tensor_copy(ve[p][0:r, t0:t1, :, 0:HD], vt_view[0:r, t0:t1, :, 0:HD])
                last.then_inc(ve_done, 1)

            def steps_of(b, p, first=False, final=False):
                for T in range(10):
                    if T < 9:
                        clip_even(b, T + 1, first and T == 0)
                    elif not final:
                        clip_even(b + 1, 0)
                    n = 5 * b + 2
                    if T == 1 and not first:
                        out_spikes(b - 1, 1, n)
                    if T in (2, 4, 5) and not final:
                        at = (2, 4, 5).index(T)
                        spikes_of(b + 1, 1 - p, at, n + 1 + at, first)
                    if T == 3 and not first:
                        residual(b - 1, 1)
                    if T == 6:
                        out_spikes(b, 0, n + 1 if final else n + 4)
                    if T == 8:
                        residual(b, 0)
                    if T == 9 and not final:
                        even_values(b + 1, 1 - p)

            nc.vector.memset(four[:], 4.0).then_inc(ready, 1)
            nc.vector.memset(fours[:], -4.0)
            for p in range(2):
                nc.vector.memset(ve[p][:], 0.0)
                nc.vector.memset(vo[p][:], 0.0)
            nc.vector.tensor_copy(ident[:], k["ident"][:])
            dve.wait_ge(w_in, 32)
            for part in range(3):
                nc.vector.tensor_copy(w3[:, part, :], w[:]).then_inc(cut, 1)
                dve.wait_ge(cut, 2 * part + 1)
                nc.vector.tensor_tensor(w[:], w[:], w3[:, part, :], ALU.subtract).then_inc(cut, 1)
                dve.wait_ge(cut, 2 * part + 2)
            dve.sem_inc(ready, 1)
            dve.sem_inc(out_spiked, 1)
            for n in range(3):
                spikes_of(0, 0, n, n, True)
            even_values(0, 0)
            clip_even(0, 0, True)
            steps_of(0, 0, first=True)
            with dve.Fori(0, (B - 2) // 2) as i:
                steps_of(2 * i + 1, 1)
                steps_of(2 * i + 2, 0)
            steps_of(B - 1, 1, final=True)
            out_spikes(B - 1, 1, 5 * (B - 1) + 4)
            residual(B - 1, 1)


def last_ffn(nc, k, x, H, out):
    with ExitStack() as st:
        sb = lambda n, s, d=F32: st.enter_context(nc.sbuf_tensor(f"ff_{n}", s, d))
        F = sb("tokens", [P, NTP])
        layernorm(nc, k, H, F, [(1.0 + 1e-5, 1e-10)], "ln4")
        comb = sb("comb", [P, TILES, NEX])
        cnt = sb("cnt", [P, TILES, NEX + 1])
        shapes = {"expert_in": [P, 4 * P], "shared_in": [P, 4 * P], "expert_out": [P, 2, NEX * P], "shared_out": [P, 2, P],
                  "out_bias": [NEX + 1, P]}
        high = {n: sb(f"{n}_high", s, F32R) for n, s in shapes.items()}
        low = {n: sb(f"{n}_low", s, F32R) for n, s in shapes.items()}
        route_tokens(nc, k, x, F, comb, cnt, high, low)
        mix_experts(nc, k, H, F, comb, cnt, high, low, out)


def route_tokens(nc, k, x, F, comb, cnt, high, low):
    with ExitStack() as st:
        sb = lambda n, s, d=F32: st.enter_context(nc.sbuf_tensor(f"rt_{n}", s, d))
        sem = lambda n: st.enter_context(nc.semaphore(f"rt_s_{n}"))
        gates = sb("gates", [P, 10])
        weights = {n: sb(n, list(t.shape)) for n, t in high.items()}
        NB = 4
        fb = [sb(f"chunk{p}", [P, CH]) for p in range(NB)]
        GL = sb("logits", [P, TILES, 10])
        s, ns, mx, tot = (sb(n, [P, TILES]) for n in ("second", "first", "max", "total"))
        es, tmp, pr, sel = (sb(n, [P, TILES, 4]) for n in ("chosen", "tmp", "probs", "sel"))
        beats = sb("beats", [P, TILES, 6])
        gl_ps = [st.enter_context(nc.psum_tensor(f"rt_ps{p}", [P, 512], F32)) for p in range(NB)]
        gates_in, scaled, kept, gated, copied, step, shifted, exps, met, loaded, w_high, w_low = (
            sem(n) for n in ("gates_in", "scaled", "kept", "gated", "copied", "step", "shifted", "exps", "met", "loaded",
                             "w_high", "w_low"))
        GLW = CT * 10
        block = st.enter_context(nc.Block())

        @block.sync
        def _(sp):
            sp.dma_start(gates[:], x["gates"]).then_inc(gates_in, 16)
            for name in weights:
                sp.dma_start(weights[name][:], x[name]).then_inc(loaded, 16)
            sp.wait_ge(loaded, 16 * len(weights))

        def loop(eng, body):
            with eng.Fori(0, CHUNKS // NB) as i:
                for m in range(NB):
                    body(NB * i + m, m)
            for c in range(CHUNKS // NB * NB, CHUNKS):
                body(c, c % NB)

        @block.gpsimd
        def _(pool):
            for n, name in enumerate(weights):
                pool.wait_ge(w_high, n + 1)
                nc.gpsimd.tensor_tensor(low[name][:], weights[name][:], high[name][:], ALU.subtract).then_inc(w_low, 1)

        @block.scalar
        def _(act):
            def keep(c, p):
                act.wait_ge(gated, c + 1)
                act.sem_inc(met, 1)
                nc.scalar.activation(fb[p][:], F[:, bass.ds(c * CH, CH)], ACT.Copy).then_inc(kept, 1)

            act.wait_ge(scaled, 1)
            loop(act, keep)
            act.wait_ge(shifted, 1)
            nc.scalar.activation(es[:], es[:], ACT.Exp).then_inc(exps, 1)

        @block.tensor
        def _(pe):
            def gate(c, p):
                pe.wait_ge(kept, c + 1)
                pe.wait_ge(copied, c + 1)
                for t in range(CT):
                    last = nc.tensor.matmul(gl_ps[p][:, 10 * t:10 * t + 10], fb[p][:, t * P:(t + 1) * P], gates[:],
                                            start=True, stop=True)
                last.then_inc(gated, 1)

            pe.sem_inc(gated, NB)
            pe.wait_ge(gates_in, 16)
            loop(pe, gate)

        @block.vector
        def _(dve):
            def copy(c, p):
                dve.wait_ge(gated, NB + c + 1)
                nc.vector.tensor_copy(GL[:, bass.ds(c * CT, CT), :].rearrange("p t e -> p (t e)"), gl_ps[p][:, 0:GLW]).then_inc(copied, 1)

            chain = [0]

            def link(ins):
                chain[0] += 1
                ins.then_inc(step, 1)
                dve.wait_ge(step, chain[0])

            wide = lambda a, n: a[:].unsqueeze(2).broadcast_to([P, TILES, n])
            link(nc.vector.memset(F[:, NT:NTP], 0.0))
            at, bt, gt = COLS["ln_scale"][0], COLS["ln_bias"][0], COLS["gate_b"][0]
            nc.vector.tensor_scalar(F[:], F[:], k["cols"][:, at:at + 1], k["cols"][:, bt:bt + 1], ALU.mult, ALU.add).then_inc(scaled, 1)
            dve.sem_inc(copied, NB)
            dve.wait_ge(loaded, 16 * len(weights))
            for name in weights:
                nc.vector.tensor_copy(high[name][:], weights[name][:]).then_inc(w_high, 1)
            loop(dve, copy)
            dve.wait_ge(copied, CHUNKS + NB)
            link(nc.vector.tensor_tensor(GL[:], GL[:], k["cols"][:, gt:gt + 10].unsqueeze(1).broadcast_to([P, TILES, 10]), ALU.add))
            link(nc.vector.tensor_tensor(s[:], GL[:, :, 1], GL[:, :, 0], ALU.is_gt))
            link(nc.vector.tensor_scalar(ns[:], s[:], -1.0, 1.0, ALU.mult, ALU.add))
            nc.vector.tensor_tensor(tmp[:], GL[:, :, 6:10], wide(s, 4), ALU.mult)
            link(nc.vector.tensor_tensor(es[:], GL[:, :, 2:6], wide(ns, 4), ALU.mult))
            link(nc.vector.tensor_tensor(es[:], es[:], tmp[:], ALU.add))
            link(nc.vector.tensor_reduce(mx[:], es[:], AX.X, ALU.max))
            nc.vector.tensor_tensor(es[:], es[:], wide(mx, 4), ALU.subtract).then_inc(shifted, 1)
            dve.wait_ge(exps, 1)
            link(nc.vector.tensor_reduce(tot[:], es[:], AX.X, ALU.add))
            link(nc.vector.reciprocal(tot[:], tot[:]))
            link(nc.vector.tensor_tensor(pr[:], es[:], wide(tot, 4), ALU.mult))
            pairs = [(i, j) for i in range(4) for j in range(i + 1, 4)]
            for n, (i, j) in enumerate(pairs):
                last = nc.vector.tensor_tensor(beats[:, :, n], pr[:, :, i], pr[:, :, j], ALU.is_ge)
            link(last)
            won = [beats[:, :, n] for n in range(6)]
            nc.vector.tensor_tensor(sel[:, :, 3], won[2], won[4], ALU.add)
            nc.vector.tensor_tensor(sel[:, :, 2], won[1], won[3], ALU.add)
            nc.vector.tensor_tensor(sel[:, :, 1], won[0], won[3], ALU.subtract)
            link(nc.vector.tensor_tensor(sel[:, :, 0], won[0], won[1], ALU.add))
            nc.vector.tensor_tensor(sel[:, :, 3], sel[:, :, 3], won[5], ALU.add)
            nc.vector.tensor_tensor(sel[:, :, 2], sel[:, :, 2], won[5], ALU.subtract)
            nc.vector.tensor_tensor(sel[:, :, 1], sel[:, :, 1], won[4], ALU.subtract)
            link(nc.vector.tensor_tensor(sel[:, :, 0], sel[:, :, 0], won[2], ALU.add))
            nc.vector.tensor_scalar(sel[:, :, 3], sel[:, :, 3], 2.0, None, ALU.is_lt)
            nc.vector.tensor_scalar(sel[:, :, 2], sel[:, :, 2], 1.0, None, ALU.is_lt)
            nc.vector.tensor_scalar(sel[:, :, 1], sel[:, :, 1], 0.0, None, ALU.is_lt)
            link(nc.vector.tensor_scalar(sel[:, :, 0], sel[:, :, 0], 1.0, None, ALU.is_gt))
            link(nc.vector.tensor_tensor(pr[:], pr[:], sel[:], ALU.mult))
            link(nc.vector.tensor_reduce(tot[:], pr[:], AX.X, ALU.add))
            link(nc.vector.tensor_scalar(tot[:], tot[:], 1e-8, None, ALU.add))
            link(nc.vector.reciprocal(tot[:], tot[:]))
            link(nc.vector.tensor_tensor(pr[:], pr[:], wide(tot, 4), ALU.mult))
            nc.vector.tensor_tensor(comb[:, :, 0:4], pr[:], wide(ns, 4), ALU.mult)
            nc.vector.tensor_tensor(comb[:, :, 4:8], pr[:], wide(s, 4), ALU.mult)
            nc.vector.tensor_tensor(cnt[:, :, 0:4], sel[:], wide(ns, 4), ALU.mult)
            nc.vector.tensor_tensor(cnt[:, :, 4:8], sel[:], wide(s, 4), ALU.mult)
            nc.vector.memset(cnt[:, :, 8:9], 1.0)


def mix_experts(nc, k, H, F, comb, cnt, high, low, out):
    with ExitStack() as st:
        sb = lambda n, s, d=F32: st.enter_context(nc.sbuf_tensor(f"mx_{n}", s, d))
        sem = lambda n: st.enter_context(nc.semaphore(f"mx_s_{n}"))
        silu = {s: sb(f"silu_{s}", [P, 2, CH]) for s in "ES"}
        hid = {s: sb(f"hid_{s}", [P, 2, CH]) for s in "ES"}
        h = {s: [[sb(f"h_{s}{p}{q}", [P, 2, CH], F32R) for q in range(2)] for p in range(2)] for s in "ES"}
        f_parts = [[sb(f"f{p}{q}", [P, CH], F32R) for q in range(2)] for p in range(2)]
        weighted = sb("weighted", [P, NEX, P])
        R = [[sb(f"routed{p}{t}", [P, P]) for t in range(CT)] for p in range(2)]
        cnt_b = sb("cnt_chunk", [P, CT, NEX + 1])
        cnt_t = sb("cnt_turned", [NEX + 1, CH], F32R)
        a_ps = st.enter_context(nc.psum_tensor("mx_a", [P, 2, 512], F32))
        b_ps = st.enter_context(nc.psum_tensor("mx_b", [P, 2, 512], F32))
        e_ps = [st.enter_context(nc.psum_tensor(f"mx_e{n}", [P, 512], F32)) for n in range(2)]
        y_ps = st.enter_context(nc.psum_tensor("mx_y", [P, 512], F32))
        r_ps = st.enter_context(nc.psum_tensor("mx_r", [P, 512], F32))
        high_done, low_done, f_high, f_low, stored, met = (sem(n) for n in ("high", "low", "f_high", "f_low", "stored", "met"))
        (projected, silu_done, hidden, expert_done, weighed, reduced, cnt_kept, cnt_ps, cnt_out, y_done,
         added) = (sem(n) for n in (
             "projected", "silu", "hidden", "expert", "weighed", "reduced", "cnt_kept", "cnt_ps", "cnt_out",
             "y_done", "added"))
        block = st.enter_context(nc.Block())

        def ahead(c):
            return not isinstance(c, int) or c + 2 < CHUNKS

        def loop(eng, body):
            body(0, 0, True, False)
            with eng.Fori(0, (CHUNKS - 3) // 2) as i:
                body(2 * i + 1, 1, False, False)
                body(2 * i + 2, 0, False, False)
            body(CHUNKS - 2, 1, False, False)
            body(CHUNKS - 1, 0, False, True)

        @block.sync
        def _(sp):
            with sp.Fori(0, CHUNKS - 1) as c:
                sp.wait_ge(added, 2 * c + 3)
                sp.sem_inc(met, 1)
                sp.dma_start(out[:, bass.ds(c * CH, CH)], H[:, bass.ds(c * CH, CH)]).then_inc(stored, 16)
            sp.wait_ge(added, 2 * (CHUNKS - 1) + 3)
            sp.dma_start(out[:, (CHUNKS - 1) * CH:NT], H[:, (CHUNKS - 1) * CH:NT]).then_inc(stored, 16)
            sp.wait_ge(stored, 16 * CHUNKS)

        @block.tensor
        def _(pe):
            def project(c, p, s):
                if s == "E":
                    pe.wait_ge(hidden, 2 * c)
                else:
                    pe.wait_ge(hidden, 2 * c + 1)
                pe.wait_ge(f_low, c + 1)
                name = "expert_in" if s == "E" else "shared_in"
                for ps, at in ((a_ps, 0), (b_ps, 2)):
                    for f in range(2):
                        cols = slice((at + f) * P, (at + f + 1) * P)
                        last = split_matmul(nc, ps[:, f, 0:CH], (high[name][:, cols], low[name][:, cols]),
                                            (f_parts[p][0][:], f_parts[p][1][:]), True, True)
                last.then_inc(projected, 1)

            def experts(c, p, t):
                if t == 0:
                    pe.wait_ge(low_done, 2 * c + 1)
                tokens = slice(t * P, (t + 1) * P)
                for a in range(2):
                    pe.wait_ge(weighed, 6 * c + 2 * t + a + 1)
                    for f in range(2):
                        cols = slice(a * 512, (a + 1) * 512)
                        last = split_matmul(nc, e_ps[a][:], [part[:, f, tokens] for part in h["E"][p]],
                                            (high["expert_out"][:, f, cols], low["expert_out"][:, f, cols]), f == 0, f == 1)
                    last.then_inc(expert_done, 1)

            def turn_cnt(c):
                pe.wait_ge(cnt_kept, c + 1)
                pe.wait_ge(added, 2 * c + 1)
                for t in range(CT):
                    last = nc.tensor.transpose(r_ps[0:NEX + 1, t * P:(t + 1) * P], cnt_b[:, t, :], k["ident"][:])
                last.then_inc(cnt_ps, 1)

            def finish(c, p):
                pe.wait_ge(low_done, 2 * c + 2)
                pe.wait_ge(added, 2 * c + 1)
                for f in range(2):
                    split_matmul(nc, y_ps[:, 0:CH], (high["shared_out"][:, f, :], low["shared_out"][:, f, :]),
                                 [part[:, f, :] for part in h["S"][p]], f == 0, False)
                pe.wait_ge(cnt_out, c + 1)
                nc.tensor.matmul(y_ps[:, 0:CH], high["out_bias"][:], cnt_t[:], start=False, stop=False)
                nc.tensor.matmul(y_ps[:, 0:CH], low["out_bias"][:], cnt_t[:], start=False, stop=True)
                pe.wait_ge(reduced, CT * c + CT)
                for t in range(CT):
                    last = nc.tensor.transpose(r_ps[:, t * P:(t + 1) * P], R[p][t][:], k["ident"][:])
                last.then_inc(y_done, 1)

            def body(c, p, first, final):
                experts(c, p, 0)
                if not first:
                    finish(c - 1, 1 - p)
                if not final:
                    project(c + 1, 1 - p, "E")
                experts(c, p, 1)
                turn_cnt(c)
                if not final:
                    project(c + 1, 1 - p, "S")
                experts(c, p, 2)

            pe.sem_inc(cnt_ps, 1)
            project(0, 0, "E")
            project(0, 0, "S")
            loop(pe, body)
            finish(CHUNKS - 1, 0)

        @block.scalar
        def _(act):
            def swish(c, s):
                act.wait_ge(projected, 2 * c + 1 + (s == "S"))
                nc.scalar.activation(silu[s][:], a_ps[:, :, 0:CH], ACT.Silu).then_inc(silu_done, 1)

            def body(c, p, first, final):
                if not final:
                    swish(c + 1, "E")
                act.wait_ge(cnt_ps, c + 2)
                nc.scalar.activation(cnt_t[:], r_ps[0:NEX + 1, 0:CH], ACT.Copy).then_inc(cnt_out, 1)
                if not final:
                    swish(c + 1, "S")

            swish(0, "E")
            swish(0, "S")
            loop(act, body)

        @block.gpsimd
        def _(pool):
            def keep(c):
                pool.wait_ge(cnt_ps, c + 1)
                nc.gpsimd.tensor_copy(cnt_b[:], cnt[:, bass.ds(c * CT, CT), :]).then_inc(cnt_kept, 1)

            def f_low_part(c, p):
                pool.wait_ge(f_high, c + 1)
                nc.gpsimd.tensor_tensor(f_parts[p][1][:], F[:, bass.ds(c * CH, CH)], f_parts[p][0][:], ALU.subtract).then_inc(f_low, 1)

            def hid_low_part(c, p, s):
                pool.wait_ge(high_done, 2 * c + 1 + (s == "S"))
                nc.gpsimd.tensor_tensor(h[s][p][1][:], hid[s][:], h[s][p][0][:], ALU.subtract).then_inc(low_done, 1)

            def body(c, p, first, final):
                keep(c)
                if not final:
                    hid_low_part(c + 1, 1 - p, "E")
                if ahead(c):
                    f_low_part(c + 2, p)
                if not final:
                    hid_low_part(c + 1, 1 - p, "S")

            f_low_part(0, 0)
            f_low_part(1, 1)
            hid_low_part(0, 0, "E")
            hid_low_part(0, 0, "S")
            loop(pool, body)

        @block.vector
        def _(dve):
            def f_high_part(c, p):
                if not (isinstance(c, int) and c < 2):
                    dve.wait_ge(projected, 2 * c - 2)
                nc.vector.tensor_copy(f_parts[p][0][:], F[:, bass.ds(c * CH, CH)]).then_inc(f_high, 1)

            def hide(c, p, s):
                dve.wait_ge(silu_done, 2 * c + 1 + (s == "S"))
                if not (isinstance(c, int) and c == 0):
                    dve.wait_ge(low_done, 2 * c - 1 + (s == "S"))
                nc.vector.tensor_tensor(hid[s][:], silu[s][:], b_ps[:, :, 0:CH], ALU.mult).then_inc(hidden, 1)
                dve.wait_ge(hidden, 2 * c + 1 + (s == "S"))
                nc.vector.tensor_copy(h[s][p][0][:], hid[s][:]).then_inc(high_done, 1)

            def weigh(c, p, t):
                n = 6 * c + 2 * t
                for a in range(2):
                    dve.wait_ge(expert_done, n + a + 1)
                    by = comb[:, bass.ds(CT * c + t, 1), 4 * a:4 * a + 4].rearrange("p o e -> p (o e)").unsqueeze(2).broadcast_to([P, 4, P])
                    nc.vector.tensor_tensor(weighted[:, 4 * a:4 * a + 4, :], e_ps[a][:].rearrange("p (e d) -> p e d", e=4),
                                            by, ALU.mult).then_inc(weighed, 1)
                dve.wait_ge(weighed, n + 4)
                nc.vector.tensor_reduce(R[p][t][:], weighted[:].rearrange("p e d -> p d e"), AX.X, ALU.add).then_inc(reduced, 1)
                dve.wait_ge(reduced, CT * c + t + 1)

            def add(c):
                dve.wait_ge(y_done, c + 1)
                hc = H[:, bass.ds(c * CH, CH)]
                nc.vector.tensor_tensor(hc, hc, y_ps[:, 0:CH], ALU.add).then_inc(added, 1)
                dve.wait_ge(added, 2 * c + 2)
                nc.vector.tensor_tensor(hc, hc, r_ps[:, 0:CH], ALU.add).then_inc(added, 1)

            def body(c, p, first, final):
                weigh(c, p, 0)
                if not first:
                    add(c - 1)
                if not final:
                    hide(c + 1, 1 - p, "E")
                if ahead(c):
                    f_high_part(c + 2, p)
                weigh(c, p, 1)
                if not final:
                    hide(c + 1, 1 - p, "S")
                weigh(c, p, 2)

            dve.sem_inc(weighed, 2)
            dve.sem_inc(added, 1)
            f_high_part(0, 0)
            f_high_part(1, 1)
            hide(0, 0, "E")
            hide(0, 0, "S")
            loop(dve, body)
            add(CHUNKS - 1)


def build(nc, x, out):
    with ExitStack() as ctx:
        sb = lambda n, s, d=F32: ctx.enter_context(nc.sbuf_tensor(n, s, d))
        H = sb("H", [P, NTP])
        k = {"center": sb("center_sb", [P, P]), "mean32": sb("mean32_sb", [P, 32]), "pick_row": sb("pick_row_sb", [P, P]),
             "pick_row_r": sb("pick_row_r", [P, P], F32R),
             "cols": sb("cols_sb", [P, NCOLS]), "ident": sb("ident_sb", [P, P]), "W1": sb("W1_sb", [P, 5 * P]),
             "W2": sb("W2_sb", [P, 2, P]), "ones_bf": sb("ones_bf", [P, P], BF16), "b1_v3": sb("b1_v3", [P, EXPAND], BF16),
             "down_b3": sb("down_b3", [P, NE * P], BF16),
             "same_expert": sb("same_expert_sb", [P, P]), "earlier_group": sb("earlier_group_sb", [P, P]),
             "router": sb("router_sb", [P, NE]), "group_row": sb("group_row_sb", [P, 4]), "lanes": sb("lanes_sb", [P, BLK])}
        k["ln_sems"] = {n: [ctx.enter_context(nc.semaphore(f"ln_{n}")), 0] for n in LN_TOTALS}
        moe_d = (nc.dram_tensor("token_rows", [NROWS, ROWW], F32, kind="Internal").ap(),
                 [nc.dram_tensor(f"moe_sums{p}", [NROWS, P], F32, kind="Internal").ap() for p in range(2)],
                 nc.dram_tensor("expert_slots", [NE * BLOCKS, BLK], I32, kind="Internal").ap())
        load_inputs(nc, x, k, H)
        with ExitStack() as st:
            HN = st.enter_context(nc.sbuf_tensor("HN", [P, NT], F32))
            layernorm(nc, k, H, HN, [(1.0, 1e-5), (1.0 + 1e-6, 1e-11)], "ln1",
                      gain=k["cols"][:, COLS["norm"][0]:COLS["norm"][0] + 1])
            gated_attention(nc, k, x, H, HN, moe_d)
        moe_first(nc, k, x, H, moe_d)
        spiking_attention(nc, k, x, H)
        last_ffn(nc, k, x, H, out)


def _arrays(inp):
    f = np.float32
    a = {}
    img = np.asarray(inp["x"]).reshape(B, 3, 6, 16, 6, 16).transpose(1, 3, 5, 0, 2, 4)
    a["patches"] = img.reshape(TOK_K, P, B * PATCHES)
    a["text"] = np.asarray(inp["txt"]).transpose(2, 0, 1)
    a["tok_w"] = np.asarray(inp["L0_tok_w"]).T.reshape(TOK_K, P, P)
    a["W1"] = np.asarray(inp["L0_attn_W1"])
    a["W2"] = np.asarray(inp["L0_attn_W2"]).reshape(2, P, P).transpose(1, 0, 2)
    b1 = np.asarray(inp["L0_attn_b1"])
    a["bias_rows"] = np.concatenate([np.asarray(inp["L0_ffn_b_down"]), b1[EXPAND:2 * EXPAND].reshape(-1, P)], 0)
    a["router"] = np.asarray(inp["L0_ffn_W_router"])
    up_b = np.zeros((8, 3 * P), f)
    up_b[:, :DFF] = np.asarray(inp["L0_ffn_b_up"])
    gate_b = np.concatenate([np.asarray(inp["L1_ffn_group_bias"]), np.asarray(inp["L1_ffn_expert_bias"])])
    parts = {
        "tok_b": np.asarray(inp["L0_tok_b"])[:, None], "b2": np.asarray(inp["L0_attn_b2"])[:, None],
        "gamma": np.asarray(inp["L0_attn_gamma"]).T, "beta": np.asarray(inp["L0_attn_beta"]).T,
        "norm": np.broadcast_to(np.asarray(inp["L0_attn_norm_scale"]).reshape(1, 1), (P, 1)),
        "b1_base": b1[2 * EXPAND:][:, None], "b1_u": b1[:EXPAND].reshape(2, P).T,
        "router_b": np.tile(np.asarray(inp["L0_ffn_b_router"]), NGRP)[:, None],
        "bn_gamma": np.asarray(inp["L1_attn_gamma"]).reshape(3, P).T, "bn_beta": np.asarray(inp["L1_attn_beta"]).reshape(3, P).T,
        "proj_b": np.asarray(inp["L1_attn_bproj"])[:, None], "ln_scale": np.asarray(inp["L1_ffn_ln_scale"])[:, None],
        "ln_bias": np.asarray(inp["L1_ffn_ln_bias"])[:, None],
        "up_b": up_b.reshape(24, P).T, "gate_b": np.broadcast_to(gate_b[None], (P, 10)),
    }
    a["cols"] = np.concatenate([parts[n] for n in COLS], axis=1)
    a["wqkv"] = np.asarray(inp["L1_attn_Wqkv"]).T
    a["wproj"] = np.asarray(inp["L1_attn_Wproj"]).T
    up = np.asarray(inp["L0_ffn_W_up"])
    a["up"] = up
    down = np.zeros((NE, 3 * P, P), f)
    down[:, :DFF] = np.asarray(inp["L0_ffn_W_down"])
    a["down"] = down.reshape(NE, 3, P, P).transpose(0, 2, 1, 3)
    a["shared_in"] = np.asarray(inp["L1_ffn_shared_in_w"]).T
    a["expert_in"] = np.asarray(inp["L1_ffn_expert_in_w"]).T
    a["shared_out"] = np.asarray(inp["L1_ffn_shared_out_w"]).T.reshape(2, P, P).transpose(1, 0, 2)
    a["expert_out"] = np.asarray(inp["L1_ffn_expert_out_weight"]).transpose(2, 0, 1).reshape(2, P, NEX * P).transpose(1, 0, 2)
    a["out_bias"] = np.concatenate([np.asarray(inp["L1_ffn_expert_out_bias"]), np.asarray(inp["L1_ffn_shared_out_b"])[None]], 0)
    a["gates"] = np.concatenate([np.asarray(inp["L1_ffn_group_gate_w"]), np.asarray(inp["L1_ffn_expert_gate_w"])], 0).T
    a["center"] = (np.eye(P) - 1.0 / P).astype(f)
    a["mean32"] = np.full((P, 32), 1.0 / P, f)
    a["pick_row"] = np.where(np.arange(P)[:, None] % 32 == 0, 1.0, 0.0).astype(f) * np.ones((1, P), f)
    a["ident"] = np.eye(P, dtype=f)
    lane = np.arange(P)
    a["same_expert"] = (lane[:, None] % NE == lane[None] % NE).astype(f)
    a["earlier_group"] = ((lane[:, None] % NE == lane[None] % NE) & (lane[:, None] // NE < lane[None] // NE)).astype(f)
    a["group_row"] = np.stack([lane // NE * SEG, lane // NE * BLK, lane % NE * BLOCKS, lane % 2 * 0], 1).astype(f)
    a["lanes"] = np.broadcast_to(np.arange(BLK, dtype=f), (P, BLK))
    a["empty_slots"] = (TRASH + BLK * NGRP + np.arange(NE * SLOTS) % SLOTS).reshape(-1, BLK).astype(np.int32)
    a["headmask"] = (lane[:, None] // HD == np.arange(HEADS)[None]).astype(f)
    inv_freq = (10000.0 ** (-np.arange(ROPE) / ROPE)).astype(f)
    angle = (np.arange(S, dtype=f)[None] * inv_freq[:, None]).astype(f).astype(np.float64)
    cos, sin = (fn(angle) / 128 for fn in (np.cos, np.sin))
    ct, stt = np.zeros((P, 3, S), f), np.zeros((P, 3, 2, S), f)
    for t, (m0, rows) in enumerate(MTILES):
        ct[:rows, t] = cos[m0:m0 + rows]
        stt[:rows, t, 0] = sin[m0:m0 + rows]
        stt[:rows, t, 1] = -sin[m0:m0 + rows]
    a["cos"], a["sin"] = ct, stt
    return {n: np.ascontiguousarray(v) for n, v in a.items()}


def kernel(**inputs):
    import concourse.bacc as _bacc
    from concourse.bass_utils import run_bass_kernel_spmd as _run

    nc = _bacc.Bacc("TRN2", target_bir_lowering=False, num_devices=1)
    arrays = _arrays(inputs)
    x = {n: nc.dram_tensor(f"in_{n}", a.shape, mybir.dt.from_np(a.dtype), kind="ExternalInput").ap() for n, a in arrays.items()}
    out = nc.dram_tensor("out_h", (P, NT), F32, kind="ExternalOutput").ap()
    build(nc, x, out)
    r = _run(nc, [{f"in_{n}": a for n, a in arrays.items()}], core_ids=[0])
    return r.results[0]["out_h"].reshape(P, B, S).transpose(1, 2, 0)
```
